# Optimizing a Trainium2 kernel written in Bass

```python
import numpy as np
import jax
import jax.numpy as jnp

def _softmax(x, axis=-1):
    return jax.nn.softmax(x, axis=axis)

def _gelu(x):
    return jax.nn.gelu(x, approximate=True)

def _silu(x):
    return jax.nn.silu(x)

def _sigmoid(x):
    return jax.nn.sigmoid(x)

def _layernorm(x, axis=-1, eps=1e-05):
    m = jnp.mean(x, axis=axis, keepdims=True)
    v = jnp.var(x, axis=axis, keepdims=True)
    return (x - m) / jnp.sqrt(v + eps)

def _scatter_add(tgt, idx, src, axis=0):
    return tgt.at[idx].add(src)

def _segment_sum(src, seg, n):
    return jax.ops.segment_sum(src, seg, n)
kernel_name = 'mk_hybrid_d2_jaxref_r8_b94b4c'

def setup_inputs(seed: int=0):
    np.random.seed(seed)
    _w = jnp.asarray

    def _L0_attn_a_setup():
        import jax, jax.numpy as jnp
        import numpy as np
        NUM_HEADS = 16
        key = jax.random.key(seed)
        k1, k2, k3 = jax.random.split(key, 3)
        B, T, C = (2, 256, 128)
        x = jax.random.normal(k1, (B, T, C), dtype=jnp.float32)
        w_qkv = jax.random.normal(k2, (C, 3 * C), dtype=jnp.float32) * (1.0 / np.sqrt(C))
        b_qkv = jnp.zeros((3 * C,), dtype=jnp.float32)
        w_out = jax.random.normal(k3, (C, C), dtype=jnp.float32) * (1.0 / np.sqrt(C))
        b_out = jnp.zeros((C,), dtype=jnp.float32)
        return {'x': x, 'w_qkv': w_qkv, 'b_qkv': b_qkv, 'w_out': w_out, 'b_out': b_out}
    _L0_attn_a_in = _L0_attn_a_setup()

    def _L0_attn_b_setup():
        import jax, jax.numpy as jnp
        import numpy as np
        DIM, H, KV, HD, WIN = (128, 16, 4, 64, 64)
        EPS = 1e-06

        def rmsnorm(x, w, eps=EPS):
            return x * jax.lax.rsqrt(jnp.mean(x * x, axis=-1, keepdims=True) + eps) * w
        key = jax.random.key(seed)
        ks = jax.random.split(key, 7)
        B, T = (4, 256)
        s = 0.02
        return {'x': jax.random.normal(ks[0], (B, T, DIM), dtype=jnp.float32), 'wq': jax.random.normal(ks[1], (H * HD, DIM), dtype=jnp.float32) * s, 'wk': jax.random.normal(ks[2], (KV * HD, DIM), dtype=jnp.float32) * s, 'wv': jax.random.normal(ks[3], (KV * HD, DIM), dtype=jnp.float32) * s, 'wo': jax.random.normal(ks[4], (DIM, H * HD), dtype=jnp.float32) * s, 'q_norm_w': jnp.ones((HD,), dtype=jnp.float32), 'k_norm_w': jnp.ones((HD,), dtype=jnp.float32)}
    _L0_attn_b_in = _L0_attn_b_setup()

    def _L0_ffn_setup():
        import jax, jax.numpy as jnp
        import numpy as np
        B, S, D, F, E = (4, 256, 128, 512, 8)
        key = jax.random.key(seed)
        ks = jax.random.split(key, 7)
        s1 = 1.0 / np.sqrt(D)
        s2 = 1.0 / np.sqrt(F)
        x = jax.random.normal(ks[0], (B, S, D), dtype=jnp.float32)
        W1 = jax.random.uniform(ks[1], (E, D, F), jnp.float32, -s1, s1)
        b1 = jax.random.uniform(ks[2], (E, F), jnp.float32, -s1, s1)
        W2 = jax.random.uniform(ks[3], (E, F, D), jnp.float32, -s2, s2)
        b2 = jax.random.uniform(ks[4], (E, D), jnp.float32, -s2, s2)
        Wr = jax.random.uniform(ks[5], (D, E), jnp.float32, -s1, s1)
        br = jax.random.uniform(ks[6], (E,), jnp.float32, -s1, s1)
        return {'x': x, 'W1': W1, 'b1': b1, 'W2': W2, 'b2': b2, 'Wr': Wr, 'br': br}
    _L0_ffn_in = _L0_ffn_setup()

    def _L1_attn_a_setup():
        import jax, jax.numpy as jnp
        import numpy as np
        NUM_HEADS = 16
        HIDDEN = 128
        HEAD_DIM = HIDDEN // NUM_HEADS

        def _rope_cos_sin(S, head_dim):
            inv = 1.0 / 10000.0 ** (jnp.arange(0, head_dim, 2, dtype=jnp.float32) / head_dim)
            t = jnp.arange(S, dtype=jnp.float32)
            ang = jnp.outer(t, inv)
            return (jnp.cos(ang), jnp.sin(ang))

        def _apply_rope(x, cos, sin):
            B, S, nh, hd = x.shape
            xr = x[..., 0::2]
            xi = x[..., 1::2]
            c = cos[None, :, None, :]
            s = sin[None, :, None, :]
            or_ = xr * c - xi * s
            oi_ = xr * s + xi * c
            return jnp.stack([or_, oi_], axis=-1).reshape(B, S, nh, hd)
        key = jax.random.key(seed)
        k1, k2, k3, k4, k5 = jax.random.split(key, 5)
        std = 1.0 / np.sqrt(HIDDEN)
        return {'x': jax.random.normal(k1, (2, 256, HIDDEN), dtype=jnp.float32), 'wq': jax.random.normal(k2, (HIDDEN, HIDDEN), dtype=jnp.float32) * std, 'wk': jax.random.normal(k3, (HIDDEN, HIDDEN), dtype=jnp.float32) * std, 'wv': jax.random.normal(k4, (HIDDEN, HIDDEN), dtype=jnp.float32) * std, 'wo': jax.random.normal(k5, (HIDDEN, HIDDEN), dtype=jnp.float32) * std}
    _L1_attn_a_in = _L1_attn_a_setup()

    def _L1_attn_b_setup():
        import jax, jax.numpy as jnp
        import numpy as np
        H, DK, DV, CHUNK = (4, 32, 32, 32)

        def _silu(x):
            return x * jax.nn.sigmoid(x)

        def _l2norm(x, eps=1e-06):
            return x * jax.lax.rsqrt(jnp.sum(x * x, -1, keepdims=True) + eps)

        def _rmsnorm(x, w, eps=1e-05):
            return x * jax.lax.rsqrt(jnp.mean(x * x, -1, keepdims=True) + eps) * w

        def _causal_dwconv(x, w):
            C = x.shape[-1]
            K = w.shape[-1]
            xp = jnp.pad(x, ((0, 0), (K - 1, 0), (0, 0))).transpose(0, 2, 1)
            y = jax.lax.conv_general_dilated(xp, w[:, None, :], (1,), 'VALID', feature_group_count=C, dimension_numbers=('NCH', 'OIH', 'NCH'))
            return y.transpose(0, 2, 1)

        def _fir(x, filt):
            B, L, h, d = x.shape
            y = _causal_dwconv(x.reshape(B, L, h * d), filt.reshape(h * d, -1))
            return y.reshape(B, L, h, d)

        def _delta_rule_chunkwise(q, k, v, beta):
            b, h, L, dk = q.shape
            dv = v.shape[-1]
            n = L // CHUNK
            q = _l2norm(q)
            k = _l2norm(k)
            v = v * beta[..., None]
            k_beta = k * beta[..., None]
            rs = lambda t: t.reshape(b, h, n, CHUNK, -1)
            q, k, v, k_beta = (rs(q), rs(k), rs(v), rs(k_beta))
            eye = jnp.eye(CHUNK, dtype=q.dtype)
            strict_lower = jnp.tril(jnp.ones((CHUNK, CHUNK), bool), -1)
            A = jnp.where(strict_lower, jnp.einsum('bhncd,bhnsd->bhncs', k_beta, k), 0.0)
            attn_inv = jax.scipy.linalg.solve_triangular(eye + A, jnp.broadcast_to(eye, A.shape), lower=True)
            u = attn_inv @ v
            w = attn_inv @ k_beta
            incl_lower = jnp.tril(jnp.ones((CHUNK, CHUNK), bool))

            def step(S, inp):
                q_i, k_i, u_i, w_i = inp
                attn_local = jnp.where(incl_lower, q_i @ jnp.swapaxes(k_i, -1, -2), 0.0)
                u_t = u_i - w_i @ S
                o_i = q_i @ S + attn_local @ u_t
                return (S + jnp.swapaxes(k_i, -1, -2) @ u_t, o_i)
            S0 = jnp.zeros((b, h, dk, dv), q.dtype)
            xs = tuple((jnp.moveaxis(t, 2, 0) for t in (q, k, u, w)))
            S, out = jax.lax.scan(step, S0, xs)
            return (jnp.moveaxis(out, 0, 2).reshape(b, h, L, dv), S)

        def _stats(x):
            return jnp.stack([x.mean(-1), x.var(-1), jnp.abs(x).mean(-1), jnp.sqrt(jnp.sum(x * x, -1))], -1)

        def _forward(x, Wq, Wk, Wv, Wb, conv_q, conv_k, conv_v, fir_long, fir_short, W1, b1, W2, b2, log_temp, base_bias, conv_residual_logit, rms_w, Wo):
            B, L, D = x.shape
            q = _silu(_causal_dwconv(x @ Wq, conv_q)).reshape(B, L, H, DK)
            k = _silu(_causal_dwconv(x @ Wk, conv_k)).reshape(B, L, H, DK)
            v = _silu(_causal_dwconv(x @ Wv, conv_v)).reshape(B, L, H, DV)
            beta = jax.nn.sigmoid(x @ Wb)
            delta, _S = _delta_rule_chunkwise(q.transpose(0, 2, 1, 3), k.transpose(0, 2, 1, 3), v.transpose(0, 2, 1, 3), beta.transpose(0, 2, 1))
            delta = delta.transpose(0, 2, 1, 3)
            f_short = _fir(v, fir_short)
            f_long = _fir(v, fir_long)
            stats = jnp.concatenate([_stats(f_short), _stats(f_long), _stats(delta), _stats(v)], -1)
            hidden_exp = jnp.broadcast_to(x[:, :, None, :], (B, L, H, D))
            gate_in = jnp.concatenate([hidden_exp, stats], -1)
            h1 = jax.nn.gelu(gate_in @ W1 + b1, approximate=False)
            logits = h1 @ W2 + b2 + base_bias
            temp = jax.nn.softplus(log_temp) + 0.0001
            p = jax.nn.softmax(logits / temp[:, None], -1)
            eps = 0.05
            p = jnp.maximum(p, jnp.array([eps, eps, 0.0, 0.0], p.dtype))
            p = p / jnp.sum(p, -1, keepdims=True)
            o = p[..., 0:1] * f_short + p[..., 1:2] * f_long + p[..., 2:3] * delta + p[..., 3:4] * v
            o = o + 0.5 * jax.nn.sigmoid(conv_residual_logit)[None, None, :, None] * f_short
            o = _rmsnorm(o, rms_w)
            return o.reshape(B, L, H * DV) @ Wo
        key = jax.random.key(seed)
        ks = jax.random.split(key, 13)
        B, L, D = (2, 256, 128)
        f = jnp.float32
        n = lambda k, shape, s=0.02: jax.random.normal(k, shape, f) * s
        return {'x': jax.random.normal(ks[0], (B, L, D), f), 'Wq': n(ks[1], (D, D)), 'Wk': n(ks[2], (D, D)), 'Wv': n(ks[3], (D, D)), 'Wb': n(ks[4], (D, H)), 'conv_q': n(ks[5], (D, 4), 0.1), 'conv_k': n(ks[6], (D, 4), 0.1), 'conv_v': n(ks[7], (D, 4), 0.1), 'fir_long': n(ks[8], (H, DV, 64)), 'fir_short': n(ks[9], (H, DV, 5)), 'W1': n(ks[10], (D + 16, D)), 'b1': jnp.zeros((D,), f), 'W2': n(ks[11], (D, 4)), 'b2': jnp.zeros((4,), f), 'log_temp': jnp.full((H,), float(np.log(np.expm1(0.7))), f), 'base_bias': jnp.tile(jnp.array([-0.5, -0.5, 1.0, 3.0], f), (H, 1)), 'conv_residual_logit': jnp.full((H,), -2.0, f), 'rms_w': jnp.ones((DV,), f), 'Wo': n(ks[12], (D, D))}
    _L1_attn_b_in = _L1_attn_b_setup()

    def _L1_ffn_setup():
        import jax, jax.numpy as jnp
        import numpy as np
        DIM = 128

        def _reference_tuple_inner(x, W_r, W_k, W_v, mu_r, mu_k):
            B, T, C = x.shape
            x_prev = jnp.concatenate([jnp.zeros((B, 1, C), x.dtype), x[:, :-1, :]], axis=1)
            xr = mu_r * x + (1.0 - mu_r) * x_prev
            xk = mu_k * x + (1.0 - mu_k) * x_prev
            r = jax.nn.sigmoid(jnp.einsum('btc,dc->btd', xr, W_r))
            k = jnp.einsum('btc,dc->btd', xk, W_k)
            k_act = jnp.square(jax.nn.relu(k))
            out = r * jnp.einsum('btc,dc->btd', k_act, W_v)
            new_state = x[:, -1, :]
            return (out, new_state)
        key = jax.random.key(seed)
        ks = jax.random.split(key, 6)
        B, T, C = (8, 256, DIM)
        x = jax.random.normal(ks[0], (B, T, C), dtype=jnp.float32)
        s = 1.0 / np.sqrt(C)
        W_r = jax.random.uniform(ks[1], (C, C), jnp.float32, -s, s)
        W_k = jax.random.uniform(ks[2], (C, C), jnp.float32, -s, s)
        W_v = jax.random.uniform(ks[3], (C, C), jnp.float32, -s, s)
        mu_r = jax.random.uniform(ks[4], (C,), jnp.float32)
        mu_k = jax.random.uniform(ks[5], (C,), jnp.float32)
        return {'x': x, 'W_r': W_r, 'W_k': W_k, 'W_v': W_v, 'mu_r': mu_r, 'mu_k': mu_k}
    _L1_ffn_in = _L1_ffn_setup()
    _d = {'L0_attn_a_x': _L0_attn_a_in['x'], 'L0_attn_a_w_qkv': _L0_attn_a_in['w_qkv'], 'L0_attn_a_b_qkv': _L0_attn_a_in['b_qkv'], 'L0_attn_a_w_out': _L0_attn_a_in['w_out'], 'L0_attn_a_b_out': _L0_attn_a_in['b_out'], 'L0_attn_b_wq': _L0_attn_b_in['wq'], 'L0_attn_b_wk': _L0_attn_b_in['wk'], 'L0_attn_b_wv': _L0_attn_b_in['wv'], 'L0_attn_b_wo': _L0_attn_b_in['wo'], 'L0_attn_b_q_norm_w': _L0_attn_b_in['q_norm_w'], 'L0_attn_b_k_norm_w': _L0_attn_b_in['k_norm_w'], 'L0_ffn_W1': _L0_ffn_in['W1'], 'L0_ffn_b1': _L0_ffn_in['b1'], 'L0_ffn_W2': _L0_ffn_in['W2'], 'L0_ffn_b2': _L0_ffn_in['b2'], 'L0_ffn_Wr': _L0_ffn_in['Wr'], 'L0_ffn_br': _L0_ffn_in['br'], 'L1_attn_a_wq': _L1_attn_a_in['wq'], 'L1_attn_a_wk': _L1_attn_a_in['wk'], 'L1_attn_a_wv': _L1_attn_a_in['wv'], 'L1_attn_a_wo': _L1_attn_a_in['wo'], 'L1_attn_b_Wq': _L1_attn_b_in['Wq'], 'L1_attn_b_Wk': _L1_attn_b_in['Wk'], 'L1_attn_b_Wv': _L1_attn_b_in['Wv'], 'L1_attn_b_Wb': _L1_attn_b_in['Wb'], 'L1_attn_b_conv_q': _L1_attn_b_in['conv_q'], 'L1_attn_b_conv_k': _L1_attn_b_in['conv_k'], 'L1_attn_b_conv_v': _L1_attn_b_in['conv_v'], 'L1_attn_b_fir_long': _L1_attn_b_in['fir_long'], 'L1_attn_b_fir_short': _L1_attn_b_in['fir_short'], 'L1_attn_b_W1': _L1_attn_b_in['W1'], 'L1_attn_b_b1': _L1_attn_b_in['b1'], 'L1_attn_b_W2': _L1_attn_b_in['W2'], 'L1_attn_b_b2': _L1_attn_b_in['b2'], 'L1_attn_b_log_temp': _L1_attn_b_in['log_temp'], 'L1_attn_b_base_bias': _L1_attn_b_in['base_bias'], 'L1_attn_b_conv_residual_logit': _L1_attn_b_in['conv_residual_logit'], 'L1_attn_b_rms_w': _L1_attn_b_in['rms_w'], 'L1_attn_b_Wo': _L1_attn_b_in['Wo'], 'L1_ffn_W_r': _L1_ffn_in['W_r'], 'L1_ffn_W_k': _L1_ffn_in['W_k'], 'L1_ffn_W_v': _L1_ffn_in['W_v'], 'L1_ffn_mu_r': _L1_ffn_in['mu_r'], 'L1_ffn_mu_k': _L1_ffn_in['mu_k']}
    _x0 = _d['L0_attn_a_x']
    _d['L0_attn_a_x'] = jax.random.normal(jax.random.fold_in(jax.random.key(seed), 1), (16, 512, 128), dtype=_x0.dtype)
    del _x0
    return _d

def reference(L0_attn_a_x, L0_attn_a_w_qkv, L0_attn_a_b_qkv, L0_attn_a_w_out, L0_attn_a_b_out, L0_attn_b_wq, L0_attn_b_wk, L0_attn_b_wv, L0_attn_b_wo, L0_attn_b_q_norm_w, L0_attn_b_k_norm_w, L0_ffn_W1, L0_ffn_b1, L0_ffn_W2, L0_ffn_b2, L0_ffn_Wr, L0_ffn_br, L1_attn_a_wq, L1_attn_a_wk, L1_attn_a_wv, L1_attn_a_wo, L1_attn_b_Wq, L1_attn_b_Wk, L1_attn_b_Wv, L1_attn_b_Wb, L1_attn_b_conv_q, L1_attn_b_conv_k, L1_attn_b_conv_v, L1_attn_b_fir_long, L1_attn_b_fir_short, L1_attn_b_W1, L1_attn_b_b1, L1_attn_b_W2, L1_attn_b_b2, L1_attn_b_log_temp, L1_attn_b_base_bias, L1_attn_b_conv_residual_logit, L1_attn_b_rms_w, L1_attn_b_Wo, L1_ffn_W_r, L1_ffn_W_k, L1_ffn_W_v, L1_ffn_mu_r, L1_ffn_mu_k):

    def _L0_attn_a_ref(x, w_qkv, b_qkv, w_out, b_out):
        import jax, jax.numpy as jnp
        import numpy as np
        NUM_HEADS = 16
        B, T, C = x.shape
        H = NUM_HEADS
        D = C // H
        qkv = x @ w_qkv + b_qkv
        q, k, v = jnp.split(qkv, 3, axis=-1)
        q = q.reshape(B, T, H, D).transpose(0, 2, 1, 3)
        k = k.reshape(B, T, H, D).transpose(0, 2, 1, 3)
        v = v.reshape(B, T, H, D).transpose(0, 2, 1, 3)
        scale = 1.0 / jnp.sqrt(jnp.asarray(D, dtype=x.dtype))
        scores = jnp.einsum('bhqd,bhkd->bhqk', q, k) * scale
        causal = jnp.tril(jnp.ones((T, T), dtype=bool))
        scores = jnp.where(causal, scores, jnp.asarray(-jnp.inf, dtype=scores.dtype))
        attn = jax.nn.softmax(scores, axis=-1)
        out = jnp.einsum('bhqk,bhkd->bhqd', attn, v)
        out = out.transpose(0, 2, 1, 3).reshape(B, T, C)
        return out @ w_out + b_out

    def _L0_attn_b_ref(x, wq, wk, wv, wo, q_norm_w, k_norm_w):
        import jax, jax.numpy as jnp
        import numpy as np
        DIM, H, KV, HD, WIN = (128, 16, 4, 64, 64)
        EPS = 1e-06

        def rmsnorm(x, w, eps=EPS):
            return x * jax.lax.rsqrt(jnp.mean(x * x, axis=-1, keepdims=True) + eps) * w
        B, T, D = x.shape
        rep = H // KV
        q = (x @ wq.T).reshape(B, T, H, HD)
        k = (x @ wk.T).reshape(B, T, KV, HD)
        v = (x @ wv.T).reshape(B, T, KV, HD)
        q = rmsnorm(q, q_norm_w)
        k = rmsnorm(k, k_norm_w)
        k = jnp.repeat(k, rep, axis=2)
        v = jnp.repeat(v, rep, axis=2)
        scores = jnp.einsum('bqhd,bkhd->bhqk', q, k) / jnp.sqrt(jnp.float32(HD))
        i = jnp.arange(T)[:, None]
        j = jnp.arange(T)[None, :]
        mask = (i >= j) & (i - j < WIN)
        scores = jnp.where(mask, scores, -jnp.inf)
        attn = jax.nn.softmax(scores, axis=-1)
        y = jnp.einsum('bhqk,bkhd->bqhd', attn, v).reshape(B, T, H * HD)
        return y @ wo.T

    def _L0_ffn_ref(x, W1, b1, W2, b2, Wr, br):
        import jax, jax.numpy as jnp
        import numpy as np
        B, S, D, F, E = (4, 256, 128, 512, 8)
        b, s, d = x.shape
        e = Wr.shape[1]
        logits = x @ Wr + br
        idx = jnp.argmax(logits, axis=-1)
        probs = jax.nn.softmax(logits, axis=-1)
        gates = jnp.take_along_axis(probs, idx[..., None], axis=-1)[..., 0]
        xf = x.reshape(-1, d)
        idxf = idx.reshape(-1)
        gf = gates.reshape(-1)
        out = jnp.zeros_like(xf)
        for ei in range(e):
            h = jax.nn.gelu(xf @ W1[ei] + b1[ei], approximate=False)
            y = h @ W2[ei] + b2[ei]
            mask = (idxf == ei).astype(xf.dtype)
            out = out + y * (gf * mask)[:, None]
        return out.reshape(b, s, d)

    def _L1_attn_a_ref(x, wq, wk, wv, wo):
        import jax, jax.numpy as jnp
        import numpy as np
        NUM_HEADS = 16
        HIDDEN = 128
        HEAD_DIM = HIDDEN // NUM_HEADS

        def _rope_cos_sin(S, head_dim):
            inv = 1.0 / 10000.0 ** (jnp.arange(0, head_dim, 2, dtype=jnp.float32) / head_dim)
            t = jnp.arange(S, dtype=jnp.float32)
            ang = jnp.outer(t, inv)
            return (jnp.cos(ang), jnp.sin(ang))

        def _apply_rope(x, cos, sin):
            B, S, nh, hd = x.shape
            xr = x[..., 0::2]
            xi = x[..., 1::2]
            c = cos[None, :, None, :]
            s = sin[None, :, None, :]
            or_ = xr * c - xi * s
            oi_ = xr * s + xi * c
            return jnp.stack([or_, oi_], axis=-1).reshape(B, S, nh, hd)
        B, S, H = x.shape
        nh, hd = (NUM_HEADS, HEAD_DIM)
        xq = jnp.einsum('bsh,oh->bso', x, wq).reshape(B, S, nh, hd)
        xk = jnp.einsum('bsh,oh->bso', x, wk).reshape(B, S, nh, hd)
        xv = jnp.einsum('bsh,oh->bso', x, wv).reshape(B, S, nh, hd)
        cos, sin = _rope_cos_sin(S, hd)
        xq = _apply_rope(xq.astype(jnp.float32), cos, sin).astype(x.dtype)
        xk = _apply_rope(xk.astype(jnp.float32), cos, sin).astype(x.dtype)
        scores = jnp.einsum('bqhd,bkhd->bhqk', xq, xk) / np.sqrt(hd)
        probs = jax.nn.softmax(scores.astype(jnp.float32), axis=-1).astype(xq.dtype)
        out = jnp.einsum('bhqk,bkhd->bqhd', probs, xv).reshape(B, S, nh * hd)
        return jnp.einsum('bso,ho->bsh', out, wo)

    def _L1_attn_b_ref(x, Wq, Wk, Wv, Wb, conv_q, conv_k, conv_v, fir_long, fir_short, W1, b1, W2, b2, log_temp, base_bias, conv_residual_logit, rms_w, Wo):
        import jax, jax.numpy as jnp
        import numpy as np
        H, DK, DV, CHUNK = (4, 32, 32, 32)

        def _silu(x):
            return x * jax.nn.sigmoid(x)

        def _l2norm(x, eps=1e-06):
            return x * jax.lax.rsqrt(jnp.sum(x * x, -1, keepdims=True) + eps)

        def _rmsnorm(x, w, eps=1e-05):
            return x * jax.lax.rsqrt(jnp.mean(x * x, -1, keepdims=True) + eps) * w

        def _causal_dwconv(x, w):
            C = x.shape[-1]
            K = w.shape[-1]
            xp = jnp.pad(x, ((0, 0), (K - 1, 0), (0, 0))).transpose(0, 2, 1)
            y = jax.lax.conv_general_dilated(xp, w[:, None, :], (1,), 'VALID', feature_group_count=C, dimension_numbers=('NCH', 'OIH', 'NCH'))
            return y.transpose(0, 2, 1)

        def _fir(x, filt):
            B, L, h, d = x.shape
            y = _causal_dwconv(x.reshape(B, L, h * d), filt.reshape(h * d, -1))
            return y.reshape(B, L, h, d)

        def _delta_rule_chunkwise(q, k, v, beta):
            b, h, L, dk = q.shape
            dv = v.shape[-1]
            n = L // CHUNK
            q = _l2norm(q)
            k = _l2norm(k)
            v = v * beta[..., None]
            k_beta = k * beta[..., None]
            rs = lambda t: t.reshape(b, h, n, CHUNK, -1)
            q, k, v, k_beta = (rs(q), rs(k), rs(v), rs(k_beta))
            eye = jnp.eye(CHUNK, dtype=q.dtype)
            strict_lower = jnp.tril(jnp.ones((CHUNK, CHUNK), bool), -1)
            A = jnp.where(strict_lower, jnp.einsum('bhncd,bhnsd->bhncs', k_beta, k), 0.0)
            attn_inv = jax.scipy.linalg.solve_triangular(eye + A, jnp.broadcast_to(eye, A.shape), lower=True)
            u = attn_inv @ v
            w = attn_inv @ k_beta
            incl_lower = jnp.tril(jnp.ones((CHUNK, CHUNK), bool))

            def step(S, inp):
                q_i, k_i, u_i, w_i = inp
                attn_local = jnp.where(incl_lower, q_i @ jnp.swapaxes(k_i, -1, -2), 0.0)
                u_t = u_i - w_i @ S
                o_i = q_i @ S + attn_local @ u_t
                return (S + jnp.swapaxes(k_i, -1, -2) @ u_t, o_i)
            S0 = jnp.zeros((b, h, dk, dv), q.dtype)
            xs = tuple((jnp.moveaxis(t, 2, 0) for t in (q, k, u, w)))
            S, out = jax.lax.scan(step, S0, xs)
            return (jnp.moveaxis(out, 0, 2).reshape(b, h, L, dv), S)

        def _stats(x):
            return jnp.stack([x.mean(-1), x.var(-1), jnp.abs(x).mean(-1), jnp.sqrt(jnp.sum(x * x, -1))], -1)

        def _forward(x, Wq, Wk, Wv, Wb, conv_q, conv_k, conv_v, fir_long, fir_short, W1, b1, W2, b2, log_temp, base_bias, conv_residual_logit, rms_w, Wo):
            B, L, D = x.shape
            q = _silu(_causal_dwconv(x @ Wq, conv_q)).reshape(B, L, H, DK)
            k = _silu(_causal_dwconv(x @ Wk, conv_k)).reshape(B, L, H, DK)
            v = _silu(_causal_dwconv(x @ Wv, conv_v)).reshape(B, L, H, DV)
            beta = jax.nn.sigmoid(x @ Wb)
            delta, _S = _delta_rule_chunkwise(q.transpose(0, 2, 1, 3), k.transpose(0, 2, 1, 3), v.transpose(0, 2, 1, 3), beta.transpose(0, 2, 1))
            delta = delta.transpose(0, 2, 1, 3)
            f_short = _fir(v, fir_short)
            f_long = _fir(v, fir_long)
            stats = jnp.concatenate([_stats(f_short), _stats(f_long), _stats(delta), _stats(v)], -1)
            hidden_exp = jnp.broadcast_to(x[:, :, None, :], (B, L, H, D))
            gate_in = jnp.concatenate([hidden_exp, stats], -1)
            h1 = jax.nn.gelu(gate_in @ W1 + b1, approximate=False)
            logits = h1 @ W2 + b2 + base_bias
            temp = jax.nn.softplus(log_temp) + 0.0001
            p = jax.nn.softmax(logits / temp[:, None], -1)
            eps = 0.05
            p = jnp.maximum(p, jnp.array([eps, eps, 0.0, 0.0], p.dtype))
            p = p / jnp.sum(p, -1, keepdims=True)
            o = p[..., 0:1] * f_short + p[..., 1:2] * f_long + p[..., 2:3] * delta + p[..., 3:4] * v
            o = o + 0.5 * jax.nn.sigmoid(conv_residual_logit)[None, None, :, None] * f_short
            o = _rmsnorm(o, rms_w)
            return o.reshape(B, L, H * DV) @ Wo
        return _forward(x, Wq, Wk, Wv, Wb, conv_q, conv_k, conv_v, fir_long, fir_short, W1, b1, W2, b2, log_temp, base_bias, conv_residual_logit, rms_w, Wo)

    def _L1_ffn_ref(x, W_r, W_k, W_v, mu_r, mu_k):
        import jax, jax.numpy as jnp
        import numpy as np
        DIM = 128

        def _reference_tuple_inner(x, W_r, W_k, W_v, mu_r, mu_k):
            B, T, C = x.shape
            x_prev = jnp.concatenate([jnp.zeros((B, 1, C), x.dtype), x[:, :-1, :]], axis=1)
            xr = mu_r * x + (1.0 - mu_r) * x_prev
            xk = mu_k * x + (1.0 - mu_k) * x_prev
            r = jax.nn.sigmoid(jnp.einsum('btc,dc->btd', xr, W_r))
            k = jnp.einsum('btc,dc->btd', xk, W_k)
            k_act = jnp.square(jax.nn.relu(k))
            out = r * jnp.einsum('btc,dc->btd', k_act, W_v)
            new_state = x[:, -1, :]
            return (out, new_state)
        return _reference_tuple_inner(x, W_r, W_k, W_v, mu_r, mu_k)[0]
    x = L0_attn_a_x
    x = x + _L0_attn_a_ref(_layernorm(x, axis=-1), L0_attn_a_w_qkv, L0_attn_a_b_qkv, L0_attn_a_w_out, L0_attn_a_b_out)
    x = x + _L0_ffn_ref(_layernorm(x, axis=-1), L0_ffn_W1, L0_ffn_b1, L0_ffn_W2, L0_ffn_b2, L0_ffn_Wr, L0_ffn_br)
    x = x + _L0_attn_b_ref(_layernorm(x, axis=-1), L0_attn_b_wq, L0_attn_b_wk, L0_attn_b_wv, L0_attn_b_wo, L0_attn_b_q_norm_w, L0_attn_b_k_norm_w)
    x = x + _L0_ffn_ref(_layernorm(x, axis=-1), L0_ffn_W1, L0_ffn_b1, L0_ffn_W2, L0_ffn_b2, L0_ffn_Wr, L0_ffn_br)
    x = x + _L1_attn_a_ref(_layernorm(x, axis=-1), L1_attn_a_wq, L1_attn_a_wk, L1_attn_a_wv, L1_attn_a_wo)
    x = x + _L1_ffn_ref(_layernorm(x, axis=-1), L1_ffn_W_r, L1_ffn_W_k, L1_ffn_W_v, L1_ffn_mu_r, L1_ffn_mu_k)
    x = x + _L1_attn_b_ref(_layernorm(x, axis=-1), L1_attn_b_Wq, L1_attn_b_Wk, L1_attn_b_Wv, L1_attn_b_Wb, L1_attn_b_conv_q, L1_attn_b_conv_k, L1_attn_b_conv_v, L1_attn_b_fir_long, L1_attn_b_fir_short, L1_attn_b_W1, L1_attn_b_b1, L1_attn_b_W2, L1_attn_b_b2, L1_attn_b_log_temp, L1_attn_b_base_bias, L1_attn_b_conv_residual_logit, L1_attn_b_rms_w, L1_attn_b_Wo)
    x = x + _L1_ffn_ref(_layernorm(x, axis=-1), L1_ffn_W_r, L1_ffn_W_k, L1_ffn_W_v, L1_ffn_mu_r, L1_ffn_mu_k)
    return x

_drawn_inputs = setup_inputs


def setup_inputs(seed=0):
    import zlib

    import numpy as np

    out = dict(_drawn_inputs(seed))
    spreads = {'L0_attn_a_b_qkv': (0.0, 0.1),
     'L0_attn_a_b_out': (0.0, 0.1),
     'L0_attn_b_q_norm_w': (1.0, 0.6),
     'L0_attn_b_k_norm_w': (1.0, 0.6),
     'L1_attn_b_b1': (0.0, 0.8),
     'L1_attn_b_b2': (0.0, 0.8),
     'L1_attn_b_log_temp': (0.013658997602760792, 0.6),
     'L1_attn_b_conv_residual_logit': (-2.0, 0.6),
     'L1_attn_b_rms_w': (1.0, 0.2)}
    factors = {'L0_ffn_b1': 5.624,
     'L0_ffn_b2': 4.142,
     'L1_attn_b_Wq': 5.662,
     'L1_attn_b_Wk': 5.624,
     'L1_attn_b_Wb': 8.0,
     'L1_attn_b_conv_q': 5.701,
     'L1_attn_b_conv_k': 5.608,
     'L1_attn_b_fir_long': 8.0,
     'L1_attn_b_fir_short': 8.0,
     'L1_attn_b_W1': 8.0,
     'L1_attn_b_W2': 8.0,
     'L1_ffn_mu_r': 3.272}
    for name, (base, spread) in spreads.items():
        noise = np.random.default_rng([zlib.crc32(name.encode()), seed]).standard_normal(out[name].shape)
        drawn = base * np.exp(spread * noise) if base else spread * noise
        out[name] = jnp.asarray(drawn.astype(out[name].dtype))
    for name, factor in factors.items():
        out[name] = (out[name] * factor).astype(out[name].dtype)
    return out
```

```python
import concourse.bass as bass
from concourse import mybir
from contextlib import ExitStack

F32 = mybir.dt.float32
BF16 = mybir.dt.bfloat16
ACT = mybir.ActivationFunctionType
ALU = mybir.AluOpType
AX = mybir.AxisListType

P = 128
B, T, C = 16, 512, 128
TPS = T // P
NT = B * TPS
LN_EPS = 1e-5
MASKED = -1e30


class Stage:

    def __init__(self, nc, tag):
        self.nc, self.tag, self.stack, self.sems = nc, tag, ExitStack(), []

    def __enter__(self):
        return self

    def __exit__(self, kind, error, trace):
        if kind is None and self.sems:
            self.opened.close()
            for sem in self.sems:
                self.nc.sync.sem_clear(sem)
            self.nc.all_engine_barrier()
            for sem in reversed(self.sems):
                self.nc.release_semaphore(sem)
        return self.stack.__exit__(kind, error, trace)

    def sb(self, name, shape, dt=F32):
        return self.stack.enter_context(self.nc.sbuf_tensor(f"{self.tag}_{name}", shape, dt))

    def ps(self, name, shape, dt=F32):
        return self.stack.enter_context(self.nc.psum_tensor(f"{self.tag}_{name}", shape, dt))

    def sem(self, name):
        self.sems.append(self.nc.alloc_semaphore(f"{self.tag}_{name}"))
        return self.sems[-1]

    def block(self):
        self.opened = ExitStack()
        return self.opened.enter_context(self.nc.Block())

    def dram(self, name, shape, dt=F32):
        return self.nc.dram_tensor(f"{self.tag}_{name}", shape, dt, kind="Internal").ap()


def load_x(nc, io, X, stats, identity, sorted_in):
    with Stage(nc, "load") as s:
        loaded, cleared, zeroed = s.sem("loaded"), s.sem("cleared"), s.sem("zeroed")
        identity_step = s.sem("identity_step")
        zeros = s.sb("zeros", [P, C])
        block = s.block()

        @block.sync
        def _(sp):
            for b in range(0, B, 4):
                sp.dma_start(X[:, b * TPS:(b + 4) * TPS, :],
                             io["x"][b:b + 4].rearrange("b (t p) c -> p (b t) c", p=P)).then_inc(loaded, 16)
            sp.wait_ge(cleared, 1)
            n = sorted_in.shape[0] // 4
            for k in range(0, sorted_in.shape[0], n):
                sp.dma_start(sorted_in[k:k + n].rearrange("k p c -> p k c"),
                             zeros[:, :].unsqueeze(1).to_broadcast([P, n, C])).then_inc(zeroed, 16)
            sp.wait_ge(loaded, 64)
            sp.wait_ge(zeroed, 64)

        @block.vector
        def _(dve):
            nc.vector.memset(zeros[:, :], 0.0).then_inc(cleared, 1)
            nc.vector.memset(X[:, NT:, :], 0.0)
            nc.vector.memset(stats[:, :, :], 0.0)

        @block.gpsimd
        def _(pool):
            nc.gpsimd.memset(identity[:, :], 0.0).then_inc(identity_step, 1)
            pool.wait_ge(identity_step, 1)
            nc.gpsimd.affine_select(out=identity[:, :], in_=identity[:, :], compare_op=ALU.not_equal, fill=1.0,
                                    base=0, pattern=[[-1, P]], channel_multiplier=1)


def store_x(nc, io, X):
    with Stage(nc, "store") as s:
        stored = s.sem("stored")
        block = s.block()

        @block.sync
        def _(sp):
            for b in range(0, B, 4):
                sp.dma_start(io["out"][b:b + 4].rearrange("b (t p) c -> p (b t) c", p=P),
                             X[:, b * TPS:(b + 4) * TPS, :]).then_inc(stored, 16)
            sp.wait_ge(stored, 64)


def layernorm_stats(nc, tag, X, stats):
    with Stage(nc, f"{tag}_ln") as s:
        halves = s.sb("halves", [P, NT, 6])
        root = s.sb("root", [P, NT])
        s_halves, s_var, s_root = s.sem("halves_done"), s.sem("variance_ready"), s.sem("root_ready")
        block = s.block()

        @block.vector
        def _(dve):
            with dve.Fori(0, B) as b:
                for t in range(TPS):
                    last = nc.vector.bn_stats(halves[:, bass.ds(b * TPS + t, 1), :].rearrange("p o k -> p (o k)"),
                                              X[:, bass.ds(b * TPS + t, 1), :].rearrange("p o c -> p (o c)"))
                last.then_inc(s_halves, 1)
            dve.wait_ge(s_halves, B)
            for t in range(NT):
                last = nc.vector.bn_aggr(stats[:, t, :], halves[:, t, :])
            last.then_inc(s_var, 1)
            dve.wait_ge(s_var, 1)
            nc.vector.tensor_scalar(root[:, :], stats[:, 0:NT, 1], LN_EPS, None, ALU.add).then_inc(s_var, 1)
            dve.wait_ge(s_root, 1)
            nc.vector.reciprocal(stats[:, 0:NT, 1], root[:, :])

        @block.scalar
        def _(act):
            act.wait_ge(s_var, 2)
            nc.scalar.activation(root[:, :], root[:, :], ACT.Sqrt).then_inc(s_root, 1)


H, D = 16, 8
STRIP = 32
PAIRS = H // 2
UNITS = TPS * PAIRS
LEAD = PAIRS + 2
PARTS = 3
Q_SLOTS = [(0, 3, 0), (3, 2, 1), (5, 1, 2)]
K_SLOTS = [(0, 3), (3, 2), (5, 1)]
ROWS = 6 * D


def attention16(nc, tag, io, X, stats, identity, causal, rope, biased):
    with Stage(nc, tag) as s:
        w = {n: s.sb(f"w_{n}", [P, C]) for n in (["q", "k", "v", "out"] + (["q_swapped", "k_swapped"] if rope else []))}
        if biased:
            bias_col = s.sb("bias_col", [P, 2])
            bias_row = s.sb("bias_row", [1, 2, C])
            ones_row = s.sb("ones_row", [1, P])
        if rope:
            cos, sin = s.sb("cos", [P, T]), s.sb("sin", [P, T])
            rot = s.sb("rot", [P, 2, T])
        if causal:
            ident16 = s.sb("ident16", [P, P], BF16)
            mask_qk, mask_kq = s.sb("mask_qk", [P, P], BF16), s.sb("mask_kq", [P, P], BF16)
        hn = s.sb("hn", [P, TPS, C])
        hT = s.sb("hT", [P, T])
        qk = s.sb("qk", [P, 2, T])
        rest = s.sb("rest", [P, 2, T])
        parts = s.sb("parts", [P, 2, PARTS, T], BF16)
        QS = s.sb("QS", [P, 2, PAIRS, T], BF16)
        KS = s.sb("KS", [P, 2, PAIRS, T], BF16)
        V = s.sb("V", [P, 2, TPS, H, STRIP])
        M = s.sb("M", [P, 2, H])
        MT = s.sb("MT", [H, 2, P], BF16)
        probs = s.sb("probs", [P, 2, 2, T])
        rec = s.sb("rec", [P, H])
        heads_out = s.sb("heads_out", [P, T])
        on = s.sb("on", [P, C])
        oT = s.sb("oT", [P, P])
        parts_dram = s.dram("parts_dram", (2, 2, PARTS, P, T), BF16)
        max_bank = s.ps("max_bank", [P, 2, T])
        exp_bank = s.ps("exp_bank", [P, 2, 2, T])
        out_bank = s.ps("out_bank", [P, H // 4, P])
        misc = s.ps("misc", [P, T])

        loaded = s.sem("weights_loaded")
        prepared = s.sem("constants_ready")
        hn_ready = s.sem("hn_ready")
        misc_full, misc_free = s.sem("misc_full"), s.sem("misc_free")
        rotated = s.sem("rotated")
        split_step = s.sem("split_step")
        split_q, split_k = s.sem("split_q"), s.sem("split_k")
        parts_out = s.sem("parts_out")
        qk_in = [s.sem(f"qk_in{n}") for n in range(2)]
        max_scores, max_done = s.sem("max_scores"), s.sem("max_done")
        shift_in = [s.sem(f"shift_in{n}") for n in range(2)]
        scores, exp_done, pv_done = s.sem("scores"), s.sem("exp_done"), s.sem("pv_done")
        heads_kept, v_cleared = s.sem("heads_kept"), s.sem("v_cleared")
        rec_ready, waited = s.sem("rec_ready"), s.sem("waited")

        LOADED = 16 * (4 + (4 if rope else 0) + (4 if biased else 0))
        PREPARED = 3 + (1 if biased else 0) + (3 if causal else 0)

        if rope:
            early = [(1, "HT"), (2, "Q"), (3, "QS"), (4, "K"), (5, "KS"), (7, "V")]
        else:
            early = [(1, "HT"), (2, "Q"), (3, "K"), (5, "V")]
        uses = early + [(8 * t + 6, ("MAX", t + 1)) for t in range(4)]
        uses += [(8 * t + 10 + k, (what, t)) for t in range(3) for k, what in enumerate(("HEADS", "OT", "Y"))]
        uses = sorted(uses, key=lambda e: e[0]) + [(UNITS, ("HEADS", 3)), (UNITS, ("OT", 3)), (UNITS, ("Y", 3))]
        NM = len(uses)
        first = [e for e in uses if e[1] in [x[1] for x in early] or e[1] == ("MAX", 4)]
        NF = len(first)

        def at(b, n, c):
            return (b + 1) * n + c

        def steps(b, prologue):
            if prologue:
                return [(u, what, NM - NF + j) for j, (u, what) in enumerate(first)]
            return [(u, what, j) for j, (u, what) in enumerate(uses)]

        units = range(UNITS + 1)
        W = [P * (t + 1) if causal else T for t in range(TPS)]

        def in_body(u, prologue):
            return u < UNITS and (not prologue or u + LEAD >= UNITS)

        def wait(eng, sem, value):
            if not isinstance(value, int) or value > 0:
                eng.wait_ge(sem, value)

        def pairs_of(body):
            def run(eng):
                body(eng, -1, 1, True, -1)
                with eng.Fori(0, B // 2) as i:
                    body(eng, i * 2, 0, False, i)
                    body(eng, i * 2 + 1, 1, False, i)
            return run

        block = s.block()

        @block.sync
        def _(sp):
            names = [("q", "w_q"), ("k", "w_k"), ("v", "w_v"), ("out", "w_out")]
            names += [("q_swapped", "w_q_swapped"), ("k_swapped", "w_k_swapped")] if rope else []
            for n, (a, key) in enumerate(names):
                sp.dma_start(w[a][:, :], io[key]).then_inc(loaded, 16)
            if rope:
                sp.dma_start(cos[:, :], io["cos"]).then_inc(loaded, 16)
                sp.dma_start(sin[:, :], io["sin"]).then_inc(loaded, 16)
            if biased:
                for j, key in enumerate(("b_q", "b_k")):
                    sp.dma_start(bias_col[:, j:j + 1], io[key].unsqueeze(1)).then_inc(loaded, 16)
                for j, key in enumerate(("b_v", "b_out")):
                    sp.dma_start(bias_row[:, j, :], io[key].unsqueeze(0)).then_inc(loaded, 16)


            def body(sp, b, par, prologue, half):
                index = {what: j for _, what, j in steps(b, prologue)}

                def rows(t):
                    sp.wait_ge(misc_free, at(b, NM, index["MAX", t] + 1))
                    tt = t % 4
                    to = (par + 1) % 2 if t == 4 else par
                    for g in range(2):
                        sp.dma_start(QS[64 * g + ROWS:64 * g + ROWS + 1, to, :, tt * P:(tt + 1) * P],
                                     MT[g:H:2, tt % 2, :]).then_inc(shift_in[tt % 2], 16)
                if not prologue:
                    rows(1)
                to = (par + 1) % 2
                for j, done in enumerate((split_q, split_k)):
                    sp.wait_ge(done, b + 2)
                    sp.dma_start(parts_dram[to, j].rearrange("s p n -> p s n"), parts[:, j]).then_inc(parts_out, 16)
                sp.wait_ge(parts_out, (b + 2) * 32)
                sp.sem_inc(waited, 1)
                sp.wait_ge(scores, at(b, UNITS, 0))
                for g in range(2):
                    for s0, n, part in Q_SLOTS:
                        src = parts_dram[to, 0, part].rearrange("(i g d) n -> g d i n", g=2, d=D)[g]
                        for k in range(n):
                            r = 64 * g + (s0 + k) * D
                            sp.dma_start(QS[r:r + D, to, :, :], src).then_inc(qk_in[to], 16)
                    for s0, n in K_SLOTS:
                        for k in range(n):
                            src = parts_dram[to, 1, k].rearrange("(i g d) n -> g d i n", g=2, d=D)[g]
                            r = 64 * g + (s0 + k) * D
                            sp.dma_start(KS[r:r + D, to, :, :], src).then_inc(qk_in[to], 16)
                if not prologue:
                    rows(2)
                    rows(3)
                rows(4)

            sp.wait_ge(prepared, PREPARED)
            pairs_of(body)(sp)
            sp.wait_ge(shift_in[0], 32 * (2 * B + 1))
            sp.wait_ge(shift_in[1], 32 * 2 * B)
            sp.wait_ge(qk_in[0], 16 * 24 * (B // 2 + 1))

        @block.gpsimd
        def _(pool):
            nc.gpsimd.memset(KS[:, :, :, :], 1.0).then_inc(prepared, 1)
            nc.gpsimd.memset(V[:, :, :, :, :], 0.0).then_inc(v_cleared, 1)
            pool.wait_ge(v_cleared, 1)
            nc.gpsimd.memset(V[:, :, :, :, D], 1.0).then_inc(prepared, 1)
            if biased:
                nc.gpsimd.memset(ones_row[:, :], 1.0).then_inc(prepared, 1)
            if causal:
                nc.gpsimd.memset(mask_qk[:, :], 0.0).then_inc(split_step, 1)
                nc.gpsimd.memset(mask_kq[:, :], 0.0).then_inc(split_step, 1)
                pool.wait_ge(split_step, 2)
                nc.gpsimd.affine_select(out=mask_qk[:, :], in_=mask_qk[:, :], compare_op=ALU.is_ge, fill=MASKED,
                                        base=0, pattern=[[-1, P]], channel_multiplier=1).then_inc(prepared, 1)
                nc.gpsimd.affine_select(out=mask_kq[:, :], in_=mask_kq[:, :], compare_op=ALU.is_ge, fill=MASKED,
                                        base=0, pattern=[[1, P]], channel_multiplier=-1).then_inc(prepared, 1)
                nc.gpsimd.tensor_copy(ident16[:, :], identity[:, :]).then_inc(prepared, 1)
            step0 = 2 if causal else 0
            pool.wait_ge(loaded, LOADED)

            def body(pool, b, par, prologue, half):
                index = {what: j for _, what, j in steps(b, prologue)}
                NS = 10 if rope else 6
                count = [step0]

                def chained(ins):
                    count[0] += 1
                    ins.then_inc(split_step, 1)
                    pool.wait_ge(split_step, (b + 1) * NS + count[0])
                    pool.sem_inc(waited, 1)

                for j, (raw, swapped, done) in enumerate((("Q", "QS", split_q), ("K", "KS", split_k))):
                    pool.wait_ge(misc_free, at(b, NM, index[swapped if rope else raw] + 1))
                    v = qk[:, j]
                    if rope:
                        chained(nc.gpsimd.tensor_tensor(v, v, cos[:, :], ALU.mult))
                        nc.gpsimd.tensor_tensor(rot[:, j], rot[:, j], sin[:, :], ALU.mult).then_inc(rotated, 1)
                        pool.wait_ge(rotated, (b + 1) * 2 + j + 1)
                        chained(nc.gpsimd.tensor_tensor(v, v, rot[:, j], ALU.add))
                    if not prologue:
                        pool.wait_ge(parts_out, (b + 1) * 32)
                        pool.sem_inc(waited, 1)
                    chained(nc.gpsimd.tensor_copy(parts[:, j, 0], v))
                    chained(nc.gpsimd.tensor_tensor(rest[:, j], v, parts[:, j, 0], ALU.subtract))
                    chained(nc.gpsimd.tensor_copy(parts[:, j, 1], rest[:, j]))
                    nc.gpsimd.tensor_tensor(parts[:, j, 2], rest[:, j], parts[:, j, 1], ALU.subtract)\
                        .then_inc(done, 1)

            pairs_of(body)(pool)

        @block.tensor
        def _(pe):
            pe.sem_inc(misc_full, NM - NF)
            pe.sem_inc(max_scores, 2 * (UNITS - LEAD))
            pe.sem_inc(scores, UNITS)
            pe.sem_inc(pv_done, UNITS)
            pe.wait_ge(loaded, LOADED)
            pe.wait_ge(prepared, PREPARED)

            def pv(b, par, u):
                t, i = u // PAIRS, u % PAIRS
                pe.wait_ge(exp_done, at(b, UNITS, u + 1))
                if i == 0:
                    pe.wait_ge(heads_kept, at(b, TPS, t))
                for g in range(2):
                    h = 2 * i + g
                    strip = slice(STRIP * (h % 4), STRIP * (h % 4 + 1))
                    nk = t + 1 if causal else TPS
                    for kb in range(nk):
                        last = nc.tensor.matmul(out_bank[strip, h // 4, :], V[:, par, kb, h, :],
                                                probs[:, u % 2, g, kb * P:(kb + 1) * P],
                                                start=(kb == 0), stop=(kb == nk - 1))
                last.then_inc(pv_done, 1)

            def body(pe, b, par, prologue, half):
                to = (par + 1) % 2
                uses_at = {}
                for u, what, j in steps(b, prologue):
                    uses_at.setdefault(u, []).append((what, j))

                def misc_use(what, j):
                    if not (prologue and what == "HT"):
                        pe.wait_ge(misc_free, at(b, NM, j))
                    if what == "HT":
                        pe.wait_ge(hn_ready, b + 2)
                        for t in range(TPS):
                            last = nc.tensor.transpose(misc[:, t * P:(t + 1) * P], hn[:, t, :], identity[:, :])
                    elif what in ("Q", "K", "QS", "KS"):
                        name = {"Q": "q", "K": "k", "QS": "q_swapped", "KS": "k_swapped"}[what]
                        last = nc.tensor.matmul(misc[:, :], w[name][:, :], hT[:, :], start=True, stop=True)
                    elif what == "V":
                        for t in range(TPS):
                            o = misc[:, t * P:(t + 1) * P]
                            last = nc.tensor.matmul(o, hT[:, t * P:(t + 1) * P], w["v"][:, :],
                                                    start=True, stop=not biased)
                            if biased:
                                last = nc.tensor.matmul(o, ones_row[:, :], bias_row[:, 0, :], start=False, stop=True)
                    elif what[0] == "MAX":
                        tt = what[1] % 4
                        pe.wait_ge(max_done, at(b, 2 * UNITS, 2 * u))
                        last = nc.tensor.transpose(misc[0:H, 0:P], M[:, tt % 2, :], identity[:, :])
                    elif what[0] == "HEADS":
                        pe.wait_ge(heads_kept, at(b, TPS, what[1] + 1))
                        for k in range(H // 4):
                            last = nc.tensor.transpose(misc[:, k * P:(k + 1) * P], heads_out[:, k * P:(k + 1) * P],
                                                       identity[:, :])
                    elif what[0] == "OT":
                        last = nc.tensor.transpose(misc[:, 0:P], on[:, :], identity[:, :])
                    else:
                        last = nc.tensor.matmul(misc[:, 0:C], oT[:, :], w["out"][:, :], start=True, stop=not biased)
                        if biased:
                            last = nc.tensor.matmul(misc[:, 0:C], ones_row[:, :], bias_row[:, 1, :],
                                                    start=False, stop=True)
                    last.then_inc(misc_full, 1)

                for u in units:
                    if u == UNITS and not prologue:
                        pv(b, par, UNITS - 1)
                    for what, j in uses_at.get(u, []):
                        misc_use(what, j)
                    if in_body(u, prologue):
                        n = u + LEAD
                        pb = to if n >= UNITS else par
                        t, i = (n % UNITS) // PAIRS, n % PAIRS
                        if n == UNITS:
                            pe.wait_ge(qk_in[pb], 16 * 24 * (half + (par + 1) // 2 + 1))
                        for g in range(2):
                            if not (prologue and u + LEAD == UNITS):
                                pe.wait_ge(max_done, at(b, 2 * UNITS, 2 * u + g - 1))
                            last = nc.tensor.matmul(max_bank[:, g, 0:W[t]],
                                                    QS[64 * g:64 * g + ROWS, pb, i, t * P:(t + 1) * P],
                                                    KS[64 * g:64 * g + ROWS, pb, i, 0:W[t]],
                                                    start=True, stop=True)
                            if causal:
                                last = nc.tensor.matmul(max_bank[:, g, t * P:(t + 1) * P], ident16[:, :],
                                                        mask_qk[:, :], start=False, stop=True, skip_group_check=True)
                            last.then_inc(max_scores, 1)
                    if u < UNITS and not prologue:
                        t, i = u // PAIRS, u % PAIRS
                        if i == 0:
                            pe.wait_ge(shift_in[t % 2], 32 * (2 * b + t // 2 + 1))
                        pe.wait_ge(exp_done, at(b, UNITS, u - 1))
                        for g in range(2):
                            nk = t + 1 if causal else TPS
                            for kb in range(nk):
                                diagonal = causal and kb == t
                                o = exp_bank[:, u % 2, g, kb * P:(kb + 1) * P]
                                last = nc.tensor.matmul(o, KS[64 * g:64 * g + ROWS + 1, par, i, kb * P:(kb + 1) * P],
                                                        QS[64 * g:64 * g + ROWS + 1, par, i, t * P:(t + 1) * P],
                                                        start=True, stop=not diagonal)
                                if diagonal:
                                    last = nc.tensor.matmul(o, ident16[:, :], mask_kq[:, :], start=False, stop=True)
                        last.then_inc(scores, 1)
                        if u >= 1:
                            pv(b, par, u - 1)

            pairs_of(body)(pe)

        @block.scalar
        def _(act):
            act.sem_inc(misc_free, NM - NF)
            act.sem_inc(exp_done, UNITS)
            act.sem_inc(heads_kept, TPS)
            if biased:
                act.wait_ge(loaded, LOADED)

            def keep_heads(b, t):
                act.wait_ge(pv_done, at(b, UNITS, (t + 1) * PAIRS))
                nc.scalar.activation(heads_out[:, :], out_bank[:, :, :].rearrange("p k n -> p (k n)"), ACT.Copy)\
                    .then_inc(heads_kept, 1)

            def body(act, b, par, prologue, half):
                to = (par + 1) % 2
                for u in units:
                    if not prologue and (u == UNITS or u % PAIRS == 1 and u > 1):
                        keep_heads(b, (u - 1) // PAIRS - (u != UNITS))
                    for _, what, j in [e for e in steps(b, prologue) if e[0] == u]:
                        if what in ("HT", "Q", "K", "QS", "KS", "V") or what[0] in ("MAX", "OT"):
                            act.wait_ge(misc_full, at(b, NM, j + 1))
                        if what == "HT":
                            nc.scalar.activation(hT[:, :], misc[:, :], ACT.Copy).then_inc(misc_free, 1)
                        elif what in ("Q", "K", "QS", "KS"):
                            side = 0 if what[0] == "Q" else 1
                            if not prologue:
                                act.wait_ge((split_q, split_k)[side], b + 1)
                            dst = qk[:, side] if len(what) == 1 else rot[:, side]
                            if biased:
                                nc.scalar.activation(dst, misc[:, :], ACT.Identity,
                                                     bias=bias_col[:, side:side + 1]).then_inc(misc_free, 1)
                            else:
                                nc.scalar.activation(dst, misc[:, :], ACT.Copy).then_inc(misc_free, 1)
                        elif what == "V":
                            if prologue:
                                act.wait_ge(prepared, PREPARED)
                            nc.scalar.activation(V[:, to, :, :, 0:D],
                                                 misc[:, :].rearrange("p (t h d) -> p t h d", t=TPS, d=D),
                                                 ACT.Copy).then_inc(misc_free, 1)
                        elif what[0] == "MAX":
                            tt = what[1] % 4
                            nb = b + 1 if what[1] == 4 else b
                            if not prologue:
                                act.wait_ge(shift_in[tt % 2], 32 * (2 * nb + tt // 2))
                            nc.scalar.activation(MT[:, tt % 2, :], misc[0:H, 0:P], ACT.Copy, scale=-1.0)\
                                .then_inc(misc_free, 1)
                        elif what[0] == "OT":
                            nc.scalar.activation(oT[:, :], misc[:, 0:P], ACT.Copy).then_inc(misc_free, 1)
                    if u < UNITS and not prologue:
                        t = u // PAIRS
                        act.wait_ge(scores, at(b, UNITS, u + 1))
                        act.wait_ge(pv_done, at(b, UNITS, u - 1))
                        nc.scalar.activation(probs[:, u % 2, :, 0:W[t]], exp_bank[:, u % 2, :, 0:W[t]], ACT.Exp,
                                             scale=float(D) ** -0.5).then_inc(exp_done, 1)

            pairs_of(body)(act)

        @block.vector
        def _(dve):
            nc.vector.memset(QS[:, :, :, :], 0.0).then_inc(prepared, 1)
            dve.sem_inc(max_done, 2 * (UNITS - LEAD))

            def normalise(b, t):
                heads = misc[:, :].rearrange("p (h d) -> p h d", d=STRIP)
                nc.vector.reciprocal(rec[:, :], heads[:, :, D]).then_inc(rec_ready, 1)
                dve.wait_ge(rec_ready, b * TPS + t + 1)
                nc.vector.tensor_tensor(on[:, :].rearrange("p (h d) -> p h d", d=D), heads[:, :, 0:D],
                                        rec[:, :].unsqueeze(2).to_broadcast([P, H, D]), ALU.mult)\
                    .then_inc(misc_free, 1)

            def body(dve, b, par, prologue, half):
                if not prologue:
                    dve.wait_ge(misc_full, at(b, NM, 0))
                for t in range(TPS):
                    tile = bass.ds((b + 1) * TPS + t, 1)
                    last = nc.vector.tensor_scalar(hn[:, t, :], X[:, tile, :].rearrange("p o c -> p (o c)"),
                                                   stats[:, tile, 0], stats[:, tile, 1], ALU.subtract, ALU.mult)
                last.then_inc(hn_ready, 1)
                for u in units:
                    for _, what, j in [e for e in steps(b, prologue) if e[0] == u]:
                        if what[0] == "HEADS":
                            dve.wait_ge(misc_full, at(b, NM, j + 1))
                            normalise(b, what[1])
                        if what[0] == "Y":
                            tile = bass.ds(b * TPS + what[1], 1)
                            dve.wait_ge(misc_full, at(b, NM, j + 1))
                            x = X[:, tile, :].rearrange("p o c -> p (o c)")
                            nc.vector.tensor_tensor(x, x, misc[:, 0:C], ALU.add).then_inc(misc_free, 1)
                    if in_body(u, prologue):
                        n = (u + LEAD) % UNITS
                        t, i = n // PAIRS, n % PAIRS
                        for g in range(2):
                            dve.wait_ge(max_scores, at(b, 2 * UNITS, 2 * u + g + 1))
                            nc.vector.reduce_max(M[:, t % 2, 2 * i + g:2 * i + g + 1], max_bank[:, g, 0:W[t]], AX.X)\
                                .then_inc(max_done, 1)

            pairs_of(body)(dve)


E, FF = 8, 512
FC = FF // P
SORTED = NT + E
SPARE = 4
B1_AT = 2 * FF


def tile_of(x, tile):
    return x[:, bass.ds(tile, 1), :].rearrange("p o c -> p (o c)")


def mixture(nc, tag, io, X, stats, identity, sorted_in, sorted_out):
    with Stage(nc, tag) as s:
        w_router, b_router = s.sb("w_router", [P, E]), s.sb("b_router", [P, E])
        experts = s.sb("experts", [P, E, B1_AT + FC])
        b2 = s.sb("b2", [1, E, C])
        ones_row = s.sb("ones_row", [1, P])
        hn, hT = s.sb("hn", [P, 2, TPS, C]), s.sb("hT", [P, 2, T])
        L = s.sb("L", [P, NT, E])
        top, total, gate = s.sb("top", [P, NT]), s.sb("total", [P, NT]), s.sb("gate", [P, NT])
        ex = s.sb("ex", [P, NT, E])
        chosen = s.sb("chosen", [P, NT, E], BF16)
        iota_e, iota_k = s.sb("iota_e", [P, E]), s.sb("iota_k", [P, SORTED + SPARE])
        before, ones16 = s.sb("before", [P, P], BF16), s.sb("ones16", [P, P], BF16)
        upto = s.sb("upto", [P, E, E])
        tile_counts = s.sb("tile_counts", [NT, E], BF16)
        earlier = s.sb("earlier", [NT, NT, E], BF16)
        n_int, n_tiles = s.sb("n_int", [P, E], mybir.dt.int32), s.sb("n_tiles", [P, E])
        ends_by = s.sb("ends_by", [P, E, E])
        ends, base = s.sb("ends", [P, E]), s.sb("base", [P, E])
        place = s.sb("place", [P, NT])
        place_int = s.sb("place_int", [P, NT + 2 * TPS], mybir.dt.int32)
        past = s.sb("past", [1, SORTED + SPARE, E])
        expert_of = s.sb("expert_of", [1, SORTED + SPARE])
        expert_int = s.sb("expert_int", [1, SORTED + SPARE], mybir.dt.int32)
        index = s.sb("index", [P, 2, TPS], mybir.dt.int32)
        rows = s.sb("rows", [P, 4, C])
        rowsT = s.sb("rowsT", [P, 2, P])
        own = s.sb("own", [P, 4, B1_AT + FC])
        own_b2 = s.sb("own_b2", [1, 4, C])
        hidden = s.sb("hidden", [P, 2, FC, P])
        result = s.sb("result", [P, 4, C])
        back = s.sb("back", [P, 2, TPS, C])

        t_bank = s.ps("t_bank", [P, 2, T])
        small_bank = s.ps("small_bank", [P, 2, T])
        up_bank = s.ps("up_bank", [P, 2, T])
        down_bank = s.ps("down_bank", [P, 2, T])

        loaded, made = s.sem("weights_loaded"), s.sem("constants_made")
        hn_ready, turned, hT_ready = s.sem("hn_ready"), s.sem("turned"), s.sem("hT_ready")
        logits_done, logits_kept = s.sem("logits_done"), s.sem("logits_kept")
        step, shifted_ready, exp_ready = s.sem("step"), s.sem("shifted_ready"), s.sem("exp_ready")
        chosen_ready, counts_done, counts_kept = s.sem("chosen_ready"), s.sem("counts_done"), s.sem("counts_kept")
        places_done, places_kept = s.sem("places_done"), s.sem("places_kept")
        scatter_ready = s.sem("scatter_ready")
        rows_in = [s.sem(f"rows_in{n}") for n in range(4)]
        rows_turned, rowsT_ready = s.sem("rows_turned"), s.sem("rowsT_ready")
        own_ready, up_done, gelu_done = s.sem("own_ready"), s.sem("up_done"), s.sem("gelu_done")
        down_done, result_ready = s.sem("down_done"), s.sem("result_ready")
        stored = [s.sem(f"stored{n}") for n in range(4)]
        index_ready, added = s.sem("index_ready"), s.sem("added")
        scattered = [nc.alloc_semaphore(f"{tag}_scattered{n}") for n in range(2)]
        gathered = [nc.alloc_semaphore(f"{tag}_gathered{n}") for n in range(2)]
        waited = s.sem("waited")

        LOADED = 16 * (5 + E)
        MADE = 11
        block = s.block()

        @block.sync
        def _(sp):
            sp.dma_start(w_router[:, :], io["w_router"]).then_inc(loaded, 16)
            sp.dma_start(b_router[:, :], io["b_router"].partition_broadcast(P)).then_inc(loaded, 16)
            sp.dma_start(experts[:, :, 0:FF], io["w1"].rearrange("e c f -> c e f")).then_inc(loaded, 16)
            for e in range(E):
                sp.dma_start(experts[:, e, FF:2 * FF].rearrange("p (q c) -> p q c", q=FC),
                             io["w2"][e].rearrange("(q p) c -> p q c", p=P)).then_inc(loaded, 16)
            sp.dma_start(experts[:, :, B1_AT:], io["b1"]).then_inc(loaded, 16)
            sp.dma_start(b2[:, :, :], io["b2"].unsqueeze(0)).then_inc(loaded, 16)
            for n in range(4):
                sp.sem_inc(stored[n], 16)
            for n in range(2):
                sp.wait_ge(scattered[n], 16 * TPS * (B // 2))

            def load(k, n):
                sp.dma_start(rows[:, n, :], sorted_in[bass.ds(k, 1)].rearrange("o p c -> p (o c)"))\
                  .then_inc(rows_in[n], 16)
            for n in range(4):
                load(n, n)
            with sp.Fori(0, SORTED // 4) as i:
                for n in range(4):
                    k = i * 4 + n
                    sp.wait_ge(rows_turned, k + 1)
                    load(k + 4, n)
                    sp.wait_ge(result_ready, k + 3)
                    sp.dma_start(sorted_out[bass.ds(k, 1)].rearrange("o p c -> p (o c)"), result[:, n, :])\
                      .then_inc(stored[n], 16)
            for n in range(4):
                sp.wait_ge(rows_in[n], 16 * (SORTED // 4 + 1))

        @block.gpsimd
        def _(pool):
            g = nc.gpsimd
            g.iota(iota_e[:, :], pattern=[[1, E]], base=0, channel_multiplier=0,
                   allow_small_or_imprecise_dtypes=True).then_inc(made, 1)
            g.iota(iota_k[:, :], pattern=[[1, SORTED + SPARE]], base=0, channel_multiplier=0,
                   allow_small_or_imprecise_dtypes=True).then_inc(made, 1)
            g.memset(ones16[:, :], 1.0).then_inc(made, 1)
            g.memset(before[:, :], 1.0).then_inc(made, 1)
            g.memset(upto[:, :, :], 1.0).then_inc(made, 1)
            g.memset(earlier[:, :, :], 1.0).then_inc(made, 1)
            g.memset(ones_row[:, :], 1.0).then_inc(made, 1)
            g.memset(place_int[:, NT:], 0).then_inc(made, 1)
            pool.wait_ge(made, 8)
            g.affine_select(out=before[:, :], in_=before[:, :], compare_op=ALU.is_gt, fill=0.0, base=0,
                            pattern=[[1, P]], channel_multiplier=-1).then_inc(made, 1)
            g.affine_select(out=upto[:, :, :], in_=upto[:, :, :], compare_op=ALU.is_ge, fill=0.0, base=0,
                            pattern=[[1, E], [-1, E]], channel_multiplier=0).then_inc(made, 1)
            g.affine_select(out=earlier[:, :, :], in_=earlier[:, :, :], compare_op=ALU.is_gt, fill=0.0, base=0,
                            pattern=[[1, NT], [0, E]], channel_multiplier=-1).then_inc(made, 1)
            with pool.Fori(0, B // 2) as i:
                for n in range(2):
                    pool.wait_ge(scatter_ready, i * 2 + n + 1)
                    pool.sem_inc(waited, 1)
                    for t in range(TPS):
                        g.indirect_dma_start(out=sorted_in.rearrange("k p c -> (k p) c"),
                                             out_offset=bass.IndirectOffsetOnAxis(ap=index[:, n, t:t + 1], axis=0),
                                             in_=hn[:, n, t, :], in_offset=None).then_inc(scattered[n], 16)
            for n in range(4):
                pool.wait_ge(stored[n], 16 * (SORTED // 4 + 1))
            with pool.Fori(0, B // 2) as i:
                for n in range(2):
                    pool.wait_ge(index_ready, i * 2 + n + 1)
                    pool.sem_inc(waited, 1)
                    pool.wait_ge(added, i * 2 + n + 1)
                    pool.sem_inc(waited, 1)
                    for t in range(TPS):
                        g.indirect_dma_start(out=back[:, n, t, :], out_offset=None,
                                             in_=sorted_out.rearrange("k p c -> (k p) c"),
                                             in_offset=bass.IndirectOffsetOnAxis(ap=index[:, n, t:t + 1], axis=0))\
                         .then_inc(gathered[n], 16)

        @block.tensor
        def _(pe):
            pe.wait_ge(loaded, LOADED)
            pe.wait_ge(made, MADE)
            pe.sem_inc(turned, 1)
            pe.sem_inc(down_done, 2)
            with pe.Fori(0, B // 2) as i:
                for n in range(2):
                    b = i * 2 + n
                    pe.wait_ge(hn_ready, b + 1)
                    pe.wait_ge(hT_ready, b + 1)
                    for t in range(TPS):
                        last = nc.tensor.transpose(t_bank[:, n, t * P:(t + 1) * P], hn[:, n, t, :], identity[:, :])
                    last.then_inc(turned, 1)
                    pe.wait_ge(hT_ready, b + 3)
                    pe.wait_ge(logits_kept, b + 1)
                    for t in range(TPS):
                        last = nc.tensor.matmul(small_bank[:, n, t * E:(t + 1) * E], hT[:, n, t * P:(t + 1) * P],
                                                w_router[:, :], start=True, stop=True)
                    last.then_inc(logits_done, 1)
            pe.wait_ge(chosen_ready, 1)
            for e in range(E):
                last = nc.tensor.matmul(small_bank[0:NT, 0, e:e + 1], chosen[:, :, e], ones16[:, 0:1],
                                        start=True, stop=True)
            last.then_inc(counts_done, 1)
            pe.wait_ge(counts_kept, 1)
            nc.tensor.matmul(t_bank[:, 0, :], before[:, :], chosen[:, :, :].rearrange("p t e -> p (t e)"),
                             start=True, stop=False)
            nc.tensor.matmul(t_bank[:, 0, :], ones16[0:NT, :], earlier[:, :, :].rearrange("p t e -> p (t e)"),
                             start=False, stop=True)
            nc.tensor.matmul(small_bank[:, 1, 0:E], ones16[0:NT, :], tile_counts[:, :], start=True, stop=True)\
              .then_inc(places_done, 1)

            def turn(k, n4, n2):
                pe.wait_ge(rows_in[n4], 16 * (k[0] + k[1] + 1))
                nc.tensor.transpose(t_bank[:, n2, 0:P], rows[:, n4, :], identity[:, :]).then_inc(rows_turned, 1)

            def up(n4, n2):
                for f in range(FC):
                    last = nc.tensor.matmul(up_bank[:, n2, f * P:(f + 1) * P], own[:, n4, f * P:(f + 1) * P],
                                            rowsT[:, n2, :], start=True, stop=True)
                last.then_inc(up_done, 1)

            def down(n4, n2):
                for f in range(FC):
                    nc.tensor.matmul(down_bank[:, n2, 0:C], hidden[:, n2, f, :],
                                     own[:, n4, FF + f * C:FF + (f + 1) * C], start=(f == 0), stop=False)
                nc.tensor.matmul(down_bank[:, n2, 0:C], ones_row[:, :], own_b2[:, n4, :], start=False, stop=True)\
                  .then_inc(down_done, 1)

            pe.wait_ge(places_kept, 1)
            turn((0, 0), 0, 0)
            turn((0, 0), 1, 1)
            pe.wait_ge(rowsT_ready, 1)
            pe.wait_ge(own_ready, 1)
            up(0, 0)
            with pe.Fori(0, SORTED // 4) as i:
                for n in range(4):
                    k = i * 4 + n
                    pe.wait_ge(rowsT_ready, k + 2)
                    turn((i, (n + 2) // 4), (n + 2) % 4, n % 2)
                    pe.wait_ge(own_ready, k + 2)
                    pe.wait_ge(gelu_done, k + 1)
                    up((n + 1) % 4, (n + 1) % 2)
                    pe.wait_ge(gelu_done, k + 2)
                    pe.wait_ge(result_ready, k + 1)
                    down(n, n % 2)

        @block.scalar
        def _(act):
            act.sem_inc(hT_ready, 2)
            act.sem_inc(gelu_done, 1)
            with act.Fori(0, B // 2) as i:
                for n in range(2):
                    b = i * 2 + n
                    act.wait_ge(turned, b + 2)
                    act.wait_ge(logits_kept, b + 1)
                    nc.scalar.activation(hT[:, n, :], t_bank[:, n, :], ACT.Copy).then_inc(hT_ready, 1)
            act.wait_ge(shifted_ready, 1)
            nc.scalar.activation(ex[:, :, :], L[:, :, :], ACT.Exp).then_inc(exp_ready, 1)

            def turned_rows(n2):
                nc.scalar.activation(rowsT[:, n2, :], t_bank[:, n2, 0:P], ACT.Copy).then_inc(rowsT_ready, 1)

            def gelu(n4, n2):
                for f in range(FC):
                    last = nc.scalar.activation(hidden[:, n2, f, :], up_bank[:, n2, f * P:(f + 1) * P], ACT.Gelu,
                                                bias=own[:, n4, B1_AT + f:B1_AT + f + 1])
                last.then_inc(gelu_done, 1)

            for n in range(2):
                act.wait_ge(rows_turned, n + 1)
                turned_rows(n)
            act.wait_ge(up_done, 1)
            gelu(0, 0)
            with act.Fori(0, SORTED // 4) as i:
                for n in range(4):
                    k = i * 4 + n
                    act.wait_ge(rows_turned, k + 3)
                    act.wait_ge(up_done, k + 1)
                    turned_rows(n % 2)
                    act.wait_ge(up_done, k + 2)
                    act.wait_ge(down_done, k + 2)
                    gelu((n + 1) % 4, (n + 1) % 2)

        @block.vector
        def _(dve):
            v = nc.vector
            dve.sem_inc(logits_kept, 2)
            dve.sem_inc(result_ready, 2)
            dve.sem_inc(added, 2)

            def normalise(b, n, done):
                for t in range(TPS):
                    tile = b * TPS + t
                    last = v.tensor_scalar(hn[:, n, t, :], tile_of(X, tile), stats[:, bass.ds(tile, 1), 0],
                                           stats[:, bass.ds(tile, 1), 1], ALU.subtract, ALU.mult)
                last.then_inc(done, 1)

            dve.wait_ge(loaded, LOADED)
            dve.wait_ge(made, MADE)

            normalise(0, 0, hn_ready)
            with dve.Fori(0, B // 2) as i:
                for n in range(2):
                    b = i * 2 + n
                    dve.wait_ge(turned, b + 1)
                    normalise(b + 1, (n + 1) % 2, hn_ready)
                    dve.wait_ge(logits_done, b + 1)
                    v.tensor_tensor(L[:, bass.ds(b * TPS, TPS), :],
                                    small_bank[:, n, 0:TPS * E].rearrange("p (t e) -> p t e", e=E),
                                    b_router[:, :].unsqueeze(1).to_broadcast([P, TPS, E]), ALU.add)\
                     .then_inc(logits_kept, 1)
            dve.wait_ge(logits_kept, B + 2)

            count = [0]

            def chained(ins):
                count[0] += 1
                ins.then_inc(step, 1)
                dve.wait_ge(step, count[0])

            def over_tiles(x):
                return x.unsqueeze(1).to_broadcast([P, NT, E])

            def over_experts(x):
                return x.unsqueeze(2).to_broadcast([P, NT, E])

            chained(v.reduce_max(top[:, :], L[:, :, :], AX.X))
            v.tensor_tensor(L[:, :, :], L[:, :, :], over_experts(top[:, :]), ALU.subtract).then_inc(shifted_ready, 1)
            dve.wait_ge(shifted_ready, 1)
            dve.wait_ge(exp_ready, 1)
            chained(v.reduce_sum(total[:, :], ex[:, :, :], AX.X))
            chained(v.tensor_scalar(ex[:, :, :], L[:, :, :], 0.0, -float(E), ALU.is_equal, ALU.mult))
            v.reciprocal(gate[:, :], total[:, :])
            chained(v.tensor_tensor(ex[:, :, :], ex[:, :, :], over_tiles(iota_e[:, :]), ALU.add))
            chained(v.tensor_reduce(top[:, :], ex[:, :, :], AX.X, ALU.min))
            v.tensor_tensor(chosen[:, :, :], ex[:, :, :], over_experts(top[:, :]), ALU.is_equal)\
             .then_inc(chosen_ready, 1)
            dve.wait_ge(counts_done, 1)
            chained(v.tensor_copy(tile_counts[:, :], small_bank[0:NT, 0, 0:E]))
            v.tensor_tensor(earlier[:, :, :], earlier[:, :, :],
                            tile_counts[:, :].unsqueeze(1).to_broadcast([NT, NT, E]), ALU.mult)\
             .then_inc(counts_kept, 1)
            dve.wait_ge(places_done, 1)
            chained(v.tensor_scalar(n_int[:, :], small_bank[:, 1, 0:E], float(P - 1), None, ALU.add))
            chained(v.tensor_scalar(n_int[:, :], n_int[:, :], 7, None, ALU.arith_shift_right))
            chained(v.tensor_copy(n_tiles[:, :], n_int[:, :]))
            chained(v.tensor_tensor(ends_by[:, :, :], upto[:, :, :],
                                    n_tiles[:, :].unsqueeze(1).to_broadcast([P, E, E]), ALU.mult))
            chained(v.reduce_sum(ends[:, :], ends_by[:, :, :], AX.X))
            chained(v.tensor_tensor(base[:, :], ends[:, :], n_tiles[:, :], ALU.subtract))
            chained(v.tensor_scalar(base[:, :], base[:, :], float(P), None, ALU.mult))
            v.tensor_tensor(ex[:, :, :], t_bank[:, 0, :].rearrange("p (t e) -> p t e", e=E),
                            over_tiles(base[:, :]), ALU.add).then_inc(places_kept, 1)
            dve.wait_ge(places_kept, 1)
            chained(v.tensor_tensor(ex[:, :, :], ex[:, :, :], chosen[:, :, :], ALU.mult))
            chained(v.reduce_sum(place[:, :], ex[:, :, :], AX.X))
            chained(v.tensor_copy(place_int[:, 0:NT], place[:, :]))
            nk = SORTED + SPARE
            chained(v.tensor_tensor(past[:, :, :], iota_k[0:1, :].unsqueeze(2).to_broadcast([1, nk, E]),
                                    ends[0:1, :].unsqueeze(1).to_broadcast([1, nk, E]), ALU.is_ge))
            chained(v.reduce_sum(expert_of[:, :], past[:, :, :], AX.X))
            chained(v.tensor_scalar(expert_int[:, :], expert_of[:, :], float(E - 1), None, ALU.min))

            dve.wait_ge(turned, B + 1)
            def rows_and_places(b, n):
                v.tensor_copy(index[:, n, :], place_int[:, bass.ds(b * TPS, TPS)]).then_inc(step, 1)
                dve.wait_ge(step, b + 1 + count[0])
                normalise(b, n, scatter_ready)

            for n in range(2):
                rows_and_places(n, n)
            with dve.Fori(0, B // 2 - 1) as i:
                for n in range(2):
                    dve.wait_ge(scattered[n], (i + 1) * (16 * TPS))
                    rows_and_places(i * 2 + (n + 2), n)

            def fetch(k, n4):
                e = dve.value_load(expert_int[0:1, bass.ds(k, 1)], min_val=0, max_val=E - 1)
                v.tensor_copy(own[:, n4, :], tile_of(experts, e))
                v.tensor_copy(own_b2[:, n4, :], tile_of(b2, e)).then_inc(own_ready, 1)

            fetch(0, 0)
            fetch(1, 1)
            with dve.Fori(0, SORTED // 4) as i:
                for n in range(4):
                    k = i * 4 + n
                    dve.wait_ge(down_done, k + 1)
                    fetch(k + 2, (n + 2) % 4)
                    dve.wait_ge(down_done, k + 3)
                    dve.wait_ge(stored[n], 16 * (i + 1))
                    v.tensor_copy(result[:, n, :], down_bank[:, n % 2, 0:C]).then_inc(result_ready, 1)

            def place_of(b, n):
                v.tensor_copy(index[:, n, :], place_int[:, bass.ds(b * TPS, TPS)]).then_inc(index_ready, 1)

            for n in range(2):
                dve.wait_ge(scattered[n], 16 * TPS * (B // 2))
                place_of(n, n)
            with dve.Fori(0, B // 2) as i:
                for n in range(2):
                    b = i * 2 + n
                    dve.wait_ge(gathered[n], (i + 1) * (16 * TPS))
                    for t in range(TPS):
                        tile = b * TPS + t
                        last = v.scalar_tensor_tensor(tile_of(X, tile), back[:, n, t, :],
                                                      gate[:, bass.ds(tile, 1)], tile_of(X, tile),
                                                      ALU.mult, ALU.add)
                    last.then_inc(added, 1)
                    place_of(b + 2, n)

def channel_mix(nc, tag, io, X, stats, identity):
    with Stage(nc, tag) as s:
        w = {n: s.sb(f"w_{n}", [P, C]) for n in "rkv"}
        mu = s.sb("mu", [P, 2])
        hn = s.sb("hn", [P, 2, TPS, C])
        hT = s.sb("hT", [P, 2, 1 + T])
        diff = s.sb("diff", [P, 2, T])
        mix = s.sb("mix", [P, 2, 2, T])
        act_k = s.sb("act_k", [P, 2, T])
        squared = s.sb("squared", [P, 2, T])
        gate = s.sb("gate", [P, 2, T])
        product = s.sb("product", [P, 2, T])
        t_bank, k_bank = s.ps("t_bank", [P, 2, T]), s.ps("k_bank", [P, 2, T])
        r_bank, y_bank = s.ps("r_bank", [P, 2, T]), s.ps("y_bank", [P, 2, T])

        loaded, made = s.sem("weights_loaded"), s.sem("first_column_zero")
        hn_ready, turned, hT_ready = s.sem("hn_ready"), s.sem("turned_1"), s.sem("hT_ready_1")
        diff_ready, mixed = s.sem("diff_ready"), s.sem("mixed_2")
        k_done, relu_done, squares_ready = s.sem("k_done"), s.sem("relu_done_2"), s.sem("squares_ready")
        r_done, gate_ready = s.sem("r_done_2"), s.sem("gate_ready_2")
        y_done, product_ready, added = s.sem("y_done_2"), s.sem("product_ready"), s.sem("added_2")
        LOADED = 16 * 5
        block = s.block()

        @block.sync
        def _(sp):
            for n in "rkv":
                sp.dma_start(w[n][:, :], io[f"w_{n}"]).then_inc(loaded, 16)
            for j, n in enumerate("kr"):
                sp.dma_start(mu[:, j:j + 1], io[f"mu_{n}"].unsqueeze(1)).then_inc(loaded, 16)

        @block.gpsimd
        def _(pool):
            nc.gpsimd.memset(hT[:, :, 0:1], 0.0).then_inc(made, 1)
            pool.wait_ge(made, 1)
            with pool.Fori(0, B // 2) as i:
                for n in range(2):
                    b = i * 2 + n
                    pool.wait_ge(hT_ready, b + 2)
                    pool.wait_ge(mixed, b + 1)
                    nc.gpsimd.tensor_tensor(diff[:, n, :], hT[:, n, 1:1 + T], hT[:, n, 0:T], ALU.subtract)\
                      .then_inc(diff_ready, 1)

        @block.tensor
        def _(pe):
            pe.sem_inc(turned, 1)
            pe.sem_inc(r_done, 2)
            pe.sem_inc(y_done, 2)

            def turn(n):
                for t in range(TPS):
                    last = nc.tensor.transpose(t_bank[:, n, t * P:(t + 1) * P], hn[:, n, t, :], identity[:, :])
                last.then_inc(turned, 1)

            pe.wait_ge(loaded, LOADED)
            pe.wait_ge(hn_ready, 1)
            turn(0)
            with pe.Fori(0, B // 2) as i:
                for n in range(2):
                    b = i * 2 + n
                    pe.wait_ge(mixed, b + 3)
                    pe.wait_ge(relu_done, b + 1)
                    nc.tensor.matmul(k_bank[:, n, :], w["k"][:, :], mix[:, n, 0, :], start=True, stop=True)\
                      .then_inc(k_done, 1)
                    pe.wait_ge(gate_ready, b + 1)
                    for t in range(TPS):
                        last = nc.tensor.matmul(r_bank[:, n, t * P:(t + 1) * P], mix[:, n, 1, t * P:(t + 1) * P],
                                                w["r"][:, :], start=True, stop=True)
                    last.then_inc(r_done, 1)
                    pe.wait_ge(hn_ready, b + 2)
                    pe.wait_ge(hT_ready, b + 1)
                    turn((n + 1) % 2)
                    pe.wait_ge(squares_ready, b + 1)
                    pe.wait_ge(added, b + 1)
                    for t in range(TPS):
                        last = nc.tensor.matmul(y_bank[:, n, t * P:(t + 1) * P], squared[:, n, t * P:(t + 1) * P],
                                                w["v"][:, :], start=True, stop=True)
                    last.then_inc(y_done, 1)

        @block.scalar
        def _(act):
            act.sem_inc(hT_ready, 1)
            act.sem_inc(relu_done, 2)
            act.sem_inc(gate_ready, 2)
            act.wait_ge(turned, 2)
            nc.scalar.activation(hT[:, 0, 1:1 + T], t_bank[:, 0, :], ACT.Copy).then_inc(hT_ready, 1)
            with act.Fori(0, B // 2) as i:
                for n in range(2):
                    b = i * 2 + n
                    act.wait_ge(k_done, b + 1)
                    act.wait_ge(y_done, b + 1)
                    nc.scalar.activation(act_k[:, n, :], k_bank[:, n, :], ACT.Relu).then_inc(relu_done, 1)
                    act.wait_ge(relu_done, b + 3)
                    nc.scalar.activation(squared[:, n, :], act_k[:, n, :], ACT.Square).then_inc(squares_ready, 1)
                    act.wait_ge(r_done, b + 3)
                    act.wait_ge(added, b + 1)
                    nc.scalar.activation(gate[:, n, :], r_bank[:, n, :], ACT.Sigmoid).then_inc(gate_ready, 1)
                    act.wait_ge(turned, b + 3)
                    act.wait_ge(mixed, b + 2)
                    nc.scalar.activation(hT[:, (n + 1) % 2, 1:1 + T], t_bank[:, (n + 1) % 2, :], ACT.Copy)\
                      .then_inc(hT_ready, 1)

        @block.vector
        def _(dve):
            dve.sem_inc(mixed, 2)
            dve.sem_inc(added, 2)

            def normalise(b, n):
                for t in range(TPS):
                    tile = b * TPS + t
                    last = nc.vector.tensor_scalar(hn[:, n, t, :], tile_of(X, tile), stats[:, bass.ds(tile, 1), 0],
                                                   stats[:, bass.ds(tile, 1), 1], ALU.subtract, ALU.mult)
                last.then_inc(hn_ready, 1)

            normalise(0, 0)
            dve.wait_ge(loaded, LOADED)
            with dve.Fori(0, B // 2) as i:
                for n in range(2):
                    b = i * 2 + n
                    dve.wait_ge(diff_ready, b + 1)
                    dve.wait_ge(r_done, b + 1)
                    for j in range(2):
                        last = nc.vector.scalar_tensor_tensor(mix[:, n, j, :], diff[:, n, :], mu[:, j:j + 1],
                                                              hT[:, n, 0:T], ALU.mult, ALU.add)
                    last.then_inc(mixed, 1)
                    dve.wait_ge(turned, b + 1)
                    normalise(b + 1, (n + 1) % 2)
                    dve.wait_ge(y_done, b + 3)
                    dve.wait_ge(gate_ready, b + 3)
                    nc.vector.tensor_tensor(product[:, n, :], gate[:, n, :], y_bank[:, n, :], ALU.mult)\
                      .then_inc(product_ready, 1)
                    dve.wait_ge(product_ready, b + 1)
                    x = X[:, bass.ds(b * TPS, TPS), :].rearrange("p t c -> p (t c)")
                    nc.vector.tensor_tensor(x, x, product[:, n, :], ALU.add).then_inc(added, 1)


QH, KVH, HD, WINDOW = 16, 4, 64, 64
REP = QH // KVH
NORMED = QH + KVH
RMS_EPS = 1e-6
G_UNITS = TPS * KVH
G_LEAD = KVH + 1
BAND = P + WINDOW


def window_attention(nc, tag, io, X, stats, identity):
    with Stage(nc, tag) as s:
        wq, wkv, wo = s.sb("wq", [P, QH * HD]), s.sb("wkv", [P, 2 * KVH * HD]), s.sb("wo", [P, 8, C])
        norm_w = s.sb("norm_w", [P, 2])
        ident16 = s.sb("ident16", [P, P], BF16)
        mask_qk = s.sb("mask_qk", [P, BAND], BF16)
        mask_kq = s.sb("mask_kq", [P, P], BF16)
        mask_prev = s.sb("mask_prev", [P, WINDOW], BF16)
        select = s.sb("select", [QH, QH, P], BF16)
        hn, hT = s.sb("hn", [P, TPS, C]), s.sb("hT", [P, T])
        raw = s.sb("raw", [P, 2, NORMED, HD])
        squares = s.sb("squares", [P, NORMED, HD])
        ssq, rms = s.sb("ssq", [P, NORMED]), s.sb("rms", [P, NORMED])
        minus_half = s.sb("minus_half", [P, NORMED])
        scaled = s.sb("scaled", [P, 2, NORMED, HD])
        QT, KT = s.sb("QT", [P, 2, 2, TPS, REP, P]), s.sb("KT", [P, 2, 2, T])
        QT16, KT16 = s.sb("QT16", [P, 2, 2, TPS, REP, P], BF16), s.sb("KT16", [P, 2, 2, T], BF16)
        V = s.sb("V", [P, 2, TPS, KVH, HD + 1])
        M, MT = s.sb("M", [P, 2, QH]), s.sb("MT", [QH, 2, P], BF16)
        probs, probs_prev = s.sb("probs", [P, 2, REP, P]), s.sb("probs_prev", [P, 2, REP, WINDOW])
        rec = s.sb("rec", [P, REP])
        on, yT = s.sb("on", [P, QH * HD]), s.sb("yT", [P, 8, P])

        max_bank = s.ps("max_bank", [P, 2, T])
        exp_bank, prev_bank = s.ps("exp_bank", [P, 2, T]), s.ps("prev_bank", [P, T])
        out_bank, banks = s.ps("out_bank", [P, T]), s.ps("banks", [P, 2, T])

        loaded, made, made_step = s.sem("weights_loaded"), s.sem("constants_made"), s.sem("made_step")
        hn_ready = s.sem("hn_ready")
        misc_full, misc_free = s.sem("misc_full"), s.sem("misc_free")
        squares_ready, ssq_ready, rms_step = s.sem("squares_ready"), s.sem("ssq_ready"), s.sem("rms_step")
        rms_ready, scaled_ready = s.sem("rms_ready"), s.sem("scaled_ready")
        cast_ready = s.sem("cast_ready")
        max_scores, max_done = s.sem("max_scores"), s.sem("max_done")
        scores, exp_done, pv_done = s.sem("scores"), s.sem("exp_done"), s.sem("pv_done")
        rec_ready, norm_ready, added = s.sem("rec_ready"), s.sem("norm_ready"), s.sem("added")
        waited = s.sem("waited")

        uses = [((0, 0), ("HT",))]
        for t in range(TPS):
            raw_at = [(0, 1), (0, 2), (1, 0)] if t == 0 else [(3 * t, x) for x in range(3)]
            uses += list(zip(raw_at, (("QA", t), ("QB", t), ("KV", t))))
            uses += [((3 * t + 5, x), (what, t)) for x, what in enumerate(("TQA", "TQB", "TK"))]
            uses += [((4 * t + 3, 0), ("MAX", t + 1))]
        for t in range(TPS):
            after = [(4 * t + 5, 0), (4 * t + 5, 1), (4 * t + 6, 1)] if t < 3 else [(G_UNITS, 0)] * 3
            uses += list(zip(after, (("YT0", t), ("YT1", t), ("OUT", t))))
        uses.sort(key=lambda e: e[0])
        NM, NA = len(uses), len(uses) - TPS
        early = ("HT", "QA", "QB", "KV", "TQA", "TQB", "TK")
        first = [e for e in uses if e[1][0] in early or e[1] == ("MAX", 4)]
        NF = len(first)

        def at(b, n, c):
            return (b + 1) * n + c

        def steps(prologue):
            chosen = first if prologue else uses
            found, a = [], NA - NF if prologue else 0
            for j, (place, what) in enumerate(chosen):
                found.append((place, what, NM - len(chosen) + j, a))
                a += what[0] != "OUT"
            return found

        def released(prologue, what):
            return {w: a + 1 for _, w, _, a in steps(prologue)}[what]

        def filled(prologue, what):
            return {w: j + 1 for _, w, j, _ in steps(prologue)}[what]

        def in_body(u, prologue):
            return u < G_UNITS and (not prologue or u + G_LEAD >= G_UNITS)

        def pairs_of(body, eng):
            body(eng, -1, 1, True)
            with eng.Fori(0, B // 2) as i:
                body(eng, i * 2, 0, False)
                body(eng, i * 2 + 1, 1, False)

        LOADED, MADE = 16 * 7, 8
        block = s.block()

        @block.sync
        def _(sp):
            sp.dma_start(wq[:, :], io["w_q"]).then_inc(loaded, 16)
            sp.dma_start(wkv[:, :], io["w_kv"]).then_inc(loaded, 16)
            sp.dma_start(wo[:, :, :], io["w_out"].rearrange("(q p) c -> p q c", p=P)).then_inc(loaded, 16)
            for j, n in enumerate(("q_norm", "k_norm")):
                for x in range(2):
                    sp.dma_start(norm_w[HD * x:HD * (x + 1), j:j + 1], io[n].unsqueeze(1)).then_inc(loaded, 16)

        @block.gpsimd
        def _(pool):
            g = nc.gpsimd
            for m in (mask_qk, mask_kq, mask_prev):
                g.memset(m[:, :], 0.0).then_inc(made_step, 1)
            g.memset(select[:, :, :], 0.0).then_inc(made_step, 1)
            g.memset(V[:, :, :, :, :], 1.0).then_inc(made, 1)
            g.tensor_copy(ident16[:, :], identity[:, :]).then_inc(made, 1)
            g.memset(minus_half[:, :], -0.5).then_inc(made, 1)
            pool.wait_ge(made_step, 4)
            g.affine_select(out=mask_qk[:, :], in_=mask_qk[:, :], compare_op=ALU.is_gt, fill=MASKED, base=0,
                            pattern=[[1, BAND]], channel_multiplier=-1).then_inc(made_step, 1)
            g.affine_select(out=mask_kq[:, :], in_=mask_kq[:, :], compare_op=ALU.is_ge, fill=MASKED, base=0,
                            pattern=[[1, P]], channel_multiplier=-1).then_inc(made_step, 1)
            g.affine_select(out=select[:, :, :], in_=select[:, :, :], compare_op=ALU.not_equal, fill=1.0, base=0,
                            pattern=[[1, QH], [0, P]], channel_multiplier=-1).then_inc(made, 1)
            g.affine_select(out=mask_prev[:, :], in_=mask_prev[:, :], compare_op=ALU.is_gt, fill=MASKED,
                            base=-WINDOW, pattern=[[-1, WINDOW]], channel_multiplier=1).then_inc(made, 1)
            pool.wait_ge(made_step, 6)
            g.affine_select(out=mask_qk[:, :], in_=mask_qk[:, :], compare_op=ALU.is_ge, fill=MASKED, base=WINDOW,
                            pattern=[[-1, BAND]], channel_multiplier=1).then_inc(made, 1)
            g.affine_select(out=mask_kq[:, :], in_=mask_kq[:, :], compare_op=ALU.is_gt, fill=MASKED, base=WINDOW,
                            pattern=[[-1, P]], channel_multiplier=1).then_inc(made, 1)
            pool.wait_ge(loaded, LOADED)
            g.tensor_tensor(norm_w[:, 0:1], norm_w[:, 0:1], norm_w[:, 1:2], ALU.mult).then_inc(made, 1)
            pool.wait_ge(made, MADE)

            def body(pool, b, par, prologue):
                to = (par + 1) % 2
                def scale_factors(t):
                    n = at(b, TPS, t)
                    pool.wait_ge(ssq_ready, n + 1)
                    pool.sem_inc(waited, 1)
                    g.tensor_scalar(rms[:, :], ssq[:, :], 1.0 / HD, RMS_EPS, ALU.mult, ALU.add).then_inc(rms_step, 1)
                    pool.wait_ge(rms_step, n + 1)
                    pool.sem_inc(waited, 1)
                    g.tensor_tensor(rms[:, :], rms[:, :], minus_half[:, :], ALU.pow).then_inc(rms_ready, 1)

                def narrow(t):
                    pool.wait_ge(misc_free, at(b, NA, released(prologue, ("TK", t))))
                    pool.sem_inc(waited, 1)
                    for i in range(2):
                        g.tensor_copy(QT16[:, to, i, t, :, :], QT[:, to, i, t, :, :])
                    g.tensor_copy(KT16[:, to, :, t * P:(t + 1) * P], KT[:, to, :, t * P:(t + 1) * P])\
                     .then_inc(cast_ready, 1)

                for t in range(TPS):
                    scale_factors(t)
                    if t:
                        narrow(t - 1)
                narrow(TPS - 1)

            pairs_of(body, pool)

        @block.tensor
        def _(pe):
            pe.sem_inc(misc_full, NM - NF)
            pe.sem_inc(max_scores, 2 * (G_UNITS - G_LEAD))
            pe.sem_inc(scores, G_UNITS)
            pe.sem_inc(pv_done, G_UNITS)
            pe.wait_ge(loaded, LOADED)
            pe.wait_ge(made, MADE)

            def pv(b, par, u):
                t, g = u // KVH, u % KVH
                pe.wait_ge(exp_done, at(b, G_UNITS, u + 1))
                pe.wait_ge(norm_ready, at(b, G_UNITS, u))
                for a in range(REP):
                    o = out_bank[:, a * (HD + 1):(a + 1) * (HD + 1)]
                    last = nc.tensor.matmul(o, probs[:, u % 2, a, :], V[:, par, t, g, :], start=True, stop=True)
                    if t:
                        last = nc.tensor.matmul(o[0:WINDOW], probs_prev[P - WINDOW:, u % 2, a, :],
                                                V[P - WINDOW:, par, t - 1, g, :], start=False, stop=True,
                                                skip_group_check=True)
                last.then_inc(pv_done, 1)

            def body(pe, b, par, prologue):
                to = (par + 1) % 2

                def misc_use(u, what, j):
                    known = {j_: (w_, a_) for _, w_, j_, a_ in steps(prologue)}
                    if j - 2 in known:
                        before, a = known[j - 2]
                        if before[0] == "OUT":
                            pe.wait_ge(added, at(b, TPS, before[1] + 1))
                        else:
                            pe.wait_ge(misc_free, at(b, NA, a + 1))
                    elif not prologue:
                        pe.wait_ge(misc_free, at(b, NA, 0))
                        if j == 0:
                            pe.wait_ge(added, at(b, TPS, 0))
                    kind, t = what[0], what[-1]
                    misc = banks[:, j % 2, :]
                    if kind == "HT":
                        pe.wait_ge(hn_ready, b + 2)
                        for t in range(TPS):
                            last = nc.tensor.transpose(misc[:, t * P:(t + 1) * P], hn[:, t, :], identity[:, :])
                    elif kind in ("QA", "QB", "KV"):
                        if (kind, t) == ("QA", 0):
                            pe.wait_ge(misc_free, at(b, NA, released(prologue, ("HT",))))
                        w = {"QA": wq[:, 0:T], "QB": wq[:, T:], "KV": wkv[:, :]}[kind]
                        last = nc.tensor.matmul(misc[:, :], hT[:, t * P:(t + 1) * P], w, start=True, stop=True)
                    elif kind in ("TQA", "TQB", "TK"):
                        if kind == "TQA":
                            pe.wait_ge(scaled_ready, at(b, TPS, t + 1))
                        h0 = {"TQA": 0, "TQB": 8, "TK": 16}[kind]
                        for x in range(2 if kind == "TK" else 4):
                            last = nc.tensor.transpose(misc[:, x * P:(x + 1) * P],
                                                       scaled[:, t % 2, h0 + 2 * x:h0 + 2 * x + 2, :]
                                                       .rearrange("p h d -> p (h d)"), identity[:, :])
                    elif kind == "MAX":
                        pe.wait_ge(max_done, at(b, 2 * G_UNITS, 2 * u))
                        last = nc.tensor.transpose(misc[0:QH, 0:P], M[:, t % 2, :], identity[:, :])
                    elif kind in ("YT0", "YT1"):
                        pe.wait_ge(norm_ready, at(b, G_UNITS, KVH * (t + 1)))
                        for x in range(4):
                            q = x + (4 if kind == "YT1" else 0)
                            last = nc.tensor.transpose(misc[:, x * P:(x + 1) * P], on[:, q * P:(q + 1) * P],
                                                       identity[:, :])
                    else:
                        pe.wait_ge(misc_free, at(b, NA, released(False, ("YT1", t))))
                        for q in range(8):
                            last = nc.tensor.matmul(misc[:, 0:C], yT[:, q, :], wo[:, q, :],
                                                    start=(q == 0), stop=(q == 7))
                    last.then_inc(misc_full, 1)

                def misc_uses(u, place):
                    for _, what, j, _ in [e for e in steps(prologue) if e[0] == (u, place)]:
                        misc_use(u, what, j)

                for u in range(G_UNITS + 1):
                    if u == G_UNITS and not prologue:
                        pv(b, par, G_UNITS - 1)
                    misc_uses(u, 0)
                    if in_body(u, prologue):
                        n = u + G_LEAD
                        pb = to if n >= G_UNITS else par
                        t, g = (n % G_UNITS) // KVH, n % KVH
                        if g == 0:
                            pe.wait_ge(cast_ready, at(b, TPS, t + 1) if n >= G_UNITS else at(b, TPS, 0))
                        rows, i = slice(64 * (g % 2), 64 * (g % 2) + 64), g // 2
                        W, c0 = (BAND, t * P - WINDOW) if t else (P, 0)
                        for half in range(2):
                            if not (prologue and n == G_UNITS):
                                pe.wait_ge(max_done, at(b, 2 * G_UNITS, 2 * u + half - 1))
                            for x in range(2):
                                nc.tensor.matmul(max_bank[:, half, x * W:(x + 1) * W],
                                                 QT16[rows, pb, i, t, 2 * half + x, :],
                                                 KT16[rows, pb, i, c0:c0 + W], start=True, stop=True)
                            nc.tensor.matmul(max_bank[:, half, 0:2 * W].rearrange("p (x k) -> p x k", x=2),
                                             ident16[:, :],
                                             mask_qk[:, BAND - W:].unsqueeze(1).to_broadcast([P, 2, W]),
                                             start=False, stop=True, skip_group_check=True)\
                              .then_inc(max_scores, 1)
                    misc_uses(u, 1)
                    if u < G_UNITS and not prologue:
                        t, g = u // KVH, u % KVH
                        rows, i = slice(64 * (g % 2), 64 * (g % 2) + 64), g // 2
                        if g == 0:
                            if t:
                                pe.wait_ge(misc_free, at(b, NA, released(False, ("MAX", t))))
                        pe.wait_ge(exp_done, at(b, G_UNITS, u - 1))
                        o = exp_bank[:, u % 2, :]
                        nc.tensor.matmul(o, KT[rows, par, i, t * P:(t + 1) * P],
                                         QT[rows, par, i, t, :, :].rearrange("p a q -> p (a q)"),
                                         start=True, stop=True)
                        nc.tensor.matmul(o.rearrange("p (a q) -> p a q", a=REP), ident16[:, :],
                                         mask_kq[:, :].unsqueeze(1).to_broadcast([P, REP, P]),
                                         start=False, stop=True, skip_group_check=True)
                        for a in range(REP):
                            oa = exp_bank[:, u % 2, a * P:(a + 1) * P]
                            last = nc.tensor.matmul(oa, select[:, REP * g + a, :], MT[:, t % 2, :],
                                                    start=False, stop=True, skip_group_check=True)
                        if t:
                            top = slice(P - WINDOW, P)
                            nc.tensor.matmul(prev_bank[rows, 0:REP * WINDOW],
                                             KT[rows, par, i, t * P - WINDOW:t * P],
                                             QT[rows, par, i, t, :, 0:WINDOW], start=True, stop=True)
                            nc.tensor.matmul(prev_bank[rows, 0:REP * WINDOW]
                                             .rearrange("p (a q) -> p a q", a=REP), ident16[:, top],
                                             mask_prev[:, :].unsqueeze(1).to_broadcast([P, REP, WINDOW]),
                                             start=False, stop=True, skip_group_check=True)
                            for a in range(REP):
                                oa = prev_bank[rows, a * WINDOW:(a + 1) * WINDOW]
                                last = nc.tensor.matmul(oa, select[:, REP * g + a, 0:WINDOW], MT[:, t % 2, 0:WINDOW],
                                                        start=False, stop=True, skip_group_check=True)
                        last.then_inc(scores, 1)
                        if u >= 1:
                            pv(b, par, u - 1)
                    misc_uses(u, 2)

            pairs_of(body, pe)

        @block.scalar
        def _(act):
            act.sem_inc(misc_free, NA - NF)
            act.sem_inc(exp_done, G_UNITS)
            act.wait_ge(made, MADE)

            def body(act, b, par, prologue):
                to = (par + 1) % 2

                def misc_uses(u, places):
                    for _, what, j, _ in [e for e in steps(prologue)
                                          if e[0][0] == u and e[0][1] in places and e[1][0] != "OUT"]:
                        kind, t = what[0], what[-1]
                        misc = banks[:, j % 2, :]
                        act.wait_ge(misc_full, at(b, NM, j + 1))
                        if kind == "HT":
                            last = nc.scalar.activation(hT[:, :], misc[:, :], ACT.Copy)
                        elif kind in ("QA", "QB", "KV"):
                            if kind == "QA" and not (prologue and t == 0):
                                act.wait_ge(ssq_ready, at(b, TPS, t))
                            if kind == "QA" and not (prologue and t < 2):
                                act.wait_ge(scaled_ready, at(b, TPS, t - 1))
                            h0, nh = {"QA": (0, 8), "QB": (8, 8), "KV": (16, 4)}[kind]
                            flat = lambda x: x[:, h0:h0 + nh, :].rearrange("p h d -> p (h d)")
                            nc.scalar.activation(flat(raw[:, t % 2]), misc[:, 0:nh * HD], ACT.Copy)
                            last = nc.scalar.activation(flat(squares), misc[:, 0:nh * HD], ACT.Square)
                            if kind == "KV":
                                last.then_inc(squares_ready, 1)
                                last = nc.scalar.activation(V[:, to, t, :, 0:HD],
                                                            misc[:, KVH * HD:].rearrange("p (h d) -> p h d", d=HD),
                                                            ACT.Copy)
                        elif kind in ("TQA", "TQB"):
                            last = nc.scalar.activation(QT[:, to, 0 if kind == "TQA" else 1, t, :, :]
                                                        .rearrange("p a q -> p (a q)"), misc[:, :], ACT.Copy)
                        elif kind == "TK":
                            last = nc.scalar.activation(KT[:, to, :, t * P:(t + 1) * P],
                                                        misc[:, 0:2 * P].rearrange("p (i k) -> p i k", i=2),
                                                        ACT.Identity, scale=norm_w[:, 0:1])
                        elif kind == "MAX":
                            last = nc.scalar.activation(MT[:, t % 2, :], misc[0:QH, 0:P], ACT.Copy, scale=-1.0)
                        else:
                            q0 = 0 if kind == "YT0" else 4
                            if kind == "YT0":
                                act.wait_ge(misc_full, at(b, NM, filled(False, ("OUT", t - 1)) if t else 0))
                            last = nc.scalar.activation(yT[:, q0:q0 + 4, :].rearrange("p q n -> p (q n)"),
                                                        misc[:, :], ACT.Copy)
                        last.then_inc(misc_free, 1)

                for u in range(G_UNITS + 1):
                    misc_uses(u, (0, 1))
                    if u < G_UNITS and not prologue:
                        t = u // KVH
                        act.wait_ge(scores, at(b, G_UNITS, u + 1))
                        act.wait_ge(pv_done, at(b, G_UNITS, u - 1))
                        last = nc.scalar.activation(probs[:, u % 2, :, :].rearrange("p a q -> p (a q)"),
                                                    exp_bank[:, u % 2, :], ACT.Exp, scale=HD ** -0.5)
                        if t:
                            top = slice(P - WINDOW, P)
                            half = slice(64 * (u % 2), 64 * (u % 2) + 64)
                            last = nc.scalar.activation(probs_prev[top, u % 2, :, :].rearrange("p a q -> p (a q)"),
                                                        prev_bank[half, 0:REP * WINDOW], ACT.Exp,
                                                        scale=HD ** -0.5)
                        last.then_inc(exp_done, 1)
                    misc_uses(u, (2,))

            pairs_of(body, act)

        @block.vector
        def _(dve):
            v = nc.vector
            dve.sem_inc(max_done, 2 * (G_UNITS - G_LEAD))
            dve.sem_inc(norm_ready, G_UNITS)
            dve.sem_inc(added, TPS)

            def normalise(b, u):
                g = u % KVH
                dve.wait_ge(pv_done, at(b, G_UNITS, u + 1))
                o = out_bank[:, 0:REP * (HD + 1)].rearrange("p (a d) -> p a d", a=REP)
                v.reciprocal(rec[:, :], o[:, :, HD]).then_inc(rec_ready, 1)
                dve.wait_ge(rec_ready, b * G_UNITS + u + 1)
                if g == 0 and u:
                    dve.wait_ge(misc_full, at(b, NM, filled(False, ("YT1", u // KVH - 1))))
                n = REP * HD
                v.tensor_tensor(on[:, g * n:(g + 1) * n].rearrange("p (a d) -> p a d", a=REP), o[:, :, 0:HD],
                                rec[:, :].unsqueeze(2).to_broadcast([P, REP, HD]), ALU.mult).then_inc(norm_ready, 1)

            def body(dve, b, par, prologue):
                if not prologue:
                    dve.wait_ge(misc_full, at(b, NM, 0))
                for t in range(TPS):
                    tile = (b + 1) * TPS + t
                    last = v.tensor_scalar(hn[:, t, :], tile_of(X, tile), stats[:, bass.ds(tile, 1), 0],
                                           stats[:, bass.ds(tile, 1), 1], ALU.subtract, ALU.mult)
                last.then_inc(hn_ready, 1)
                for u in range(G_UNITS + 1):
                    if u == G_UNITS and not prologue:
                        normalise(b, G_UNITS - 1)
                    if in_body(u, prologue):
                        n = (u + G_LEAD) % G_UNITS
                        t, g = n // KVH, n % KVH
                        W = BAND if t else P
                        for half in range(2):
                            dve.wait_ge(max_scores, at(b, 2 * G_UNITS, 2 * u + half + 1))
                            h = REP * g + 2 * half
                            v.reduce_max(M[:, t % 2, h:h + 2],
                                         max_bank[:, half, 0:2 * W].rearrange("p (x w) -> p x w", x=2), AX.X)\
                             .then_inc(max_done, 1)
                    for _, what, j, _ in [e for e in steps(prologue) if e[0][0] == u and e[1][0] == "OUT"]:
                        tile = b * TPS + what[1]
                        dve.wait_ge(misc_full, at(b, NM, j + 1))
                        v.tensor_tensor(tile_of(X, tile), tile_of(X, tile), banks[:, j % 2, 0:C], ALU.add)\
                         .then_inc(added, 1)
                    if u < G_UNITS and not prologue and u >= 1:
                        normalise(b, u - 1)
                    if u % 3 == 1 and u // 3 < TPS:
                        dve.wait_ge(squares_ready, at(b, TPS, u // 3 + 1))
                        v.reduce_sum(ssq[:, :], squares[:, :, :], AX.X).then_inc(ssq_ready, 1)
                    if u % 3 == 0 and u and u // 3 <= TPS:
                        t = u // 3 - 1
                        dve.wait_ge(rms_ready, at(b, TPS, t + 1))
                        if t >= 2:
                            dve.wait_ge(misc_full, at(b, NM, filled(prologue, ("TK", t - 2))))
                        v.tensor_tensor(scaled[:, t % 2, :, :], raw[:, t % 2, :, :],
                                        rms[:, :].unsqueeze(2).to_broadcast([P, NORMED, HD]), ALU.mult)\
                         .then_inc(scaled_ready, 1)

            pairs_of(body, dve)


DH, DK = 4, 32
TAPS = 4
QKV = 3 * C
L2_EPS = 1e-6
REACH = 2 * P
FILTER_PAD = 3 * P
CH_GROUP = 8


def delta_inputs(nc, tag, io, X, stats, identity, v_all, beta, qk_dram):
    with Stage(nc, tag) as s:
        w = s.sb("w", [P, QKV])
        taps = s.sb("taps", [P, TAPS, QKV])
        w_beta = s.sb("w_beta", [P, DH])
        minus_half = s.sb("minus_half", [P, TPS * 2 * DH])
        hn = s.sb("hn", [P, 2, TPS, C])
        hT = s.sb("hT", [P, 2, TAPS - 1 + T])
        qk = s.sb("qk", [P, 2, TPS, 2 * C])
        squares = s.sb("squares", [P, TPS, 2 * C])
        ssq, scale = s.sb("ssq", [P, TPS * 2 * DH]), s.sb("scale", [P, TPS * 2 * DH])
        unit = s.sb("unit", [P, 2, TPS, 2 * C])
        t_bank = s.ps("t_bank", [P, 2, T])
        p_bank = s.ps("p_bank", [P, TPS, T])

        loaded, made = s.sem("weights_loaded"), s.sem("constants_made")
        hn_ready, turned, hT_ready = s.sem("hn_ready"), s.sem("turned_1"), s.sem("hT_ready_1")
        projected, silu_done, beta_kept = s.sem("projected_1"), s.sem("silu_done_1"), s.sem("beta_kept_1")
        squares_ready, ssq_ready = s.sem("squares_ready"), s.sem("ssq_ready")
        scale_step, scale_ready, unit_ready = s.sem("scale_step"), s.sem("scale_ready"), s.sem("unit_ready_2")
        stored = [s.sem(f"stored{n}_1") for n in range(2)]
        beta_all, waited = s.sem("beta_all"), s.sem("waited")
        LOADED, MADE = 16 * 3, 4
        block = s.block()

        @block.sync
        def _(sp):
            sp.dma_start(w[:, :], io["w_qkv"]).then_inc(loaded, 16)
            sp.dma_start(taps[:, :, :], io["conv"].partition_broadcast(P)).then_inc(loaded, 16)
            sp.dma_start(w_beta[:, :], io["w_beta"]).then_inc(loaded, 16)
            for n in range(2):
                sp.sem_inc(stored[n], 16)
            with sp.Fori(0, B // 2) as i:
                for n in range(2):
                    sp.wait_ge(unit_ready, i * 2 + (n + 3))
                    sp.dma_start(qk_dram[bass.ds(i * 2 + n, 1)].rearrange("o p t c -> p (o t) c"), unit[:, n, :, :])\
                      .then_inc(stored[n], 16)
            for n in range(2):
                sp.wait_ge(stored[n], 16 * (B // 2 + 1))

        @block.gpsimd
        def _(pool):
            g = nc.gpsimd
            g.memset(hT[:, :, 0:TAPS - 1], 0.0).then_inc(made, 1)
            g.memset(minus_half[:, :], -0.5).then_inc(made, 1)
            g.memset(v_all[:, :, :], 0.0).then_inc(made, 1)
            pool.wait_ge(made, MADE)
            with pool.Fori(0, B // 2) as i:
                for n in range(2):
                    b = i * 2 + n
                    pool.wait_ge(silu_done, b + 2)
                    g.tensor_tensor(squares[:, :, :], qk[:, n, :, :], qk[:, n, :, :], ALU.mult)\
                     .then_inc(squares_ready, 1)
                    pool.wait_ge(ssq_ready, b + 1)
                    pool.sem_inc(waited, 1)
                    g.tensor_scalar(scale[:, :], ssq[:, :], L2_EPS, None, ALU.add).then_inc(scale_step, 1)
                    pool.wait_ge(scale_step, b + 1)
                    g.tensor_tensor(scale[:, :], scale[:, :], minus_half[:, :], ALU.pow).then_inc(scale_ready, 1)

        @block.tensor
        def _(pe):
            pe.sem_inc(turned, 1)
            pe.sem_inc(projected, 1)

            def turn(n):
                for t in range(TPS):
                    last = nc.tensor.transpose(t_bank[:, n, t * P:(t + 1) * P], hn[:, n, t, :], identity[:, :])
                last.then_inc(turned, 1)

            pe.wait_ge(made, MADE)
            pe.wait_ge(hn_ready, 1)
            turn(0)
            with pe.Fori(0, B // 2) as i:
                for n in range(2):
                    b = i * 2 + n
                    pe.wait_ge(hn_ready, b + 2)
                    pe.wait_ge(hT_ready, b + 1)
                    turn((n + 1) % 2)
                    pe.wait_ge(hT_ready, b + 2)
                    pe.wait_ge(silu_done, b + 1)
                    pe.wait_ge(beta_kept, b + 1)
                    for t in range(TPS):
                        for j in range(TAPS):
                            nc.tensor.matmul(p_bank[:, t, 0:QKV], hT[:, n, t * P + j:t * P + j + P], taps[:, j, :],
                                             start=(j == 0), stop=(j == TAPS - 1))
                        now = hT[:, n, TAPS - 1 + t * P:TAPS - 1 + (t + 1) * P]
                        last = nc.tensor.matmul(p_bank[:, t, QKV:QKV + DH], now, w_beta[:, :], start=True, stop=True)
                    last.then_inc(projected, 1)

        @block.scalar
        def _(act):
            act.sem_inc(hT_ready, 1)
            act.sem_inc(silu_done, 1)
            act.wait_ge(made, MADE)
            act.wait_ge(turned, 2)
            nc.scalar.activation(hT[:, 0, TAPS - 1:], t_bank[:, 0, :], ACT.Copy).then_inc(hT_ready, 1)
            with act.Fori(0, B // 2) as i:
                for n in range(2):
                    b = i * 2 + n
                    act.wait_ge(turned, b + 3)
                    act.wait_ge(projected, b + 1)
                    nc.scalar.activation(hT[:, (n + 1) % 2, TAPS - 1:], t_bank[:, (n + 1) % 2, :], ACT.Copy)\
                      .then_inc(hT_ready, 1)
                    act.wait_ge(projected, b + 2)
                    act.wait_ge(unit_ready, b + 1)
                    nc.scalar.activation(qk[:, n, :, :], p_bank[:, :, 0:2 * C], ACT.Silu)
                    nc.scalar.activation(v_all[:, bass.ds(b * (TPS + 1) + 1, TPS), :], p_bank[:, :, 2 * C:QKV],
                                         ACT.Silu).then_inc(silu_done, 1)
            act.wait_ge(beta_kept, B + 1)
            nc.scalar.activation(beta[:, 0:NT, :], beta[:, 0:NT, :], ACT.Sigmoid).then_inc(beta_all, 1)

        @block.vector
        def _(dve):
            v = nc.vector
            dve.sem_inc(beta_kept, 1)
            dve.sem_inc(unit_ready, 2)
            dve.wait_ge(loaded, LOADED)
            v.tensor_tensor(taps[:, :, :], taps[:, :, :], w[:, :].unsqueeze(1).to_broadcast([P, TAPS, QKV]),
                            ALU.mult).then_inc(made, 1)

            def normalise(b, n):
                for t in range(TPS):
                    tile = b * TPS + t
                    last = v.tensor_scalar(hn[:, n, t, :], tile_of(X, tile), stats[:, bass.ds(tile, 1), 0],
                                           stats[:, bass.ds(tile, 1), 1], ALU.subtract, ALU.mult)
                last.then_inc(hn_ready, 1)

            normalise(0, 0)
            with dve.Fori(0, B // 2) as i:
                for n in range(2):
                    b = i * 2 + n
                    dve.wait_ge(turned, b + 1)
                    normalise(b + 1, (n + 1) % 2)
                    dve.wait_ge(projected, b + 2)
                    dve.wait_ge(silu_done, b + 2)
                    v.tensor_copy(beta[:, bass.ds(b * TPS, TPS), :], p_bank[:, :, QKV:QKV + DH]).then_inc(beta_kept, 1)
                    dve.wait_ge(squares_ready, b + 1)
                    v.reduce_sum(ssq[:, :], squares[:, :, :].rearrange("p t (h d) -> p (t h) d", d=DK), AX.X)\
                     .then_inc(ssq_ready, 1)
                    dve.wait_ge(scale_ready, b + 1)
                    dve.wait_ge(stored[n], (i + 1) * 16)
                    v.tensor_tensor(unit[:, n, :, :].rearrange("p t (h d) -> p (t h) d", d=DK),
                                    qk[:, n, :, :].rearrange("p t (h d) -> p (t h) d", d=DK),
                                    scale[:, :].unsqueeze(2).to_broadcast([P, TPS * 2 * DH, DK]), ALU.mult)\
                     .then_inc(unit_ready, 1)


def long_filters(nc, tag, io, v_all, filtered):
    groups = C // CH_GROUP
    HALF = B * (TPS + 1) // 2
    with Stage(nc, tag) as s:
        band = s.sb("band", [P, 4, CH_GROUP, REACH])
        flip = s.sb("flip", [P, P])
        flipped = s.sb("flipped", [P, 2, 2, HALF, CH_GROUP])
        bank = s.ps("bank", [P, 4, T])
        flip_bank = s.ps("flip_bank", [P, 2, 2, T])

        loaded = [s.sem(f"loaded{n}") for n in range(4)]
        made, step, products = s.sem("flip_made"), s.sem("flip_step"), s.sem("products")
        flip_done, flip_kept = s.sem("flip_done"), s.sem("flip_kept_1")
        kept = [s.sem("kept_short_2"), s.sem("kept_long_2")]
        block = s.block()

        @block.sync
        def _(sp):
            def load(g, n):
                for j, name in enumerate(("short", "long")):
                    rows = io[name]
                    src = bass.AP(tensor=rows.tensor, offset=g * (CH_GROUP * FILTER_PAD),
                                  ap=[[1, P], [FILTER_PAD, CH_GROUP], [1, REACH]])
                    sp.dma_start(band[:, 2 * n + j, :, :], src).then_inc(loaded[2 * n + j], 16)
            for n in range(2):
                load(n, n)
            with sp.Fori(0, groups // 2 - 1) as i:
                for n in range(2):
                    sp.wait_ge(products, (i * 2 + (n + 1)) * 2)
                    load(i * 2 + (n + 2), n)

        @block.gpsimd
        def _(pool):
            nc.gpsimd.memset(flip[:, :], 0.0).then_inc(step, 1)
            pool.wait_ge(step, 1)
            nc.gpsimd.affine_select(out=flip[:, :], in_=flip[:, :], compare_op=ALU.not_equal, fill=1.0,
                                    base=1 - P, pattern=[[1, P]], channel_multiplier=1).then_inc(made, 1)

        def groups_of(body, eng):
            with eng.Fori(0, groups // 2 - 1) as i:
                for n in range(2):
                    body(i, i * 2 + n, n, True)
            body(groups // 2 - 1, groups - 2, 0, True)
            body(groups // 2 - 1, groups - 1, 1, False)

        @block.tensor
        def _(pe):
            pe.wait_ge(made, 1)

            def turn(g, n):
                for half in range(2):
                    last = nc.tensor.matmul(flip_bank[:, n, half, 0:HALF * CH_GROUP], flip[:, :],
                                            v_all[:, half * HALF:(half + 1) * HALF, bass.ds(g * CH_GROUP, CH_GROUP)],
                                            start=True, stop=True)
                last.then_inc(flip_done, 1)

            def body(i, g, n, ahead):
                if ahead:
                    turn(g + 1, (n + 1) % 2)
                pe.wait_ge(flip_kept, g + 2)
                for j in range(2):
                    m = 2 * n + j
                    pe.wait_ge(loaded[m], (i + 1) * 16)
                    pe.wait_ge(kept[j], g + 1)
                    for c in range(CH_GROUP):
                        o = bank[:, m, c * NT:(c + 1) * NT]
                        tiles = flipped[:, n, :, :, c].rearrange("p f (b t) -> p (f b) t", t=TPS + 1)
                        nc.tensor.matmul(o, band[:, m, c, 0:P], tiles[:, :, 1:], start=True, stop=False)
                        last = nc.tensor.matmul(o, band[:, m, c, P:REACH], tiles[:, :, 0:TPS],
                                                start=False, stop=True)
                    last.then_inc(products, 1)

            turn(0, 0)
            groups_of(body, pe)

        def keep(eng, copy, i, g, n, j):
            m = 2 * n + j
            eng.wait_ge(products, g * 2 + (j + 1))
            copy(filtered[:, j, :, bass.ds(g * CH_GROUP, CH_GROUP)],
                 bank[:, m, :].rearrange("p (c t) -> p t c", c=CH_GROUP)).then_inc(kept[j], 1)

        @block.scalar
        def _(act):
            act.sem_inc(kept[0], 2)
            act.sem_inc(flip_kept, 1)

            def keep_flipped(g, n):
                act.wait_ge(flip_done, g + 1)
                nc.scalar.activation(flipped[:, n, :, :, :].rearrange("p f t c -> p f (t c)"),
                                     flip_bank[:, n, :, 0:HALF * CH_GROUP], ACT.Copy).then_inc(flip_kept, 1)

            def body(i, g, n, ahead):
                if ahead:
                    keep_flipped(g + 1, (n + 1) % 2)
                keep(act, lambda o, x: nc.scalar.activation(o, x, ACT.Copy), i, g, n, 0)

            keep_flipped(0, 0)
            groups_of(body, act)

        @block.vector
        def _(dve):
            dve.sem_inc(kept[1], 2)
            groups_of(lambda i, g, n, ahead: keep(dve, nc.vector.tensor_copy, i, g, n, 1), dve)


def delta_rule(nc, tag, io, identity, v_all, beta, qk_dram, delta_dram):
    LEVELS = 7
    NL = LEVELS - 1
    with Stage(nc, tag) as s:
        level_masks = s.sb("level_masks", [P, LEVELS + 1, P])
        minus_first = s.sb("minus_first", [P, 2, P])
        upto, same_head = s.sb("upto", [P, P]), s.sb("same_head", [P, P])
        qk = s.sb("qk", [P, 2, TPS, 2 * C])
        kb, vb = s.sb("kb", [P, 2, C]), s.sb("vb", [P, 2, C])
        turned = s.sb("turned", [P, 2, 3, P])
        X, XT, AT = s.sb("X", [P, 2, DH, P]), s.sb("XT", [P, 2, DH, P]), s.sb("AT", [P, 2, DH, P])
        local = s.sb("local", [P, 2, DH, P])
        Y = s.sb("Y", [P, 2, DH, P])
        R, U = s.sb("R", [P, C]), s.sb("U", [P, C])
        S, dS = s.sb("S", [P, C]), s.sb("dS", [P, C])
        out = s.sb("out", [P, 2, TPS, C])
        bank = s.ps("bank", [P, 4, DH * P])
        zt_bank = s.ps("zt_bank", [P, 2, DH * P])
        t_bank, s_bank = s.ps("t_bank", [P, DH * P]), s.ps("s_bank", [P, 4, C])

        masks_in, made, made_step = s.sem("masks_in"), s.sem("constants_made"), s.sem("made_step")
        cleared = s.sem("same_head_cleared")
        qk_in = [s.sem(f"qk_in{n}") for n in range(2)]
        scaled, turns_done, turned_kept = s.sem("scaled"), s.sem("turns_done"), s.sem("turned_kept_1")
        products, starts_kept, at_kept, starts_ready = (
            s.sem("products"), s.sem("starts_kept"), s.sem("at_kept_1"), s.sem("starts_ready"))
        y_done, y_kept, z_done, x_kept = s.sem("y_done"), s.sem("y_kept"), s.sem("z_done"), s.sem("x_kept")
        r_done, r_kept, u_done, u_kept = s.sem("r_done"), s.sem("r_kept"), s.sem("u_done"), s.sem("u_kept")
        s_done, ds_kept, s_kept = s.sem("s_done_1"), s.sem("ds_kept"), s.sem("s_kept")
        out_kept = s.sem("out_kept_1")
        stored = [s.sem(f"stored{n}_1") for n in range(2)]
        MADE = 4
        block = s.block()

        def pairs(body, eng):
            with eng.Fori(0, B // 2) as i:
                for n in range(2):
                    body(i, i * 2 + n, n)

        def lv(b, t, l):
            return b * (TPS * NL) + (t // 2) * (2 * NL) + (l - 1) * 2 + t % 2

        @block.sync
        def _(sp):
            sp.dma_start(level_masks[:, :, :], io["level_masks"].rearrange("l p n -> p l n")).then_inc(masks_in, 16)
            for n in range(2):
                sp.sem_inc(stored[n], 16)
                sp.dma_start(qk[:, n, :, :], qk_dram[n]).then_inc(qk_in[n], 16)

            def store(b, n):
                sp.wait_ge(out_kept, b * TPS + (TPS + 1))
                sp.dma_start(delta_dram[bass.ds(b, 1)].rearrange("o p t c -> p (o t) c"), out[:, n, :, :])\
                  .then_inc(stored[n], 16)

            with sp.Fori(0, B // 2 - 1) as i:
                for n in range(2):
                    b = i * 2 + n
                    store(b, n)
                    sp.dma_start(qk[:, n, :, :], qk_dram[bass.ds(b + 2, 1)].rearrange("o p t c -> p (o t) c"))\
                      .then_inc(qk_in[n], 16)
            for n in range(2):
                store(B - 2 + n, n)
            for n in range(2):
                sp.wait_ge(stored[n], 16 * (B // 2 + 1))

        @block.gpsimd
        def _(pool):
            g = nc.gpsimd
            g.memset(upto[:, :], 1.0).then_inc(made_step, 1)
            pool.wait_ge(made_step, 1)
            g.affine_select(out=upto[:, :], in_=upto[:, :], compare_op=ALU.is_ge, fill=0.0, base=0,
                            pattern=[[1, P]], channel_multiplier=-1).then_inc(made, 1)
            pool.wait_ge(masks_in, 16)
            g.tensor_scalar(minus_first[:, 0, :], level_masks[:, 0, :], -1.0, None, ALU.mult).then_inc(made, 1)
            g.tensor_scalar(minus_first[:, 1, :], level_masks[:, LEVELS, :], -1.0, None, ALU.mult).then_inc(made, 1)
            pool.wait_ge(made, MADE)

            def body(i, b, n):
                for t in range(TPS):
                    m = t % 2
                    if t == 0:
                        pool.wait_ge(qk_in[n], i * 16 + 16)
                    pool.wait_ge(s_done, b * TPS + (t if t >= 2 else 1))
                    w = beta[:, bass.ds(b * TPS + t, 1), :].rearrange("p o h -> p (o h)").unsqueeze(2)\
                        .to_broadcast([P, DH, DK])
                    heads = lambda x: x.rearrange("p (h d) -> p h d", d=DK)
                    g.tensor_tensor(heads(kb[:, m, :]), heads(qk[:, n, t, C:]), w, ALU.mult)
                    vt = v_all[:, bass.ds(b * (TPS + 1) + (1 + t), 1), :].rearrange("p o c -> p (o c)")
                    g.tensor_tensor(heads(vb[:, m, :]), heads(vt), w, ALU.mult).then_inc(scaled, 1)
                    if t % 2:
                        for tt in (t - 1, t):
                            pool.wait_ge(starts_kept, b * TPS + (tt + 1))
                            for x in (X, XT):
                                last = g.tensor_tensor(x[:, tt % 2, :, :], x[:, tt % 2, :, :],
                                                       identity[:, :].unsqueeze(1).to_broadcast([P, DH, P]), ALU.add)
                            last.then_inc(starts_ready, 1)

            pairs(body, pool)

        @block.tensor
        def _(pe):
            pe.sem_inc(s_done, 1)
            pe.wait_ge(made, MADE)

            def body(i, b, n):
                def first(t):
                    m = t % 2
                    c = b * TPS + t
                    pe.wait_ge(scaled, c + 1)
                    pe.wait_ge(turned_kept, c + 1)
                    for x, src in enumerate((qk[:, n, t, C:], kb[:, m, :], qk[:, n, t, 0:C])):
                        last = nc.tensor.transpose(t_bank[:, x * P:(x + 1) * P], src, identity[:, :])
                    last.then_inc(turns_done, 1)
                    pe.wait_ge(turned_kept, c + 2)
                    pe.wait_ge(at_kept, c + 1)
                    if t == 2:
                        pe.wait_ge(x_kept, lv(b, 1, NL) + 1)
                    for h in range(DH):
                        rows = slice(DK * h, DK * h + DK)
                        nc.tensor.matmul(bank[:, h, 0:P], turned[rows, m, 1, :], turned[rows, m, 0, :],
                                         start=True, stop=True)
                        last = nc.tensor.matmul(bank[:, h, P:3 * P], turned[rows, m, 0, :],
                                                turned[rows, m, 1:3, :].rearrange("p x n -> p (x n)"),
                                                start=True, stop=True)
                    last.then_inc(products, 1)

                def state(t):
                    m = t % 2
                    c = b * TPS + t
                    pe.wait_ge(x_kept, lv(b, t, NL) + 1)
                    pe.wait_ge(s_kept, c + 1)
                    nc.tensor.matmul(s_bank[:, 0, :], turned[:, m, 1, :], S[:, :], start=True, stop=True)\
                      .then_inc(r_done, 1)
                    pe.wait_ge(r_kept, c + 1)
                    for h in range(DH):
                        cols = slice(DK * h, DK * h + DK)
                        last = nc.tensor.matmul(s_bank[:, 1, cols], XT[:, m, h, :], R[:, cols], start=True, stop=True)
                    last.then_inc(u_done, 1)
                    pe.wait_ge(u_kept, c + 1)
                    for h in range(DH):
                        cols = slice(DK * h, DK * h + DK)
                        nc.tensor.matmul(s_bank[:, 2, cols], turned[:, m, 2, :], S[:, cols], start=True, stop=False)
                        last = nc.tensor.matmul(s_bank[:, 2, cols], local[:, m, h, :], U[:, cols],
                                                start=False, stop=True)
                    if t < TPS - 1:
                        last = nc.tensor.matmul(s_bank[:, 3, :], qk[:, n, t, C:], U[:, :], start=True, stop=True)
                    last.then_inc(s_done, 1)

                for t0 in (0, 2):
                    first(t0)
                    first(t0 + 1)
                    for l in range(1, LEVELS):
                        for m in range(2):
                            t = t0 + m
                            k = lv(b, t, l)
                            if l == 1:
                                pe.wait_ge(starts_ready, b * TPS + t + 1)
                                pe.wait_ge(at_kept, b * TPS + t0 + 3)
                            else:
                                pe.wait_ge(x_kept, k - 1)
                            for h in range(DH):
                                last = nc.tensor.matmul(bank[:, m, h * P:(h + 1) * P], AT[:, m, h, :], X[:, m, h, :],
                                                        start=True, stop=True)
                            last.then_inc(y_done, 1)
                        for m in range(2):
                            k = lv(b, t0 + m, l)
                            pe.wait_ge(y_kept, k + 1)
                            for h in range(DH):
                                if l < NL:
                                    nc.tensor.matmul(bank[:, 2 + m, h * P:(h + 1) * P], XT[:, m, h, :], Y[:, m, h, :],
                                                     start=True, stop=True)
                                last = nc.tensor.matmul(zt_bank[:, m, h * P:(h + 1) * P], Y[:, m, h, :],
                                                        XT[:, m, h, :], start=True, stop=True)
                            last.then_inc(z_done, 1)
                    state(t0)
                    state(t0 + 1)

            pairs(body, pe)

        @block.scalar
        def _(act):
            act.sem_inc(turned_kept, 1)
            act.sem_inc(at_kept, 1)
            act.sem_inc(out_kept, 1)

            def body(i, b, n):
                for t0 in (0, 2):
                    for t in (t0, t0 + 1):
                        m, c = t % 2, b * TPS + t
                        act.wait_ge(turns_done, c + 1)
                        act.wait_ge(s_done, b * TPS + t0 + 1)
                        nc.scalar.activation(turned[:, m, :, :].rearrange("p x n -> p (x n)"), t_bank[:, 0:3 * P],
                                             ACT.Copy).then_inc(turned_kept, 1)
                        act.wait_ge(starts_kept, c + 1)
                        nc.scalar.activation(AT[:, m, :, :], bank[:, :, P:2 * P], ACT.Copy).then_inc(at_kept, 1)
                    for t in (t0, t0 + 1):
                        c = b * TPS + t
                        act.wait_ge(u_done, c + 1)
                        nc.scalar.activation(U[:, :], s_bank[:, 1, :], ACT.Copy).then_inc(u_kept, 1)
                        if t == 0:
                            act.wait_ge(stored[n], i * 16 + 16)
                        act.wait_ge(s_done, c + 2)
                        nc.scalar.activation(out[:, n, t, :], s_bank[:, 2, :], ACT.Copy).then_inc(out_kept, 1)

            pairs(body, act)

        @block.vector
        def _(dve):
            v = nc.vector
            v.memset(same_head[:, :], 0.0).then_inc(cleared, 1)
            dve.wait_ge(cleared, 1)
            for h in range(DH):
                last = v.memset(same_head[DK * h:DK * h + DK, DK * h:DK * h + DK], 1.0)
            last.then_inc(made, 1)
            dve.wait_ge(made, MADE)
            dve.wait_ge(masks_in, 16)

            def over_heads(x):
                return x.unsqueeze(1).to_broadcast([P, DH, P])

            def body(i, b, n):
                dve.wait_ge(s_done, b * TPS + 1)
                v.memset(S[:, :], 0.0).then_inc(s_kept, 1)
                for t0 in (0, 2):
                    for t in (t0, t0 + 1):
                        m, c = t % 2, b * TPS + t
                        dve.wait_ge(products, c + 1)
                        v.tensor_tensor(X[:, m, :, :], bank[:, :, 0:P], over_heads(minus_first[:, 0, :]), ALU.mult)
                        v.tensor_tensor(XT[:, m, :, :], bank[:, :, P:2 * P], over_heads(minus_first[:, 1, :]), ALU.mult)
                        v.tensor_tensor(local[:, m, :, :], bank[:, :, 2 * P:3 * P], over_heads(upto[:, :]), ALU.mult)\
                         .then_inc(starts_kept, 1)
                    for l in range(1, LEVELS):
                        for m in range(2):
                            k = lv(b, t0 + m, l)
                            dve.wait_ge(y_done, k + 1)
                            v.tensor_tensor(Y[:, m, :, :], bank[:, m, :].rearrange("p (h n) -> p h n", h=DH),
                                            over_heads(level_masks[:, l, :]), ALU.mult).then_inc(y_kept, 1)
                        for m in range(2):
                            k = lv(b, t0 + m, l)
                            dve.wait_ge(z_done, k + 1)
                            heads = lambda x: x.rearrange("p h n -> p (h n)")
                            if l < NL:
                                v.tensor_tensor(heads(X[:, m, :, :]), heads(X[:, m, :, :]), bank[:, 2 + m, :],
                                                ALU.subtract)
                            v.tensor_tensor(heads(XT[:, m, :, :]), heads(XT[:, m, :, :]), zt_bank[:, m, :],
                                            ALU.subtract).then_inc(x_kept, 1)
                    for t in (t0, t0 + 1):
                        c = b * TPS + t
                        dve.wait_ge(r_done, c + 1)
                        v.tensor_tensor(R[:, :], vb[:, t % 2, :], s_bank[:, 0, :], ALU.subtract).then_inc(r_kept, 1)
                        if t < TPS - 1:
                            dve.wait_ge(s_done, c + 2)
                            dve.wait_ge(out_kept, c + 2)
                            v.tensor_tensor(dS[:, :], s_bank[:, 3, :], same_head[:, :], ALU.mult).then_inc(ds_kept, 1)
                            dve.wait_ge(ds_kept, b * (TPS - 1) + t + 1)
                            v.tensor_tensor(S[:, :], S[:, :], dS[:, :], ALU.add).then_inc(s_kept, 1)

            pairs(body, dve)


SOURCES = 4
KINDS = 4
FLOOR = 0.05
SUM_EPS = 1e-5


def gated_sum(nc, tag, io, X, stats, identity, v_all, filtered, delta_dram):
    TH = TPS * DH
    with Stage(nc, tag) as s:
        w1 = s.sb("w1", [P, C])
        w1_stats = s.sb("w1_stats", [P, C])
        b1, w2, wo = s.sb("b1", [P, 1]), s.sb("w2", [P, SOURCES]), s.sb("wo", [P, C])
        rms_w = s.sb("rms_w", [P, DK])
        bias, b2 = s.sb("bias", [P, DH, SOURCES]), s.sb("b2", [P, SOURCES])
        log_temp, inv_temp = s.sb("log_temp", [P, DH]), s.sb("inv_temp", [P, DH])
        soft, residual = s.sb("soft", [P, DH]), s.sb("residual", [P, DH])
        half = s.sb("half", [P, TH * SOURCES])
        minus_half = s.sb("minus_half", [P, TH])
        delta = s.sb("delta", [P, 2, TPS, C])
        stat = s.sb("stat", [P, 2, TH, DK])
        squares = s.sb("squares", [P, SOURCES, TH, DK])
        weighted = s.sb("weighted", [P, SOURCES, TH, DK])
        length = s.sb("length", [P, TH, SOURCES])
        hn = s.sb("hn", [P, 2, TPS, C])
        hT, statT = s.sb("hT", [P, T]), s.sb("statT", [P, T])
        hidden = s.sb("hidden", [P, DH, T])
        logits, top = s.sb("logits", [P, TH, SOURCES]), s.sb("top", [P, TH])
        shares, rec = s.sb("shares", [P, TH, SOURCES]), s.sb("rec", [P, TH])
        o, o_sq = s.sb("o", [P, TH, DK]), s.sb("o_sq", [P, TH, DK])
        rms = s.sb("rms", [P, TH])
        on, oT = s.sb("on", [P, TH, DK]), s.sb("oT", [P, T])
        t_bank, stat_bank = s.ps("t_bank", [P, T]), s.ps("stat_bank", [P, T])
        hidden_bank = s.ps("hidden_bank", [P, DH, T])
        logit_bank, y_bank = s.ps("logit_bank", [P, T]), s.ps("y_bank", [P, T])

        loaded, made, step = s.sem("weights_loaded"), s.sem("constants_made"), s.sem("constants_step")
        delta_in = [s.sem(f"delta_in{n}") for n in range(2)]
        sums_step, sums_ready = s.sem("sums_step"), s.sem("sums_ready")
        centred, squares_ready = s.sem("centred"), s.sem("squares_ready")
        length_step, stats_ready, hn_ready = s.sem("length_step"), s.sem("stats_ready"), s.sem("hn_ready")
        turned, turned_kept = s.sem("turned"), s.sem("turned_kept")
        hidden_done, gelu_done, logits_done = s.sem("hidden_done"), s.sem("gelu_done"), s.sem("logits_done")
        soft_step, exp_ready, shares_ready = s.sem("soft_step"), s.sem("exp_ready"), s.sem("shares_ready")
        shared, o_ready, o_sq_ready = s.sem("sources_shared"), s.sem("o_ready"), s.sem("o_sq_ready")
        ms_ready, rms_step, rms_ready = s.sem("ms_ready"), s.sem("rms_step"), s.sem("rms_ready")
        waited = s.sem("waited")
        floor_done, on_step, on_ready, added = s.sem("floor_done"), s.sem("on_step"), s.sem("on_ready"), s.sem("added")
        o_turned, oT_kept, y_done = s.sem("o_turned"), s.sem("oT_kept"), s.sem("y_done")
        LOADED, MADE = 16 * 13, 8
        SOFT_STEPS = 10
        block = s.block()

        def sequences(body, eng):
            with eng.Fori(0, B // 2 - 1) as i:
                for n in range(2):
                    body(i, i * 2 + n, n, True)
            body(B // 2 - 1, B - 2, 0, True)
            body(B // 2 - 1, B - 1, 1, False)

        def heads(x):
            return x.rearrange("p t (h d) -> p (t h) d", d=DK)

        def sources(b, n):
            filters = filtered[:, :, bass.ds(b * TPS, TPS), :].rearrange("p s t (h d) -> p s (t h) d", d=DK)
            return [(0, 2, filters), (2, 1, heads(delta[:, n, :, :]).unsqueeze(1)),
                    (3, 1, heads(v_all[:, bass.ds(b * (TPS + 1) + 1, TPS), :]).unsqueeze(1))]

        def kind(n, k):
            return stat[:, n, :, k:SOURCES * KINDS:KINDS]

        @block.sync
        def _(sp):
            sp.dma_start(w1[:, :], io["w1"][0:C]).then_inc(loaded, 16)
            for h in range(DH):
                sp.dma_start(w1_stats[DK * h:DK * h + SOURCES * KINDS, :], io["w1"][C:]).then_inc(loaded, 16)
            sp.dma_start(b1[:, :], io["b1"].unsqueeze(1)).then_inc(loaded, 16)
            sp.dma_start(w2[:, :], io["w2"]).then_inc(loaded, 16)
            sp.dma_start(wo[:, :], io["wo"]).then_inc(loaded, 16)
            sp.dma_start(rms_w[:, :], io["rms_w"].partition_broadcast(P)).then_inc(loaded, 16)
            sp.dma_start(bias[:, :, :], io["base_bias"].partition_broadcast(P)).then_inc(loaded, 16)
            sp.dma_start(b2[:, :], io["b2"].partition_broadcast(P)).then_inc(loaded, 16)
            sp.dma_start(log_temp[:, :], io["log_temp"].partition_broadcast(P)).then_inc(loaded, 16)
            sp.dma_start(residual[:, :], io["residual"].partition_broadcast(P)).then_inc(loaded, 16)
            for n in range(2):
                sp.dma_start(delta[:, n, :, :], delta_dram[n]).then_inc(delta_in[n], 16)
            with sp.Fori(0, B // 2 - 1) as i:
                for n in range(2):
                    sp.wait_ge(shared, i * 2 + (n + 1))
                    sp.dma_start(delta[:, n, :, :], delta_dram[bass.ds(i * 2 + (n + 2), 1)]
                                 .rearrange("o p t c -> p (o t) c")).then_inc(delta_in[n], 16)

        @block.gpsimd
        def _(pool):
            g = nc.gpsimd
            g.memset(half[:, :], 0.5).then_inc(made, 1)
            g.memset(minus_half[:, :], -0.5).then_inc(made, 1)
            g.memset(stat[:, :, :, :], 0.0).then_inc(made, 1)
            pool.wait_ge(loaded, LOADED)
            pool.wait_ge(made, MADE)

            def centre(b, n):
                pool.wait_ge(sums_ready, b + 1)
                pool.sem_inc(waited, 1)
                for s0, k, x in sources(b, n):
                    mean = kind(n, 0)[:, :, s0:s0 + k].rearrange("p n s -> p s n").unsqueeze(3)\
                        .to_broadcast([P, k, TH, DK])
                    last = g.tensor_tensor(squares[:, s0:s0 + k, :, :], x, mean, ALU.subtract)
                last.then_inc(centred, 1)

            def lengths(b, n):
                pool.wait_ge(length_step, b * 2 + 2)
                g.tensor_tensor(kind(n, 3), length[:, :, :],
                                half[:, :].rearrange("p (n s) -> p n s", s=SOURCES), ALU.pow).then_inc(stats_ready, 1)

            def body(i, b, n, ahead):
                m = (n + 1) % 2
                if ahead:
                    centre(b + 1, m)
                    lengths(b + 1, m)
                pool.wait_ge(shares_ready, b + 1)
                pool.sem_inc(waited, 1)
                for s0, k, x in sources(b, n):
                    share = shares[:, :, s0:s0 + k].rearrange("p n s -> p s n").unsqueeze(3)\
                        .to_broadcast([P, k, TH, DK])
                    last = g.tensor_tensor(weighted[:, s0:s0 + k, :, :], x, share, ALU.mult)
                last.then_inc(shared, 1)
                pool.wait_ge(ms_ready, b + 1)
                pool.sem_inc(rms_step, 1)
                g.tensor_scalar(rms[:, :], rms[:, :], 1.0 / DK, SUM_EPS, ALU.mult, ALU.add).then_inc(rms_step, 1)
                pool.wait_ge(rms_step, b * 2 + 2)
                g.tensor_tensor(rms[:, :], rms[:, :], minus_half[:, :], ALU.pow).then_inc(rms_ready, 1)
                pool.wait_ge(on_step, b + 1)
                g.tensor_tensor(on[:, :, :], on[:, :, :], rms_w[:, :].unsqueeze(1).to_broadcast([P, TH, DK]),
                                ALU.mult).then_inc(on_ready, 1)

            centre(0, 0)
            lengths(0, 0)
            sequences(body, pool)

        @block.tensor
        def _(pe):
            pe.wait_ge(loaded, LOADED)
            pe.wait_ge(made, MADE)

            def body(i, b, n, ahead):
                pe.wait_ge(hn_ready, b + 1)
                pe.wait_ge(stats_ready, b * 2 + 2)
                for t in range(TPS):
                    cols = slice(t * P, (t + 1) * P)
                    nc.tensor.transpose(t_bank[:, cols], hn[:, n, t, :], identity[:, :])
                    last = nc.tensor.transpose(stat_bank[:, cols],
                                               stat[:, n, t * DH:(t + 1) * DH, :].rearrange("p h k -> p (h k)"),
                                               identity[:, :])
                last.then_inc(turned, 1)
                pe.wait_ge(turned_kept, b + 1)
                for h in range(DH):
                    rows = slice(DK * h, DK * h + SOURCES * KINDS)
                    nc.tensor.matmul(hidden_bank[:, h, :], w1[:, :], hT[:, :], start=True, stop=False)
                    nc.tensor.matmul(hidden_bank[:, h, :], w1_stats[rows, :], statT[rows, :], start=False, stop=True)\
                      .then_inc(hidden_done, 1)
                for h in range(DH):
                    pe.wait_ge(gelu_done, b * DH + (h + 1))
                    for t in range(TPS):
                        c = (t * DH + h) * SOURCES
                        last = nc.tensor.matmul(logit_bank[:, c:c + SOURCES], hidden[:, h, t * P:(t + 1) * P],
                                                w2[:, :], start=True, stop=True)
                last.then_inc(logits_done, 1)
                pe.wait_ge(on_ready, b + 1)
                for t in range(TPS):
                    last = nc.tensor.transpose(t_bank[:, t * P:(t + 1) * P],
                                               on[:, t * DH:(t + 1) * DH, :].rearrange("p h d -> p (h d)"),
                                               identity[:, :])
                last.then_inc(o_turned, 1)
                pe.wait_ge(oT_kept, b + 1)
                for t in range(TPS):
                    last = nc.tensor.matmul(y_bank[:, t * P:(t + 1) * P], oT[:, t * P:(t + 1) * P], wo[:, :],
                                            start=True, stop=True)
                last.then_inc(y_done, 1)

            sequences(body, pe)

        @block.scalar
        def _(act):
            act.wait_ge(loaded, LOADED)
            nc.scalar.activation(soft[:, :], log_temp[:, :], ACT.Abs).then_inc(step, 1)
            act.wait_ge(step, 1)
            nc.scalar.activation(soft[:, :], soft[:, :], ACT.Exp, scale=-1.0).then_inc(step, 1)
            act.wait_ge(step, 3)
            nc.scalar.activation(soft[:, :], soft[:, :], ACT.Ln).then_inc(step, 1)
            nc.scalar.activation(residual[:, :], residual[:, :], ACT.Sigmoid).then_inc(step, 1)

            def square(b):
                act.wait_ge(centred, b + 1)
                nc.scalar.activation(squares[:, :, :, :], squares[:, :, :, :], ACT.Square).then_inc(squares_ready, 1)

            def body(i, b, n, ahead):
                act.wait_ge(turned, b + 1)
                nc.scalar.activation(hT[:, :], t_bank[:, :], ACT.Copy)
                nc.scalar.activation(statT[:, :], stat_bank[:, :], ACT.Copy).then_inc(turned_kept, 1)
                for h in range(DH):
                    act.wait_ge(hidden_done, b * DH + (h + 1))
                    nc.scalar.activation(hidden[:, h, :], hidden_bank[:, h, :], ACT.Gelu, bias=b1[:, 0:1])\
                      .then_inc(gelu_done, 1)
                if ahead:
                    square(b + 1)
                act.wait_ge(soft_step, b * SOFT_STEPS + 4)
                nc.scalar.activation(shares[:, :, :], logits[:, :, :], ACT.Exp).then_inc(exp_ready, 1)
                act.wait_ge(o_ready, b + 1)
                nc.scalar.activation(o_sq[:, :, :], o[:, :, :], ACT.Square).then_inc(o_sq_ready, 1)
                act.wait_ge(o_turned, b + 1)
                nc.scalar.activation(oT[:, :], t_bank[:, :], ACT.Copy).then_inc(oT_kept, 1)

            square(0)
            sequences(body, act)

        @block.vector
        def _(dve):
            v = nc.vector
            dve.wait_ge(loaded, LOADED)
            v.tensor_tensor(bias[:, :, :], bias[:, :, :], b2[:, :].unsqueeze(1).to_broadcast([P, DH, SOURCES]),
                            ALU.add).then_inc(made, 1)
            dve.wait_ge(step, 2)
            v.tensor_scalar(soft[:, :], soft[:, :], 1.0, None, ALU.add).then_inc(step, 1)
            dve.wait_ge(step, 5)
            v.tensor_scalar(residual[:, :], residual[:, :], 0.5, None, ALU.mult).then_inc(made, 1)
            v.tensor_scalar(log_temp[:, :], log_temp[:, :], 0.0, 1e-4, ALU.max, ALU.add).then_inc(made, 1)
            dve.wait_ge(made, 6)
            v.tensor_tensor(inv_temp[:, :], log_temp[:, :], soft[:, :], ALU.add).then_inc(made, 1)
            dve.wait_ge(made, 7)
            v.reciprocal(inv_temp[:, :], inv_temp[:, :]).then_inc(made, 1)
            dve.wait_ge(made, MADE)

            def sums(b, n, i):
                dve.wait_ge(delta_in[n], (i + 1) * 16)
                for s0, k, x in sources(b, n):
                    out = lambda j: kind(n, j)[:, :, s0:s0 + k].rearrange("p n s -> p s n")
                    v.reduce_sum(out(0), x, AX.X)
                    last = v.reduce_sum(out(2), x, AX.X, apply_absolute_value=True)
                last.then_inc(sums_step, 1)
                dve.wait_ge(sums_step, b + 1)
                both = stat[:, n, :, 0:SOURCES * KINDS:2]
                v.tensor_scalar(both, both, 1.0 / DK, None, ALU.mult).then_inc(sums_ready, 1)
                for t in range(TPS):
                    tile = b * TPS + t
                    last = v.tensor_scalar(hn[:, n, t, :], tile_of(X, tile), stats[:, bass.ds(tile, 1), 0],
                                           stats[:, bass.ds(tile, 1), 1], ALU.subtract, ALU.mult)
                last.then_inc(hn_ready, 1)

            def variances(b, n):
                dve.wait_ge(squares_ready, b + 1)
                v.scalar_tensor_tensor(length[:, :, :], kind(n, 0), float(DK), kind(n, 0), ALU.mult, ALU.mult)
                v.reduce_sum(kind(n, 1).rearrange("p n s -> p s n"), squares[:, :, :, :], AX.X)\
                 .then_inc(length_step, 1)
                dve.wait_ge(length_step, b * 2 + 1)
                v.tensor_tensor(length[:, :, :], length[:, :, :], kind(n, 1), ALU.add).then_inc(length_step, 1)
                dve.wait_ge(length_step, b * 2 + 2)
                v.tensor_scalar(kind(n, 1), kind(n, 1), 1.0 / DK, None, ALU.mult).then_inc(stats_ready, 1)

            def body(i, b, n, ahead):
                m = (n + 1) % 2
                if ahead:
                    sums(b + 1, m, i + n)

                def done(k):
                    return b * SOFT_STEPS + k

                def each(x):
                    return x.unsqueeze(2).to_broadcast([P, TH, SOURCES])

                dve.wait_ge(logits_done, b + 1)
                v.tensor_tensor(logits[:, :, :].rearrange("p (t h) s -> p t (h s)", h=DH),
                                logit_bank[:, 0:TH * SOURCES].rearrange("p (t k) -> p t k", t=TPS),
                                bias[:, :, :].rearrange("p h s -> p (h s)").unsqueeze(1)
                                .to_broadcast([P, TPS, DH * SOURCES]), ALU.add).then_inc(soft_step, 1)
                dve.wait_ge(soft_step, done(1))
                v.tensor_tensor(logits[:, :, :].rearrange("p (t h) s -> p t h s", h=DH),
                                logits[:, :, :].rearrange("p (t h) s -> p t h s", h=DH),
                                inv_temp[:, :].unsqueeze(1).unsqueeze(3).to_broadcast([P, TPS, DH, SOURCES]),
                                ALU.mult).then_inc(soft_step, 1)
                dve.wait_ge(soft_step, done(2))
                v.reduce_max(top[:, :], logits[:, :, :], AX.X).then_inc(soft_step, 1)
                dve.wait_ge(soft_step, done(3))
                v.tensor_tensor(logits[:, :, :], logits[:, :, :], each(top[:, :]), ALU.subtract)\
                 .then_inc(soft_step, 1)
                if ahead:
                    variances(b + 1, m)
                dve.wait_ge(exp_ready, b + 1)
                for j in range(2):
                    v.reduce_sum(rec[:, :], shares[:, :, :], AX.X).then_inc(soft_step, 1)
                    dve.wait_ge(soft_step, done(3 * j + 5))
                    v.reciprocal(rec[:, :], rec[:, :]).then_inc(soft_step, 1)
                    dve.wait_ge(soft_step, done(3 * j + 6))
                    last = v.tensor_tensor(shares[:, :, :], shares[:, :, :], each(rec[:, :]), ALU.mult)
                    last.then_inc(soft_step, 1)
                    if j == 0:
                        dve.wait_ge(soft_step, done(7))
                        v.tensor_scalar(shares[:, :, 0:2], shares[:, :, 0:2], FLOOR, None, ALU.max)\
                         .then_inc(floor_done, 1)
                        dve.wait_ge(floor_done, b + 1)
                dve.wait_ge(soft_step, done(10))
                short = shares[:, :, 0].rearrange("p (t h) -> p t h", h=DH)
                v.tensor_tensor(short, short, residual[:, :].unsqueeze(1).to_broadcast([P, TPS, DH]), ALU.add)\
                 .then_inc(shares_ready, 1)
                dve.wait_ge(shared, b + 1)
                v.reduce_sum(o[:, :, :], weighted[:, :, :, :].rearrange("p s n d -> p n d s"), AX.X)\
                 .then_inc(o_ready, 1)
                dve.wait_ge(o_sq_ready, b + 1)
                v.reduce_sum(rms[:, :], o_sq[:, :, :], AX.X).then_inc(ms_ready, 1)
                dve.wait_ge(rms_ready, b + 1)
                v.tensor_tensor(on[:, :, :], o[:, :, :], rms[:, :].unsqueeze(2).to_broadcast([P, TH, DK]), ALU.mult)\
                 .then_inc(on_step, 1)
                dve.wait_ge(y_done, b + 1)
                x = X[:, bass.ds(b * TPS, TPS), :].rearrange("p t c -> p (t c)")
                v.tensor_tensor(x, x, y_bank[:, :], ALU.add).then_inc(added, 1)

            sums(0, 0, 0)
            variances(0, 0)
            sequences(body, dve)


def gated_delta(nc, tag, io, X, stats, identity):
    qk_dram = nc.dram_tensor(f"{tag}_qk_dram", (B, P, TPS, 2 * C), F32, kind="Internal").ap()
    delta_dram = nc.dram_tensor(f"{tag}_delta_dram", (B, P, TPS, C), F32, kind="Internal").ap()
    with Stage(nc, tag) as s:
        v_all = s.sb("v_all", [P, B * (TPS + 1), C])
        beta = s.sb("beta", [P, NT + TPS, DH])
        delta_inputs(nc, f"{tag}_in", io, X, stats, identity, v_all, beta, qk_dram)
        delta_rule(nc, f"{tag}_rule", io, identity, v_all, beta, qk_dram, delta_dram)
        filtered = s.sb("filtered", [P, 2, NT, C])
        long_filters(nc, f"{tag}_fir", io, v_all, filtered)
        gated_sum(nc, f"{tag}_gate", io, X, stats, identity, v_all, filtered, delta_dram)


def build(nc, io, layers=range(8)):
    with Stage(nc, "main") as s:
        X = s.sb("X", [P, NT + TPS, C])
        stats = s.sb("stats", [P, NT + TPS, 2])
        identity = s.sb("identity", [P, P])
        sorted_in = s.dram("sorted_in", (SORTED + SPARE, P, C))
        sorted_out = s.dram("sorted_out", (SORTED, P, C))
        load_x(nc, io, X, stats, identity, sorted_in)
        for n in layers:
            layernorm_stats(nc, f"l{n}", X, stats)
            if n in (0, 4):
                sub = {k[3:]: v for k, v in io.items() if k.startswith(f"a{n}_")}
                attention16(nc, f"l{n}", sub, X, stats, identity, causal=(n == 0), rope=(n == 4), biased=(n == 0))
            elif n in (1, 3):
                sub = {k[4:]: v for k, v in io.items() if k.startswith("ffn_")}
                mixture(nc, f"l{n}", sub, X, stats, identity, sorted_in, sorted_out)
            elif n in (5, 7):
                sub = {k[4:]: v for k, v in io.items() if k.startswith("mix_")}
                channel_mix(nc, f"l{n}", sub, X, stats, identity)
            elif n == 2:
                sub = {k[4:]: v for k, v in io.items() if k.startswith("swa_")}
                window_attention(nc, f"l{n}", sub, X, stats, identity)
            else:
                sub = {k[3:]: v for k, v in io.items() if k.startswith("dr_")}
                gated_delta(nc, f"l{n}", sub, X, stats, identity)
        store_x(nc, io, X)


def layout(inputs):
    import numpy as np
    g = {k: np.asarray(v) for k, v in inputs.items()}
    a = {"x": g["L0_attn_a_x"]}
    w, bq = g["L0_attn_a_w_qkv"], g["L0_attn_a_b_qkv"]
    for j, n in enumerate("qkv"):
        a[f"a0_w_{n}"], a[f"a0_b_{n}"] = w[:, j * C:(j + 1) * C], bq[j * C:(j + 1) * C]
    a["a0_w_out"], a["a0_b_out"] = g["L0_attn_a_w_out"], g["L0_attn_a_b_out"]
    swap = np.arange(C) ^ 1
    for n in "qkv":
        a[f"a4_w_{n}"] = g[f"L1_attn_a_w{n}"].T
    for n in "qk":
        a[f"a4_w_{n}_swapped"] = g[f"L1_attn_a_w{n}"][swap].T
    a["a4_w_out"] = g["L1_attn_a_wo"].T
    f = np.float32
    inv = (f(1) / f(10000) ** (np.arange(0, D, 2, dtype=f) / f(D))).astype(f)
    angle = np.outer(np.arange(T, dtype=f), inv).astype(f)
    which = (np.arange(C) % D) // 2
    sign = np.where(np.arange(C) % 2 == 0, f(-1), f(1))
    a["a4_cos"] = np.cos(angle).astype(f).T[which]
    a["a4_sin"] = np.sin(angle).astype(f).T[which] * sign[:, None]
    a["ffn_w_router"], a["ffn_b_router"] = g["L0_ffn_Wr"], g["L0_ffn_br"]
    a["ffn_w1"], a["ffn_w2"], a["ffn_b2"] = g["L0_ffn_W1"], g["L0_ffn_W2"], g["L0_ffn_b2"]
    a["ffn_b1"] = g["L0_ffn_b1"].reshape(E, FC, P).transpose(2, 0, 1)
    for n in "rkv":
        a[f"mix_w_{n}"] = g[f"L1_ffn_W_{n}"].T
    for n in "rk":
        a[f"mix_mu_{n}"] = g[f"L1_ffn_mu_{n}"]
    wq = g["L0_attn_b_wq"].reshape(2, 2, REP, HD, C).transpose(0, 2, 1, 3, 4).reshape(QH * HD, C)
    a["swa_w_q"] = wq.T
    a["swa_w_kv"] = np.concatenate([g["L0_attn_b_wk"], g["L0_attn_b_wv"]]).T
    a["swa_w_out"] = g["L0_attn_b_wo"].T
    a["swa_q_norm"], a["swa_k_norm"] = g["L0_attn_b_q_norm_w"], g["L0_attn_b_k_norm_w"]
    d = {n: g[f"L1_attn_b_{n}"] for n in ("Wq", "Wk", "Wv", "Wb", "W1", "b1", "W2", "b2", "log_temp", "base_bias",
                                          "conv_residual_logit", "rms_w", "Wo", "conv_q", "conv_k", "conv_v",
                                          "fir_short", "fir_long")}
    a["dr_w_qkv"] = np.concatenate([d["Wq"], d["Wk"], d["Wv"]], 1)
    a["dr_conv"] = np.concatenate([d["conv_q"], d["conv_k"], d["conv_v"]]).T
    a["dr_w_beta"], a["dr_w1"], a["dr_b1"], a["dr_w2"], a["dr_b2"] = d["Wb"], d["W1"], d["b1"], d["W2"], d["b2"]
    a["dr_log_temp"], a["dr_base_bias"], a["dr_residual"] = d["log_temp"], d["base_bias"], d["conv_residual_logit"]
    a["dr_rms_w"], a["dr_wo"] = d["rms_w"], d["Wo"]
    for n in ("short", "long"):
        taps = d[f"fir_{n}"].reshape(C, -1)
        row = np.zeros((C, FILTER_PAD), taps.dtype)
        row[:, P - 1:P - 1 + taps.shape[1]] = taps[:, ::-1]
        a[f"dr_{n}"] = row
    later, earlier = np.arange(P)[:, None], np.arange(P)[None, :]
    joins = [(later >> (l + 1) == earlier >> (l + 1)) & (later >> l & 1 == 1) & (earlier >> l & 1 == 0)
             for l in range(7)]
    a["dr_level_masks"] = np.stack(joins + [joins[0].T]).astype(np.float32)
    return {k: np.ascontiguousarray(v) for k, v in a.items()}


def kernel(**inputs):
    import concourse.bacc as _bacc
    from concourse import mybir as _mybir
    from concourse.bass_utils import run_bass_kernel_spmd as _run

    arrays = {f"in_{k}_dram": v for k, v in layout(inputs).items()}
    nc = _bacc.Bacc("TRN2", target_bir_lowering=False, num_devices=1)
    io = {k[3:-5]: nc.dram_tensor(k, v.shape, _mybir.dt.from_np(v.dtype), kind="ExternalInput").ap()
          for k, v in arrays.items()}
    io["out"] = nc.dram_tensor("out_0_dram", (B, T, C), F32, kind="ExternalOutput").ap()
    build(nc, io)
    r = _run(nc, [arrays], core_ids=[0])
    return r.results[0]["out_0_dram"]
```

```python
import concourse.bass as bass
from concourse import mybir
from contextlib import ExitStack

F32 = mybir.dt.float32
BF16 = mybir.dt.bfloat16
ACT = mybir.ActivationFunctionType
ALU = mybir.AluOpType
AX = mybir.AxisListType

P = 128
B, T, C = 16, 512, 128
TPS = T // P
NT = B * TPS
LN_EPS = 1e-5
MASKED = -1e30


class Stage:

    def __init__(self, nc, tag):
        self.nc, self.tag, self.stack, self.sems = nc, tag, ExitStack(), []

    def __enter__(self):
        return self

    def __exit__(self, kind, error, trace):
        if kind is None and self.sems:
            self.opened.close()
            for sem in self.sems:
                self.nc.sync.sem_clear(sem)
            self.nc.all_engine_barrier()
            for sem in reversed(self.sems):
                self.nc.release_semaphore(sem)
        return self.stack.__exit__(kind, error, trace)

    def sb(self, name, shape, dt=F32):
        return self.stack.enter_context(self.nc.sbuf_tensor(f"{self.tag}_{name}", shape, dt))

    def ps(self, name, shape, dt=F32):
        return self.stack.enter_context(self.nc.psum_tensor(f"{self.tag}_{name}", shape, dt))

    def sem(self, name):
        self.sems.append(self.nc.alloc_semaphore(f"{self.tag}_{name}"))
        return self.sems[-1]

    def block(self):
        self.opened = ExitStack()
        return self.opened.enter_context(self.nc.Block())

    def dram(self, name, shape, dt=F32):
        return self.nc.dram_tensor(f"{self.tag}_{name}", shape, dt, kind="Internal").ap()


def load_x(nc, io, X, stats, identity):
    with Stage(nc, "load") as s:
        loaded, identity_step = s.sem("loaded"), s.sem("identity_step")
        block = s.block()

        @block.sync
        def _(sp):
            for b in range(0, B, 4):
                sp.dma_start(X[:, b * TPS:(b + 4) * TPS, :],
                             io["x"][b:b + 4].rearrange("b (t p) c -> p (b t) c", p=P)).then_inc(loaded, 16)
            sp.wait_ge(loaded, 64)

        @block.vector
        def _(dve):
            nc.vector.memset(X[:, NT:, :], 0.0)
            nc.vector.memset(stats[:, :, :], 0.0)

        @block.gpsimd
        def _(pool):
            nc.gpsimd.memset(identity[:, :], 0.0).then_inc(identity_step, 1)
            pool.wait_ge(identity_step, 1)
            nc.gpsimd.affine_select(out=identity[:, :], in_=identity[:, :], compare_op=ALU.not_equal, fill=1.0,
                                    base=0, pattern=[[-1, P]], channel_multiplier=1)


def store_x(nc, io, X):
    with Stage(nc, "store") as s:
        stored = s.sem("stored")
        block = s.block()

        @block.sync
        def _(sp):
            for b in range(0, B, 4):
                sp.dma_start(io["out"][b:b + 4].rearrange("b (t p) c -> p (b t) c", p=P),
                             X[:, b * TPS:(b + 4) * TPS, :]).then_inc(stored, 16)
            sp.wait_ge(stored, 64)


def layernorm_stats(nc, tag, X, stats):
    with Stage(nc, f"{tag}_ln") as s:
        halves = s.sb("halves", [P, NT, 6])
        root = s.sb("root", [P, NT])
        s_halves, s_var, s_root = s.sem("halves_done"), s.sem("variance_ready"), s.sem("root_ready")
        block = s.block()

        @block.vector
        def _(dve):
            with dve.Fori(0, B // 4) as i:
                tiles, to = X[:, bass.ds(i * (4 * TPS), 4 * TPS), :], halves[:, bass.ds(i * (4 * TPS), 4 * TPS), :]
                for t in range(4 * TPS):
                    last = nc.vector.bn_stats(to[:, t, :], tiles[:, t, :])
                last.then_inc(s_halves, 1)
            dve.wait_ge(s_halves, B // 4)
            for t in range(NT):
                last = nc.vector.bn_aggr(stats[:, t, :], halves[:, t, :])
            last.then_inc(s_var, 1)
            dve.wait_ge(s_var, 1)
            nc.vector.tensor_scalar(root[:, :], stats[:, 0:NT, 1], LN_EPS, None, ALU.add).then_inc(s_var, 1)
            dve.wait_ge(s_root, 1)
            nc.vector.reciprocal(stats[:, 0:NT, 1], root[:, :])

        @block.scalar
        def _(act):
            act.wait_ge(s_var, 2)
            nc.scalar.activation(root[:, :], root[:, :], ACT.Sqrt).then_inc(s_root, 1)


H, D = 16, 8
STRIP = 32
PAIRS = H // 2
UNITS = TPS * PAIRS
LEAD = PAIRS + 2
PARTS = 3
Q_SLOTS = [(0, 3, 0), (3, 2, 1), (5, 1, 2)]
K_SLOTS = [(0, 3), (3, 2), (5, 1)]
ROW_LOADS = 2 * (len(Q_SLOTS) + len(K_SLOTS))
ROWS = 6 * D


def attention16(nc, tag, io, X, stats, identity, causal, rope, biased):
    with Stage(nc, tag) as s:
        w = {n: s.sb(f"w_{n}", [P, C]) for n in (["q", "k", "v", "out"] + (["q_swapped", "k_swapped"] if rope else []))}
        if biased:
            bias_col = s.sb("bias_col", [P, 2])
            bias_row = s.sb("bias_row", [1, 2, C])
            ones_row = s.sb("ones_row", [1, P])
        if rope:
            cos, sin = s.sb("cos", [P, T]), s.sb("sin", [P, T])
            rot = s.sb("rot", [P, 2, T])
        if causal:
            ident16 = s.sb("ident16", [P, P], BF16)
            mask_qk, mask_kq = s.sb("mask_qk", [P, P], BF16), s.sb("mask_kq", [P, P], BF16)
        hn = s.sb("hn", [P, TPS, C])
        hT = s.sb("hT", [P, T])
        qk = s.sb("qk", [P, 2, T])
        rest = s.sb("rest", [P, 2, T])
        parts = s.sb("parts", [P, 2, PARTS, T], BF16)
        QS = s.sb("QS", [P, 2, PAIRS, T], BF16)
        KS = s.sb("KS", [P, 2, PAIRS, T], BF16)
        V = s.sb("V", [P, 2, TPS, H, STRIP])
        M = s.sb("M", [P, 2, H])
        MT = s.sb("MT", [H, 2, P], BF16)
        probs = s.sb("probs", [P, 2, 2, T])
        rec = s.sb("rec", [P, H])
        heads_out = s.sb("heads_out", [P, T])
        on = s.sb("on", [P, C])
        oT = s.sb("oT", [P, P])
        parts_dram = s.dram("parts_dram", (2, 2, PARTS, P, T), BF16)
        max_bank = s.ps("max_bank", [P, 2, T])
        exp_bank = s.ps("exp_bank", [P, 2, 2, T])
        out_bank = s.ps("out_bank", [P, H // 4, P])
        misc = s.ps("misc", [P, T])

        loaded = s.sem("weights_loaded")
        prepared = s.sem("constants_ready")
        hn_ready = s.sem("hn_ready")
        misc_full, misc_free = s.sem("misc_full"), s.sem("misc_free")
        rotated = s.sem("rotated")
        split_step = s.sem("split_step")
        split_q, split_k = s.sem("split_q"), s.sem("split_k")
        parts_out = s.sem("parts_out")
        qk_in = [s.sem(f"qk_in{n}") for n in range(2)]
        max_scores, max_done = s.sem("max_scores"), s.sem("max_done")
        shift_in = [s.sem(f"shift_in{n}_1") for n in range(2)]
        scores, exp_done, pv_done = s.sem("scores"), s.sem("exp_done"), s.sem("pv_done")
        heads_kept, v_cleared = s.sem("heads_kept"), s.sem("v_cleared")
        rec_ready, waited = s.sem("rec_ready"), s.sem("waited")

        LOADED = 16 * (4 + (4 if rope else 0) + (4 if biased else 0))
        PREPARED = 3 + (1 if biased else 0) + (3 if causal else 0)

        if rope:
            early = [(1, "HT"), (2, "Q"), (3, "QS"), (4, "K"), (5, "KS"), (7, "V")]
        else:
            early = [(1, "HT"), (2, "Q"), (3, "K"), (5, "V")]
        uses = early + [(8 * t + 6, ("MAX", t + 1)) for t in range(4)]
        uses += [(8 * t + 10 + k, (what, t)) for t in range(3) for k, what in enumerate(("HEADS", "OT", "Y"))]
        uses = sorted(uses, key=lambda e: e[0]) + [(UNITS, ("HEADS", 3)), (UNITS, ("OT", 3)), (UNITS, ("Y", 3))]
        NM = len(uses)
        first = [e for e in uses if e[1] in [x[1] for x in early] or e[1] == ("MAX", 4)]
        NF = len(first)

        def at(b, n, c):
            return (b + 1) * n + c

        def steps(b, prologue):
            if prologue:
                return [(u, what, NM - NF + j) for j, (u, what) in enumerate(first)]
            return [(u, what, j) for j, (u, what) in enumerate(uses)]

        units = range(UNITS + 1)
        W = [P * (t + 1) if causal else T for t in range(TPS)]

        def in_body(u, prologue):
            return u < UNITS and (not prologue or u + LEAD >= UNITS)

        def wait(eng, sem, value):
            if not isinstance(value, int) or value > 0:
                eng.wait_ge(sem, value)

        def pairs_of(body):
            def run(eng):
                body(eng, -1, 1, True, -1)
                with eng.Fori(0, B // 2) as i:
                    body(eng, i * 2, 0, False, i)
                    body(eng, i * 2 + 1, 1, False, i)
            return run

        block = s.block()

        @block.sync
        def _(sp):
            names = [("q", "w_q"), ("k", "w_k"), ("v", "w_v"), ("out", "w_out")]
            names += [("q_swapped", "w_q_swapped"), ("k_swapped", "w_k_swapped")] if rope else []
            for n, (a, key) in enumerate(names):
                sp.dma_start(w[a][:, :], io[key]).then_inc(loaded, 16)
            if rope:
                sp.dma_start(cos[:, :], io["cos"]).then_inc(loaded, 16)
                sp.dma_start(sin[:, :], io["sin"]).then_inc(loaded, 16)
            if biased:
                for j, key in enumerate(("b_q", "b_k")):
                    sp.dma_start(bias_col[:, j:j + 1], io[key].unsqueeze(1)).then_inc(loaded, 16)
                for j, key in enumerate(("b_v", "b_out")):
                    sp.dma_start(bias_row[:, j, :], io[key].unsqueeze(0)).then_inc(loaded, 16)

            def body(sp, b, par, prologue, half):
                index = {what: j for _, what, j in steps(b, prologue)}

                def rows(t):
                    sp.wait_ge(misc_free, at(b, NM, index["MAX", t] + 1))
                    tt = t % 4
                    to = (par + 1) % 2 if t == 4 else par
                    for g in range(2):
                        sp.dma_start(QS[64 * g + ROWS:64 * g + ROWS + 1, to, :, tt * P:(tt + 1) * P],
                                     MT[g:H:2, tt % 2, :]).then_inc(shift_in[tt % 2], 16)
                if not prologue:
                    rows(1)
                to = (par + 1) % 2
                for j, done in enumerate((split_q, split_k)):
                    sp.wait_ge(done, b + 2)
                    sp.dma_start(parts_dram[to, j].rearrange("s p n -> p s n"), parts[:, j]).then_inc(parts_out, 16)
                if not prologue:
                    rows(2)
                sp.wait_ge(parts_out, (b + 2) * 32)
                sp.sem_inc(waited, 1)
                if not prologue:
                    sp.wait_ge(scores, at(b, UNITS, 0))
                def rows_of(x, g, s0, n):
                    return x[64 * g + s0 * D:64 * g + (s0 + n) * D, to, :, :].rearrange("r i n -> r (i n)")

                for g in range(2):
                    for s0, n, part in Q_SLOTS:
                        src = parts_dram[to, 0, part].rearrange("(g d i) n -> g d (i n)", g=2, d=D)[g]
                        sp.dma_start(rows_of(QS, g, s0, n), src.unsqueeze(0).to_broadcast([n, D, PAIRS * T]))\
                          .then_inc(qk_in[to], 16)
                    for s0, n in K_SLOTS:
                        src = parts_dram[to, 1, 0:n].rearrange("k (g d i) n -> g k d (i n)", g=2, d=D)[g]
                        sp.dma_start(rows_of(KS, g, s0, n), src).then_inc(qk_in[to], 16)
                if not prologue:
                    rows(3)
                rows(4)

            for sem in shift_in:
                sp.sem_inc(sem, 32)
            sp.wait_ge(prepared, PREPARED)
            pairs_of(body)(sp)
            sp.wait_ge(shift_in[0], 32 * (2 * B + 2))
            sp.wait_ge(shift_in[1], 32 * (2 * B + 1))
            sp.wait_ge(qk_in[0], 16 * ROW_LOADS * (B // 2 + 1))

        @block.gpsimd
        def _(pool):
            nc.gpsimd.memset(KS[:, :, :, :], 1.0).then_inc(prepared, 1)
            nc.gpsimd.memset(V[:, :, :, :, :], 0.0).then_inc(v_cleared, 1)
            pool.wait_ge(v_cleared, 1)
            nc.gpsimd.memset(V[:, :, :, :, D], 1.0).then_inc(prepared, 1)
            if biased:
                nc.gpsimd.memset(ones_row[:, :], 1.0).then_inc(prepared, 1)
            if causal:
                nc.gpsimd.memset(mask_qk[:, :], 0.0).then_inc(split_step, 1)
                nc.gpsimd.memset(mask_kq[:, :], 0.0).then_inc(split_step, 1)
                pool.wait_ge(split_step, 2)
                nc.gpsimd.affine_select(out=mask_qk[:, :], in_=mask_qk[:, :], compare_op=ALU.is_ge, fill=MASKED,
                                        base=0, pattern=[[-1, P]], channel_multiplier=1).then_inc(prepared, 1)
                nc.gpsimd.affine_select(out=mask_kq[:, :], in_=mask_kq[:, :], compare_op=ALU.is_ge, fill=MASKED,
                                        base=0, pattern=[[1, P]], channel_multiplier=-1).then_inc(prepared, 1)
                nc.gpsimd.tensor_copy(ident16[:, :], identity[:, :]).then_inc(prepared, 1)
            step0 = 2 if causal else 0
            pool.wait_ge(loaded, LOADED)

            def body(pool, b, par, prologue, half):
                index = {what: j for _, what, j in steps(b, prologue)}
                NS = 10 if rope else 6
                count = [step0]

                def chained(ins):
                    count[0] += 1
                    ins.then_inc(split_step, 1)
                    pool.wait_ge(split_step, (b + 1) * NS + count[0])
                    pool.sem_inc(waited, 1)

                for j, (raw, swapped, done) in enumerate((("Q", "QS", split_q), ("K", "KS", split_k))):
                    pool.wait_ge(misc_free, at(b, NM, index[swapped if rope else raw] + 1))
                    v = qk[:, j]
                    if rope:
                        chained(nc.gpsimd.tensor_tensor(v, v, cos[:, :], ALU.mult))
                        nc.gpsimd.tensor_tensor(rot[:, j], rot[:, j], sin[:, :], ALU.mult).then_inc(rotated, 1)
                        pool.wait_ge(rotated, (b + 1) * 2 + j + 1)
                        chained(nc.gpsimd.tensor_tensor(v, v, rot[:, j], ALU.add))
                    if not prologue:
                        pool.wait_ge(parts_out, (b + 1) * 32)
                        pool.sem_inc(waited, 1)
                    chained(nc.gpsimd.tensor_copy(parts[:, j, 0], v))
                    chained(nc.gpsimd.tensor_tensor(rest[:, j], v, parts[:, j, 0], ALU.subtract))
                    chained(nc.gpsimd.tensor_copy(parts[:, j, 1], rest[:, j]))
                    nc.gpsimd.tensor_tensor(parts[:, j, 2], rest[:, j], parts[:, j, 1], ALU.subtract)\
                        .then_inc(done, 1)

            pairs_of(body)(pool)

        @block.tensor
        def _(pe):
            pe.sem_inc(misc_full, NM - NF)
            pe.sem_inc(max_scores, 2 * (UNITS - LEAD))
            pe.sem_inc(scores, UNITS)
            pe.sem_inc(pv_done, UNITS)
            pe.wait_ge(loaded, LOADED)
            pe.wait_ge(prepared, PREPARED)

            def pv(b, par, u):
                t, i = u // PAIRS, u % PAIRS
                pe.wait_ge(exp_done, at(b, UNITS, u + 1))
                if i == 0:
                    pe.wait_ge(heads_kept, at(b, TPS, t))
                for g in range(2):
                    h = 2 * i + g
                    strip = slice(STRIP * (h % 4), STRIP * (h % 4 + 1))
                    nk = t + 1 if causal else TPS
                    for kb in range(nk):
                        last = nc.tensor.matmul(out_bank[strip, h // 4, :], V[:, par, kb, h, :],
                                                probs[:, u % 2, g, kb * P:(kb + 1) * P],
                                                start=(kb == 0), stop=(kb == nk - 1))
                last.then_inc(pv_done, 1)

            def body(pe, b, par, prologue, half):
                to = (par + 1) % 2
                uses_at = {}
                for u, what, j in steps(b, prologue):
                    uses_at.setdefault(u, []).append((what, j))

                def misc_use(what, j):
                    if not (prologue and what == "HT"):
                        pe.wait_ge(misc_free, at(b, NM, j))
                    if what == "HT":
                        pe.wait_ge(hn_ready, b + 2)
                        for t in range(TPS):
                            last = nc.tensor.transpose(misc[:, t * P:(t + 1) * P], hn[:, t, :], identity[:, :])
                    elif what in ("Q", "K", "QS", "KS"):
                        name = {"Q": "q", "K": "k", "QS": "q_swapped", "KS": "k_swapped"}[what]
                        last = nc.tensor.matmul(misc[:, :], w[name][:, :], hT[:, :], start=True, stop=True)
                    elif what == "V":
                        for t in range(TPS):
                            o = misc[:, t * P:(t + 1) * P]
                            last = nc.tensor.matmul(o, hT[:, t * P:(t + 1) * P], w["v"][:, :],
                                                    start=True, stop=not biased)
                            if biased:
                                last = nc.tensor.matmul(o, ones_row[:, :], bias_row[:, 0, :], start=False, stop=True)
                    elif what[0] == "MAX":
                        tt = what[1] % 4
                        pe.wait_ge(max_done, at(b, 2 * UNITS, 2 * u))
                        last = nc.tensor.transpose(misc[0:H, 0:P], M[:, tt % 2, :], identity[:, :])
                    elif what[0] == "HEADS":
                        pe.wait_ge(heads_kept, at(b, TPS, what[1] + 1))
                        for k in range(H // 4):
                            last = nc.tensor.transpose(misc[:, k * P:(k + 1) * P], heads_out[:, k * P:(k + 1) * P],
                                                       identity[:, :])
                    elif what[0] == "OT":
                        last = nc.tensor.transpose(misc[:, 0:P], on[:, :], identity[:, :])
                    else:
                        last = nc.tensor.matmul(misc[:, 0:C], oT[:, :], w["out"][:, :], start=True, stop=not biased)
                        if biased:
                            last = nc.tensor.matmul(misc[:, 0:C], ones_row[:, :], bias_row[:, 1, :],
                                                    start=False, stop=True)
                    last.then_inc(misc_full, 1)

                for u in units:
                    if u == UNITS and not prologue:
                        pv(b, par, UNITS - 1)
                    for what, j in uses_at.get(u, []):
                        misc_use(what, j)
                    if in_body(u, prologue):
                        n = u + LEAD
                        pb = to if n >= UNITS else par
                        t, i = (n % UNITS) // PAIRS, n % PAIRS
                        if n == UNITS:
                            pe.wait_ge(qk_in[pb], 16 * ROW_LOADS * (half + (par + 1) // 2 + 1))
                        for g in range(2):
                            if not (prologue and u + LEAD == UNITS):
                                pe.wait_ge(max_done, at(b, 2 * UNITS, 2 * u + g - 1))
                            last = nc.tensor.matmul(max_bank[:, g, 0:W[t]],
                                                    QS[64 * g:64 * g + ROWS, pb, i, t * P:(t + 1) * P],
                                                    KS[64 * g:64 * g + ROWS, pb, i, 0:W[t]],
                                                    start=True, stop=True)
                            if causal:
                                last = nc.tensor.matmul(max_bank[:, g, t * P:(t + 1) * P], ident16[:, :],
                                                        mask_qk[:, :], start=False, stop=True, skip_group_check=True)
                            last.then_inc(max_scores, 1)
                    if u < UNITS and not prologue:
                        t, i = u // PAIRS, u % PAIRS
                        if i == 0:
                            pe.wait_ge(shift_in[t % 2], 32 * (2 * b + t // 2 + 2))
                        pe.wait_ge(exp_done, at(b, UNITS, u - 1))
                        for g in range(2):
                            nk = t + 1 if causal else TPS
                            for kb in range(nk):
                                diagonal = causal and kb == t
                                o = exp_bank[:, u % 2, g, kb * P:(kb + 1) * P]
                                last = nc.tensor.matmul(o, KS[64 * g:64 * g + ROWS + 1, par, i, kb * P:(kb + 1) * P],
                                                        QS[64 * g:64 * g + ROWS + 1, par, i, t * P:(t + 1) * P],
                                                        start=True, stop=not diagonal)
                                if diagonal:
                                    last = nc.tensor.matmul(o, ident16[:, :], mask_kq[:, :], start=False, stop=True)
                        last.then_inc(scores, 1)
                        if u >= 1:
                            pv(b, par, u - 1)

            pairs_of(body)(pe)

        @block.scalar
        def _(act):
            act.sem_inc(misc_free, NM - NF)
            act.sem_inc(exp_done, UNITS)
            act.sem_inc(heads_kept, TPS)
            if biased:
                act.wait_ge(loaded, LOADED)

            def keep_heads(b, t):
                act.wait_ge(pv_done, at(b, UNITS, (t + 1) * PAIRS))
                nc.scalar.activation(heads_out[:, :], out_bank[:, :, :].rearrange("p k n -> p (k n)"), ACT.Copy)\
                    .then_inc(heads_kept, 1)

            def body(act, b, par, prologue, half):
                to = (par + 1) % 2
                for u in units:
                    if not prologue and (u == UNITS or u % PAIRS == 1 and u > 1):
                        keep_heads(b, (u - 1) // PAIRS - (u != UNITS))
                    for _, what, j in [e for e in steps(b, prologue) if e[0] == u]:
                        if what in ("HT", "Q", "K", "QS", "KS", "V") or what[0] in ("MAX", "OT"):
                            act.wait_ge(misc_full, at(b, NM, j + 1))
                        if what == "HT":
                            nc.scalar.activation(hT[:, :], misc[:, :], ACT.Copy).then_inc(misc_free, 1)
                        elif what in ("Q", "K", "QS", "KS"):
                            side = 0 if what[0] == "Q" else 1
                            if not prologue:
                                act.wait_ge((split_q, split_k)[side], b + 1)
                            dst = qk[:, side] if len(what) == 1 else rot[:, side]
                            if biased:
                                nc.scalar.activation(dst, misc[:, :], ACT.Identity,
                                                     bias=bias_col[:, side:side + 1]).then_inc(misc_free, 1)
                            else:
                                nc.scalar.activation(dst, misc[:, :], ACT.Copy).then_inc(misc_free, 1)
                        elif what == "V":
                            if prologue:
                                act.wait_ge(prepared, PREPARED)
                            nc.scalar.activation(V[:, to, :, :, 0:D],
                                                 misc[:, :].rearrange("p (t h d) -> p t h d", t=TPS, d=D),
                                                 ACT.Copy).then_inc(misc_free, 1)
                        elif what[0] == "MAX":
                            tt = what[1] % 4
                            nb = b + 1 if what[1] == 4 else b
                            if not prologue:
                                act.wait_ge(shift_in[tt % 2], 32 * (2 * nb + tt // 2 + 1))
                            nc.scalar.activation(MT[:, tt % 2, :], misc[0:H, 0:P], ACT.Copy, scale=-1.0)\
                                .then_inc(misc_free, 1)
                        elif what[0] == "OT":
                            nc.scalar.activation(oT[:, :], misc[:, 0:P], ACT.Copy).then_inc(misc_free, 1)
                    if u < UNITS and not prologue:
                        t = u // PAIRS
                        act.wait_ge(scores, at(b, UNITS, u + 1))
                        act.wait_ge(pv_done, at(b, UNITS, u - 1))
                        nc.scalar.activation(probs[:, u % 2, :, 0:W[t]], exp_bank[:, u % 2, :, 0:W[t]], ACT.Exp,
                                             scale=float(D) ** -0.5).then_inc(exp_done, 1)

            pairs_of(body)(act)

        @block.vector
        def _(dve):
            nc.vector.memset(QS[:, :, :, :], 0.0).then_inc(prepared, 1)
            dve.sem_inc(max_done, 2 * (UNITS - LEAD))

            def layernorm(b):
                tokens, moments = X[:, bass.ds(b * TPS, TPS), :], stats[:, bass.ds(b * TPS, TPS), :]
                for t in range(TPS):
                    last = nc.vector.tensor_scalar(hn[:, t, :], tokens[:, t, :], moments[:, t:t + 1, 0],
                                                   moments[:, t:t + 1, 1], ALU.subtract, ALU.mult)
                last.then_inc(hn_ready, 1)

            def normalise(b, t):
                heads = misc[:, :].rearrange("p (h d) -> p h d", d=STRIP)
                nc.vector.reciprocal(rec[:, :], heads[:, :, D]).then_inc(rec_ready, 1)
                dve.wait_ge(rec_ready, b * TPS + t + 1)
                nc.vector.tensor_tensor(on[:, :].rearrange("p (h d) -> p h d", d=D), heads[:, :, 0:D],
                                        rec[:, :].unsqueeze(2).to_broadcast([P, H, D]), ALU.mult)\
                    .then_inc(misc_free, 1)

            def body(dve, b, par, prologue, half):
                for u in units:
                    if u == PAIRS + 4:
                        dve.wait_ge(misc_full, at(b, NM, steps(b, prologue)[0][2] + 1))
                        layernorm(b + 2)
                    for _, what, j in [e for e in steps(b, prologue) if e[0] == u]:
                        if what[0] == "HEADS":
                            dve.wait_ge(misc_full, at(b, NM, j + 1))
                            normalise(b, what[1])
                        if what[0] == "Y":
                            tile = bass.ds(b * TPS + what[1], 1)
                            dve.wait_ge(misc_full, at(b, NM, j + 1))
                            x = X[:, tile, :].rearrange("p o c -> p (o c)")
                            nc.vector.tensor_tensor(x, x, misc[:, 0:C], ALU.add).then_inc(misc_free, 1)
                    if in_body(u, prologue):
                        n = (u + LEAD) % UNITS
                        t, i = n // PAIRS, n % PAIRS
                        for g in range(2):
                            dve.wait_ge(max_scores, at(b, 2 * UNITS, 2 * u + g + 1))
                            nc.vector.reduce_max(M[:, t % 2, 2 * i + g:2 * i + g + 1], max_bank[:, g, 0:W[t]], AX.X)\
                                .then_inc(max_done, 1)

            layernorm(0)
            pairs_of(body)(dve)


E, FF = 8, 512
FC = FF // P
SORTED = NT + E
SPARE = 4
FIRST_MIXTURE = 1
B1_AT = 2 * FF


def tile_of(x, tile):
    return x[:, bass.ds(tile, 1), :].rearrange("p o c -> p (o c)")


def mixture(nc, tag, io, X, stats, identity, sorted_in, sorted_out, first):
    with Stage(nc, tag) as s:
        w_router, b_router = s.sb("w_router", [P, E]), s.sb("b_router", [P, E])
        experts = s.sb("experts", [P, E, B1_AT + FC])
        b2 = s.sb("b2", [1, E, C])
        ones_row = s.sb("ones_row", [1, P])
        hn, hT = s.sb("hn", [P, 2, TPS, C]), s.sb("hT", [P, 2, T])
        L = s.sb("L", [P, NT, E])
        top, total, gate = s.sb("top", [P, NT]), s.sb("total", [P, NT]), s.sb("gate", [P, NT])
        ex = s.sb("ex", [P, NT, E])
        chosen = s.sb("chosen", [P, NT, E], BF16)
        iota_e, iota_k = s.sb("iota_e", [P, E]), s.sb("iota_k", [P, SORTED + SPARE])
        before, ones16 = s.sb("before", [P, P], BF16), s.sb("ones16", [P, P], BF16)
        upto = s.sb("upto", [P, E, E])
        tile_counts = s.sb("tile_counts", [NT, E], BF16)
        earlier = s.sb("earlier", [NT, NT, E], BF16)
        n_int, n_tiles = s.sb("n_int", [P, E], mybir.dt.int32), s.sb("n_tiles", [P, E])
        ends_by = s.sb("ends_by", [P, E, E])
        ends, base = s.sb("ends", [P, E]), s.sb("base", [P, E])
        place = s.sb("place", [P, NT])
        place_int = s.sb("place_int", [P, NT + 2 * TPS], mybir.dt.int32)
        past = s.sb("past", [1, SORTED + SPARE, E])
        expert_of = s.sb("expert_of", [1, SORTED + SPARE])
        expert_int = s.sb("expert_int", [1, SORTED + SPARE], mybir.dt.int32)
        index = s.sb("index", [P, 2, TPS], mybir.dt.int32)
        rows = s.sb("rows", [P, 4, C])
        rowsT = s.sb("rowsT", [P, 2, P])
        own = s.sb("own", [P, 4, B1_AT + FC])
        own_b2 = s.sb("own_b2", [1, 4, C])
        hidden = s.sb("hidden", [P, 2, FC, P])
        result = s.sb("result", [P, 4, C])
        back = s.sb("back", [P, 2, TPS, C])
        zeros = s.sb("zeros", [P, C])

        t_bank = s.ps("t_bank", [P, 2, T])
        small_bank = s.ps("small_bank", [P, 2, T])
        up_bank = s.ps("up_bank", [P, 2, T])
        down_bank = s.ps("down_bank", [P, 2, T])

        router_loaded, loaded = s.sem("router_loaded"), s.sem("experts_loaded")
        made = s.sem("constants_made")
        hn_ready, turned, hT_ready = s.sem("hn_ready"), s.sem("turned"), s.sem("hT_ready")
        logits_done, logits_kept = s.sem("logits_done"), s.sem("logits_kept")
        step, shifted_ready, exp_ready = s.sem("step"), s.sem("shifted_ready"), s.sem("exp_ready")
        chosen_ready, counts_done, counts_kept = s.sem("chosen_ready"), s.sem("counts_done"), s.sem("counts_kept")
        places_done, places_kept = s.sem("places_done"), s.sem("places_kept")
        scatter_ready = s.sem("scatter_ready")
        rows_in = [s.sem(f"rows_in{n}") for n in range(4)]
        rows_turned, rowsT_ready = s.sem("rows_turned"), s.sem("rowsT_ready")
        own_ready, up_done, gelu_done = s.sem("own_ready"), s.sem("up_done"), s.sem("gelu_done")
        down_done, result_ready = s.sem("down_done"), s.sem("result_ready")
        stored = [s.sem(f"stored{n}") for n in range(4)]
        index_ready, added = s.sem("index_ready"), s.sem("added")
        cleared, zeroed = s.sem("zeros_made"), s.sem("rows_zeroed")
        scattered = [nc.alloc_semaphore(f"{tag}_scattered{n}") for n in range(2)]
        gathered = [nc.alloc_semaphore(f"{tag}_gathered{n}") for n in range(2)]
        waited = s.sem("waited")

        LOADED = 16 * (3 + E)
        MADE = 11
        block = s.block()

        @block.sync
        def _(sp):
            sp.dma_start(w_router[:, :], io["w_router"]).then_inc(router_loaded, 16)
            sp.dma_start(b_router[:, :], io["b_router"].partition_broadcast(P)).then_inc(router_loaded, 16)
            if first:
                sp.wait_ge(cleared, 1)
                n = sorted_in.shape[0] // 4
                for k in range(0, sorted_in.shape[0], n):
                    sp.dma_start(sorted_in[k:k + n].rearrange("k p c -> p k c"),
                                 zeros[:, :].unsqueeze(1).to_broadcast([P, n, C])).then_inc(zeroed, 16)
            sp.dma_start(experts[:, :, 0:FF], io["w1"].rearrange("e c f -> c e f")).then_inc(loaded, 16)
            for e in range(E):
                sp.dma_start(experts[:, e, FF:2 * FF].rearrange("p (q c) -> p q c", q=FC),
                             io["w2"][e].rearrange("(q p) c -> p q c", p=P)).then_inc(loaded, 16)
            sp.dma_start(experts[:, :, B1_AT:], io["b1"]).then_inc(loaded, 16)
            sp.dma_start(b2[:, :, :], io["b2"].unsqueeze(0)).then_inc(loaded, 16)
            for n in range(4):
                sp.sem_inc(stored[n], 16)
            for n in range(2):
                sp.wait_ge(scattered[n], 16 * TPS * (B // 2))

            def load(k, n):
                sp.dma_start(rows[:, n, :], sorted_in[bass.ds(k, 1)].rearrange("o p c -> p (o c)"))\
                  .then_inc(rows_in[n], 16)
            for n in range(4):
                load(n, n)
            with sp.Fori(0, SORTED // 4) as i:
                for n in range(4):
                    k = i * 4 + n
                    sp.wait_ge(rows_turned, k + 1)
                    load(k + 4, n)
                    sp.wait_ge(result_ready, k + 3)
                    sp.dma_start(sorted_out[bass.ds(k, 1)].rearrange("o p c -> p (o c)"), result[:, n, :])\
                      .then_inc(stored[n], 16)
            for n in range(4):
                sp.wait_ge(rows_in[n], 16 * (SORTED // 4 + 1))

        @block.gpsimd
        def _(pool):
            g = nc.gpsimd
            if first:
                g.memset(zeros[:, :], 0.0).then_inc(cleared, 1)
            g.iota(iota_e[:, :], pattern=[[1, E]], base=0, channel_multiplier=0,
                   allow_small_or_imprecise_dtypes=True).then_inc(made, 1)
            g.iota(iota_k[:, :], pattern=[[1, SORTED + SPARE]], base=0, channel_multiplier=0,
                   allow_small_or_imprecise_dtypes=True).then_inc(made, 1)
            g.memset(ones16[:, :], 1.0).then_inc(made, 1)
            g.memset(before[:, :], 1.0).then_inc(made, 1)
            g.memset(upto[:, :, :], 1.0).then_inc(made, 1)
            g.memset(earlier[:, :, :], 1.0).then_inc(made, 1)
            g.memset(ones_row[:, :], 1.0).then_inc(made, 1)
            g.memset(place_int[:, NT:], 0).then_inc(made, 1)
            pool.wait_ge(made, 8)
            g.affine_select(out=before[:, :], in_=before[:, :], compare_op=ALU.is_gt, fill=0.0, base=0,
                            pattern=[[1, P]], channel_multiplier=-1).then_inc(made, 1)
            g.affine_select(out=upto[:, :, :], in_=upto[:, :, :], compare_op=ALU.is_ge, fill=0.0, base=0,
                            pattern=[[1, E], [-1, E]], channel_multiplier=0).then_inc(made, 1)
            g.affine_select(out=earlier[:, :, :], in_=earlier[:, :, :], compare_op=ALU.is_gt, fill=0.0, base=0,
                            pattern=[[1, NT], [0, E]], channel_multiplier=-1).then_inc(made, 1)
            if first:
                pool.wait_ge(zeroed, 64)
            with pool.Fori(0, B // 2) as i:
                for n in range(2):
                    pool.wait_ge(scatter_ready, i * 2 + n + 1)
                    pool.sem_inc(waited, 1)
                    for t in range(TPS):
                        g.indirect_dma_start(out=sorted_in.rearrange("k p c -> (k p) c"),
                                             out_offset=bass.IndirectOffsetOnAxis(ap=index[:, n, t:t + 1], axis=0),
                                             in_=hn[:, n, t, :], in_offset=None).then_inc(scattered[n], 16)
            for n in range(4):
                pool.wait_ge(stored[n], 16 * (SORTED // 4 + 1))
            with pool.Fori(0, B // 2) as i:
                for n in range(2):
                    pool.wait_ge(index_ready, i * 2 + n + 1)
                    pool.sem_inc(waited, 1)
                    pool.wait_ge(added, i * 2 + n + 1)
                    pool.sem_inc(waited, 1)
                    for t in range(TPS):
                        g.indirect_dma_start(out=back[:, n, t, :], out_offset=None,
                                             in_=sorted_out.rearrange("k p c -> (k p) c"),
                                             in_offset=bass.IndirectOffsetOnAxis(ap=index[:, n, t:t + 1], axis=0))\
                         .then_inc(gathered[n], 16)

        @block.tensor
        def _(pe):
            pe.wait_ge(router_loaded, 32)
            pe.wait_ge(made, MADE)
            pe.sem_inc(turned, 1)
            pe.sem_inc(down_done, 2)
            with pe.Fori(0, B // 2) as i:
                for n in range(2):
                    b = i * 2 + n
                    pe.wait_ge(hn_ready, b + 1)
                    pe.wait_ge(hT_ready, b + 1)
                    for t in range(TPS):
                        last = nc.tensor.transpose(t_bank[:, n, t * P:(t + 1) * P], hn[:, n, t, :], identity[:, :])
                    last.then_inc(turned, 1)
                    pe.wait_ge(hT_ready, b + 3)
                    pe.wait_ge(logits_kept, b + 1)
                    for t in range(TPS):
                        last = nc.tensor.matmul(small_bank[:, n, t * E:(t + 1) * E], hT[:, n, t * P:(t + 1) * P],
                                                w_router[:, :], start=True, stop=True)
                    last.then_inc(logits_done, 1)
            pe.wait_ge(chosen_ready, 1)
            for e in range(E):
                last = nc.tensor.matmul(small_bank[0:NT, 0, e:e + 1], chosen[:, :, e], ones16[:, 0:1],
                                        start=True, stop=True)
            last.then_inc(counts_done, 1)
            pe.wait_ge(counts_kept, 1)
            nc.tensor.matmul(t_bank[:, 0, :], before[:, :], chosen[:, :, :].rearrange("p t e -> p (t e)"),
                             start=True, stop=False)
            nc.tensor.matmul(t_bank[:, 0, :], ones16[0:NT, :], earlier[:, :, :].rearrange("p t e -> p (t e)"),
                             start=False, stop=True)
            nc.tensor.matmul(small_bank[:, 1, 0:E], ones16[0:NT, :], tile_counts[:, :], start=True, stop=True)\
              .then_inc(places_done, 1)

            def turn(k, n4, n2):
                pe.wait_ge(rows_in[n4], 16 * (k[0] + k[1] + 1))
                nc.tensor.transpose(t_bank[:, n2, 0:P], rows[:, n4, :], identity[:, :]).then_inc(rows_turned, 1)

            def up(n4, n2):
                for f in range(FC):
                    last = nc.tensor.matmul(up_bank[:, n2, f * P:(f + 1) * P], own[:, n4, f * P:(f + 1) * P],
                                            rowsT[:, n2, :], start=True, stop=True)
                last.then_inc(up_done, 1)

            def down(n4, n2):
                for f in range(FC):
                    nc.tensor.matmul(down_bank[:, n2, 0:C], hidden[:, n2, f, :],
                                     own[:, n4, FF + f * C:FF + (f + 1) * C], start=(f == 0), stop=False)
                nc.tensor.matmul(down_bank[:, n2, 0:C], ones_row[:, :], own_b2[:, n4, :], start=False, stop=True)\
                  .then_inc(down_done, 1)

            pe.wait_ge(places_kept, 1)
            turn((0, 0), 0, 0)
            turn((0, 0), 1, 1)
            pe.wait_ge(rowsT_ready, 1)
            pe.wait_ge(own_ready, 1)
            up(0, 0)
            with pe.Fori(0, SORTED // 4) as i:
                for n in range(4):
                    k = i * 4 + n
                    pe.wait_ge(rowsT_ready, k + 2)
                    turn((i, (n + 2) // 4), (n + 2) % 4, n % 2)
                    pe.wait_ge(own_ready, k + 2)
                    pe.wait_ge(gelu_done, k + 1)
                    up((n + 1) % 4, (n + 1) % 2)
                    pe.wait_ge(gelu_done, k + 2)
                    pe.wait_ge(result_ready, k + 1)
                    down(n, n % 2)

        @block.scalar
        def _(act):
            act.sem_inc(hT_ready, 2)
            act.sem_inc(gelu_done, 1)
            with act.Fori(0, B // 2) as i:
                for n in range(2):
                    b = i * 2 + n
                    act.wait_ge(turned, b + 2)
                    act.wait_ge(logits_kept, b + 1)
                    nc.scalar.activation(hT[:, n, :], t_bank[:, n, :], ACT.Copy).then_inc(hT_ready, 1)
            act.wait_ge(shifted_ready, 1)
            nc.scalar.activation(ex[:, :, :], L[:, :, :], ACT.Exp).then_inc(exp_ready, 1)

            def turned_rows(n2):
                nc.scalar.activation(rowsT[:, n2, :], t_bank[:, n2, 0:P], ACT.Copy).then_inc(rowsT_ready, 1)

            def gelu(n4, n2):
                for f in range(FC):
                    last = nc.scalar.activation(hidden[:, n2, f, :], up_bank[:, n2, f * P:(f + 1) * P], ACT.Gelu,
                                                bias=own[:, n4, B1_AT + f:B1_AT + f + 1])
                last.then_inc(gelu_done, 1)

            for n in range(2):
                act.wait_ge(rows_turned, n + 1)
                turned_rows(n)
            act.wait_ge(up_done, 1)
            gelu(0, 0)
            with act.Fori(0, SORTED // 4) as i:
                for n in range(4):
                    k = i * 4 + n
                    act.wait_ge(rows_turned, k + 3)
                    act.wait_ge(up_done, k + 1)
                    turned_rows(n % 2)
                    act.wait_ge(up_done, k + 2)
                    act.wait_ge(down_done, k + 2)
                    gelu((n + 1) % 4, (n + 1) % 2)

        @block.vector
        def _(dve):
            v = nc.vector
            dve.sem_inc(logits_kept, 2)
            dve.sem_inc(result_ready, 2)
            dve.sem_inc(added, 2)

            def normalise(b, n, done):
                tokens, moments = X[:, bass.ds(b * TPS, TPS), :], stats[:, bass.ds(b * TPS, TPS), :]
                for t in range(TPS):
                    last = v.tensor_scalar(hn[:, n, t, :], tokens[:, t, :], moments[:, t:t + 1, 0],
                                           moments[:, t:t + 1, 1], ALU.subtract, ALU.mult)
                last.then_inc(done, 1)

            dve.wait_ge(router_loaded, 32)
            dve.wait_ge(made, MADE)

            normalise(0, 0, hn_ready)
            with dve.Fori(0, B // 2) as i:
                for n in range(2):
                    b = i * 2 + n
                    dve.wait_ge(turned, b + 1)
                    normalise(b + 1, (n + 1) % 2, hn_ready)
                    dve.wait_ge(logits_done, b + 1)
                    v.tensor_tensor(L[:, bass.ds(b * TPS, TPS), :],
                                    small_bank[:, n, 0:TPS * E].rearrange("p (t e) -> p t e", e=E),
                                    b_router[:, :].unsqueeze(1).to_broadcast([P, TPS, E]), ALU.add)\
                     .then_inc(logits_kept, 1)
            dve.wait_ge(logits_kept, B + 2)

            count = [0]

            def chained(ins):
                count[0] += 1
                ins.then_inc(step, 1)
                dve.wait_ge(step, count[0])

            def over_tiles(x):
                return x.unsqueeze(1).to_broadcast([P, NT, E])

            def over_experts(x):
                return x.unsqueeze(2).to_broadcast([P, NT, E])

            chained(v.reduce_max(top[:, :], L[:, :, :], AX.X))
            v.tensor_tensor(L[:, :, :], L[:, :, :], over_experts(top[:, :]), ALU.subtract).then_inc(shifted_ready, 1)
            dve.wait_ge(shifted_ready, 1)
            dve.wait_ge(exp_ready, 1)
            chained(v.reduce_sum(total[:, :], ex[:, :, :], AX.X))
            chained(v.tensor_scalar(ex[:, :, :], L[:, :, :], 0.0, -float(E), ALU.is_equal, ALU.mult))
            v.reciprocal(gate[:, :], total[:, :])
            chained(v.tensor_tensor(ex[:, :, :], ex[:, :, :], over_tiles(iota_e[:, :]), ALU.add))
            chained(v.tensor_reduce(top[:, :], ex[:, :, :], AX.X, ALU.min))
            v.tensor_tensor(chosen[:, :, :], ex[:, :, :], over_experts(top[:, :]), ALU.is_equal)\
             .then_inc(chosen_ready, 1)
            dve.wait_ge(counts_done, 1)
            chained(v.tensor_copy(tile_counts[:, :], small_bank[0:NT, 0, 0:E]))
            v.tensor_tensor(earlier[:, :, :], earlier[:, :, :],
                            tile_counts[:, :].unsqueeze(1).to_broadcast([NT, NT, E]), ALU.mult)\
             .then_inc(counts_kept, 1)
            dve.wait_ge(places_done, 1)
            chained(v.tensor_scalar(n_int[:, :], small_bank[:, 1, 0:E], float(P - 1), None, ALU.add))
            chained(v.tensor_scalar(n_int[:, :], n_int[:, :], 7, None, ALU.arith_shift_right))
            chained(v.tensor_copy(n_tiles[:, :], n_int[:, :]))
            chained(v.tensor_tensor(ends_by[:, :, :], upto[:, :, :],
                                    n_tiles[:, :].unsqueeze(1).to_broadcast([P, E, E]), ALU.mult))
            chained(v.reduce_sum(ends[:, :], ends_by[:, :, :], AX.X))
            chained(v.tensor_tensor(base[:, :], ends[:, :], n_tiles[:, :], ALU.subtract))
            chained(v.tensor_scalar(base[:, :], base[:, :], float(P), None, ALU.mult))
            v.tensor_tensor(ex[:, :, :], t_bank[:, 0, :].rearrange("p (t e) -> p t e", e=E),
                            over_tiles(base[:, :]), ALU.add).then_inc(places_kept, 1)
            dve.wait_ge(places_kept, 1)
            chained(v.tensor_tensor(ex[:, :, :], ex[:, :, :], chosen[:, :, :], ALU.mult))
            chained(v.reduce_sum(place[:, :], ex[:, :, :], AX.X))
            chained(v.tensor_copy(place_int[:, 0:NT], place[:, :]))
            nk = SORTED + SPARE
            chained(v.tensor_tensor(past[:, :, :], iota_k[0:1, :].unsqueeze(2).to_broadcast([1, nk, E]),
                                    ends[0:1, :].unsqueeze(1).to_broadcast([1, nk, E]), ALU.is_ge))
            chained(v.reduce_sum(expert_of[:, :], past[:, :, :], AX.X))
            chained(v.tensor_scalar(expert_int[:, :], expert_of[:, :], float(E - 1), None, ALU.min))

            dve.wait_ge(turned, B + 1)
            def rows_and_places(b, n):
                v.tensor_copy(index[:, n, :], place_int[:, bass.ds(b * TPS, TPS)]).then_inc(step, 1)
                dve.wait_ge(step, b + 1 + count[0])
                normalise(b, n, scatter_ready)

            for n in range(2):
                rows_and_places(n, n)
            with dve.Fori(0, B // 2 - 1) as i:
                for n in range(2):
                    dve.wait_ge(scattered[n], (i + 1) * (16 * TPS))
                    rows_and_places(i * 2 + (n + 2), n)

            def fetch(k, n4):
                e = dve.value_load(expert_int[0:1, bass.ds(k, 1)], min_val=0, max_val=E - 1)
                v.tensor_copy(own[:, n4, :], tile_of(experts, e))
                v.tensor_copy(own_b2[:, n4, :], tile_of(b2, e)).then_inc(own_ready, 1)

            dve.wait_ge(loaded, LOADED)
            fetch(0, 0)
            fetch(1, 1)
            with dve.Fori(0, SORTED // 4) as i:
                for n in range(4):
                    k = i * 4 + n
                    dve.wait_ge(down_done, k + 1)
                    fetch(k + 2, (n + 2) % 4)
                    dve.wait_ge(down_done, k + 3)
                    dve.wait_ge(stored[n], 16 * (i + 1))
                    v.tensor_copy(result[:, n, :], down_bank[:, n % 2, 0:C]).then_inc(result_ready, 1)

            def place_of(b, n):
                v.tensor_copy(index[:, n, :], place_int[:, bass.ds(b * TPS, TPS)]).then_inc(index_ready, 1)

            for n in range(2):
                dve.wait_ge(scattered[n], 16 * TPS * (B // 2))
                place_of(n, n)
            with dve.Fori(0, B // 2) as i:
                for n in range(2):
                    b = i * 2 + n
                    dve.wait_ge(gathered[n], (i + 1) * (16 * TPS))
                    tokens, gates = X[:, bass.ds(b * TPS, TPS), :], gate[:, bass.ds(b * TPS, TPS)]
                    for t in range(TPS):
                        last = v.scalar_tensor_tensor(tokens[:, t, :], back[:, n, t, :], gates[:, t:t + 1],
                                                      tokens[:, t, :], ALU.mult, ALU.add)
                    last.then_inc(added, 1)
                    place_of(b + 2, n)


def channel_mix(nc, tag, io, X, stats, identity):
    with Stage(nc, tag) as s:
        w = {n: s.sb(f"w_{n}", [P, C]) for n in "rkv"}
        mu = s.sb("mu", [P, 2])
        hn = s.sb("hn", [P, 2, TPS, C])
        hT = s.sb("hT", [P, 2, 1 + T])
        diff = s.sb("diff", [P, 2, T])
        mix = s.sb("mix", [P, 2, 2, T])
        act_k = s.sb("act_k", [P, 2, T])
        squared = s.sb("squared", [P, 2, T])
        gate = s.sb("gate", [P, 2, T])
        product = s.sb("product", [P, 2, T])
        t_bank, k_bank = s.ps("t_bank", [P, 2, T]), s.ps("k_bank", [P, 2, T])
        r_bank, y_bank = s.ps("r_bank", [P, 2, T]), s.ps("y_bank", [P, 2, T])

        loaded, made = s.sem("weights_loaded"), s.sem("first_column_zero")
        hn_ready, turned, hT_ready = s.sem("hn_ready"), s.sem("turned_1"), s.sem("hT_ready_1")
        diff_ready, mixed = s.sem("diff_ready"), s.sem("mixed_2")
        k_done, relu_done, squares_ready = s.sem("k_done"), s.sem("relu_done_2"), s.sem("squares_ready")
        r_done, gate_ready = s.sem("r_done_2"), s.sem("gate_ready_2")
        y_done, product_ready, added = s.sem("y_done_2"), s.sem("product_ready"), s.sem("added_2")
        LOADED = 16 * 5
        block = s.block()

        @block.sync
        def _(sp):
            for n in "rkv":
                sp.dma_start(w[n][:, :], io[f"w_{n}"]).then_inc(loaded, 16)
            for j, n in enumerate("kr"):
                sp.dma_start(mu[:, j:j + 1], io[f"mu_{n}"].unsqueeze(1)).then_inc(loaded, 16)

        @block.gpsimd
        def _(pool):
            nc.gpsimd.memset(hT[:, :, 0:1], 0.0).then_inc(made, 1)
            pool.wait_ge(made, 1)
            with pool.Fori(0, B // 2) as i:
                for n in range(2):
                    b = i * 2 + n
                    pool.wait_ge(hT_ready, b + 2)
                    pool.wait_ge(mixed, b + 1)
                    nc.gpsimd.tensor_tensor(diff[:, n, :], hT[:, n, 1:1 + T], hT[:, n, 0:T], ALU.subtract)\
                      .then_inc(diff_ready, 1)

        @block.tensor
        def _(pe):
            pe.sem_inc(turned, 1)
            pe.sem_inc(r_done, 2)
            pe.sem_inc(y_done, 2)

            def turn(n):
                for t in range(TPS):
                    last = nc.tensor.transpose(t_bank[:, n, t * P:(t + 1) * P], hn[:, n, t, :], identity[:, :])
                last.then_inc(turned, 1)

            pe.wait_ge(loaded, LOADED)
            pe.wait_ge(hn_ready, 1)
            turn(0)
            with pe.Fori(0, B // 2) as i:
                for n in range(2):
                    b = i * 2 + n
                    pe.wait_ge(mixed, b + 3)
                    pe.wait_ge(relu_done, b + 1)
                    nc.tensor.matmul(k_bank[:, n, :], w["k"][:, :], mix[:, n, 0, :], start=True, stop=True)\
                      .then_inc(k_done, 1)
                    pe.wait_ge(gate_ready, b + 1)
                    for t in range(TPS):
                        last = nc.tensor.matmul(r_bank[:, n, t * P:(t + 1) * P], mix[:, n, 1, t * P:(t + 1) * P],
                                                w["r"][:, :], start=True, stop=True)
                    last.then_inc(r_done, 1)
                    pe.wait_ge(hn_ready, b + 2)
                    pe.wait_ge(hT_ready, b + 1)
                    turn((n + 1) % 2)
                    pe.wait_ge(squares_ready, b + 1)
                    pe.wait_ge(added, b + 1)
                    for t in range(TPS):
                        last = nc.tensor.matmul(y_bank[:, n, t * P:(t + 1) * P], squared[:, n, t * P:(t + 1) * P],
                                                w["v"][:, :], start=True, stop=True)
                    last.then_inc(y_done, 1)

        @block.scalar
        def _(act):
            act.sem_inc(hT_ready, 1)
            act.sem_inc(relu_done, 2)
            act.sem_inc(gate_ready, 2)
            act.wait_ge(turned, 2)
            nc.scalar.activation(hT[:, 0, 1:1 + T], t_bank[:, 0, :], ACT.Copy).then_inc(hT_ready, 1)
            with act.Fori(0, B // 2) as i:
                for n in range(2):
                    b = i * 2 + n
                    act.wait_ge(k_done, b + 1)
                    act.wait_ge(y_done, b + 1)
                    nc.scalar.activation(act_k[:, n, :], k_bank[:, n, :], ACT.Relu).then_inc(relu_done, 1)
                    act.wait_ge(relu_done, b + 3)
                    nc.scalar.activation(squared[:, n, :], act_k[:, n, :], ACT.Square).then_inc(squares_ready, 1)
                    act.wait_ge(r_done, b + 3)
                    act.wait_ge(added, b + 1)
                    nc.scalar.activation(gate[:, n, :], r_bank[:, n, :], ACT.Sigmoid).then_inc(gate_ready, 1)
                    act.wait_ge(turned, b + 3)
                    act.wait_ge(mixed, b + 2)
                    nc.scalar.activation(hT[:, (n + 1) % 2, 1:1 + T], t_bank[:, (n + 1) % 2, :], ACT.Copy)\
                      .then_inc(hT_ready, 1)

        @block.vector
        def _(dve):
            dve.sem_inc(mixed, 2)
            dve.sem_inc(added, 2)

            def normalise(b, n):
                tokens, moments = X[:, bass.ds(b * TPS, TPS), :], stats[:, bass.ds(b * TPS, TPS), :]
                for t in range(TPS):
                    last = nc.vector.tensor_scalar(hn[:, n, t, :], tokens[:, t, :], moments[:, t:t + 1, 0],
                                                   moments[:, t:t + 1, 1], ALU.subtract, ALU.mult)
                last.then_inc(hn_ready, 1)

            normalise(0, 0)
            dve.wait_ge(loaded, LOADED)
            with dve.Fori(0, B // 2) as i:
                for n in range(2):
                    b = i * 2 + n
                    dve.wait_ge(diff_ready, b + 1)
                    dve.wait_ge(r_done, b + 1)
                    for j in range(2):
                        last = nc.vector.scalar_tensor_tensor(mix[:, n, j, :], diff[:, n, :], mu[:, j:j + 1],
                                                              hT[:, n, 0:T], ALU.mult, ALU.add)
                    last.then_inc(mixed, 1)
                    dve.wait_ge(turned, b + 1)
                    normalise(b + 1, (n + 1) % 2)
                    dve.wait_ge(y_done, b + 3)
                    dve.wait_ge(gate_ready, b + 3)
                    nc.vector.tensor_tensor(product[:, n, :], gate[:, n, :], y_bank[:, n, :], ALU.mult)\
                      .then_inc(product_ready, 1)
                    dve.wait_ge(product_ready, b + 1)
                    x = X[:, bass.ds(b * TPS, TPS), :].rearrange("p t c -> p (t c)")
                    nc.vector.tensor_tensor(x, x, product[:, n, :], ALU.add).then_inc(added, 1)


QH, KVH, HD, WINDOW = 16, 4, 64, 64
REP = QH // KVH
NORMED = QH + KVH
RMS_EPS = 1e-6
G_UNITS = TPS * KVH
G_LEAD = KVH + 1
BAND = P + WINDOW


def window_attention(nc, tag, io, X, stats, identity):
    with Stage(nc, tag) as s:
        wq, wkv, wo = s.sb("wq", [P, QH * HD]), s.sb("wkv", [P, 2 * KVH * HD]), s.sb("wo", [P, 8, C])
        norm_w = s.sb("norm_w", [P, 2])
        ident16 = s.sb("ident16", [P, P], BF16)
        mask_qk = s.sb("mask_qk", [P, BAND], BF16)
        mask_kq = s.sb("mask_kq", [P, P], BF16)
        mask_prev = s.sb("mask_prev", [P, WINDOW], BF16)
        select = s.sb("select", [QH, QH, P], BF16)
        hn, hT = s.sb("hn", [P, TPS, C]), s.sb("hT", [P, T])
        raw = s.sb("raw", [P, 2, NORMED, HD])
        squares = s.sb("squares", [P, NORMED, HD])
        ssq, rms = s.sb("ssq", [P, NORMED]), s.sb("rms", [P, NORMED])
        minus_half = s.sb("minus_half", [P, NORMED])
        scaled = s.sb("scaled", [P, 2, NORMED, HD])
        QT, KT = s.sb("QT", [P, 2, 2, TPS, REP, P]), s.sb("KT", [P, 2, 2, T])
        QT16, KT16 = s.sb("QT16", [P, 2, 2, TPS, REP, P], BF16), s.sb("KT16", [P, 2, 2, T], BF16)
        V = s.sb("V", [P, 2, TPS, KVH, HD + 1])
        M, MT = s.sb("M", [P, 2, QH]), s.sb("MT", [QH, 2, P], BF16)
        probs, probs_prev = s.sb("probs", [P, 2, REP, P]), s.sb("probs_prev", [P, 2, REP, WINDOW])
        rec = s.sb("rec", [P, REP])
        on, yT = s.sb("on", [P, QH * HD]), s.sb("yT", [P, 8, P])

        max_bank = s.ps("max_bank", [P, 2, T])
        exp_bank, prev_bank = s.ps("exp_bank", [P, 2, T]), s.ps("prev_bank", [P, T])
        out_bank, banks = s.ps("out_bank", [P, T]), s.ps("banks", [P, 2, T])

        loaded, made, made_step = s.sem("weights_loaded"), s.sem("constants_made"), s.sem("made_step")
        hn_ready = s.sem("hn_ready")
        misc_full, misc_free = s.sem("misc_full"), s.sem("misc_free")
        squares_ready, ssq_ready, rms_step = s.sem("squares_ready"), s.sem("ssq_ready"), s.sem("rms_step")
        rms_ready, scaled_ready = s.sem("rms_ready"), s.sem("scaled_ready")
        cast_ready = s.sem("cast_ready")
        max_scores, max_done = s.sem("max_scores"), s.sem("max_done")
        scores, exp_done, pv_done = s.sem("scores"), s.sem("exp_done"), s.sem("pv_done")
        rec_ready, norm_ready, added = s.sem("rec_ready"), s.sem("norm_ready"), s.sem("added")
        waited = s.sem("waited")

        uses = [((G_UNITS - 1, 2), ("HT",))]
        for t in range(TPS):
            raw_at = [(0, 1), (0, 2), (1, 0)] if t == 0 else [(3 * t, x) for x in range(3)]
            uses += list(zip(raw_at, (("QA", t), ("QB", t), ("KV", t))))
            uses += [((3 * t + 5, x), (what, t)) for x, what in enumerate(("TQA", "TQB", "TK"))]
            uses += [((4 * t + 3, 0), ("MAX", t + 1))]
        for t in range(TPS):
            after = [(4 * t + 5, 0), (4 * t + 5, 1), (4 * t + 6, 1)] if t < 3 else [(G_UNITS, 0)] * 3
            uses += list(zip(after, (("YT0", t), ("YT1", t), ("OUT", t))))
        uses.sort(key=lambda e: e[0])
        NM, NA = len(uses), len(uses) - TPS
        early = ("HT", "QA", "QB", "KV", "TQA", "TQB", "TK")
        first = [e for e in uses if e[1][0] in early or e[1] == ("MAX", 4)]
        NF = len(first)

        def at(b, n, c):
            return (b + 1) * n + c

        def steps(prologue):
            chosen = first if prologue else uses
            found, a = [], NA - NF if prologue else 0
            for j, (place, what) in enumerate(chosen):
                found.append((place, what, NM - len(chosen) + j, a))
                a += what[0] != "OUT"
            return found

        def released(prologue, what):
            return {w: a + 1 for _, w, _, a in steps(prologue)}[what]

        def filled(prologue, what):
            return {w: j + 1 for _, w, j, _ in steps(prologue)}[what]

        def in_body(u, prologue):
            return u < G_UNITS and (not prologue or u + G_LEAD >= G_UNITS)

        def pairs_of(body, eng):
            body(eng, -1, 1, True)
            with eng.Fori(0, B // 2) as i:
                body(eng, i * 2, 0, False)
                body(eng, i * 2 + 1, 1, False)

        LOADED, MADE = 16 * 7, 8
        block = s.block()

        @block.sync
        def _(sp):
            sp.dma_start(wq[:, :], io["w_q"]).then_inc(loaded, 16)
            sp.dma_start(wkv[:, :], io["w_kv"]).then_inc(loaded, 16)
            sp.dma_start(wo[:, :, :], io["w_out"].rearrange("(q p) c -> p q c", p=P)).then_inc(loaded, 16)
            for j, n in enumerate(("q_norm", "k_norm")):
                for x in range(2):
                    sp.dma_start(norm_w[HD * x:HD * (x + 1), j:j + 1], io[n].unsqueeze(1)).then_inc(loaded, 16)

        @block.gpsimd
        def _(pool):
            g = nc.gpsimd
            for m in (mask_qk, mask_kq, mask_prev):
                g.memset(m[:, :], 0.0).then_inc(made_step, 1)
            g.memset(select[:, :, :], 0.0).then_inc(made_step, 1)
            g.memset(V[:, :, :, :, :], 1.0).then_inc(made, 1)
            g.tensor_copy(ident16[:, :], identity[:, :]).then_inc(made, 1)
            g.memset(minus_half[:, :], -0.5).then_inc(made, 1)
            pool.wait_ge(made_step, 4)
            g.affine_select(out=mask_qk[:, :], in_=mask_qk[:, :], compare_op=ALU.is_gt, fill=MASKED, base=0,
                            pattern=[[1, BAND]], channel_multiplier=-1).then_inc(made_step, 1)
            g.affine_select(out=mask_kq[:, :], in_=mask_kq[:, :], compare_op=ALU.is_ge, fill=MASKED, base=0,
                            pattern=[[1, P]], channel_multiplier=-1).then_inc(made_step, 1)
            g.affine_select(out=select[:, :, :], in_=select[:, :, :], compare_op=ALU.not_equal, fill=1.0, base=0,
                            pattern=[[1, QH], [0, P]], channel_multiplier=-1).then_inc(made, 1)
            g.affine_select(out=mask_prev[:, :], in_=mask_prev[:, :], compare_op=ALU.is_gt, fill=MASKED,
                            base=-WINDOW, pattern=[[-1, WINDOW]], channel_multiplier=1).then_inc(made, 1)
            pool.wait_ge(made_step, 6)
            g.affine_select(out=mask_qk[:, :], in_=mask_qk[:, :], compare_op=ALU.is_ge, fill=MASKED, base=WINDOW,
                            pattern=[[-1, BAND]], channel_multiplier=1).then_inc(made, 1)
            g.affine_select(out=mask_kq[:, :], in_=mask_kq[:, :], compare_op=ALU.is_gt, fill=MASKED, base=WINDOW,
                            pattern=[[-1, P]], channel_multiplier=1).then_inc(made, 1)
            pool.wait_ge(loaded, LOADED)
            g.tensor_tensor(norm_w[:, 0:1], norm_w[:, 0:1], norm_w[:, 1:2], ALU.mult).then_inc(made, 1)
            pool.wait_ge(made, MADE)

            def body(pool, b, par, prologue):
                to = (par + 1) % 2
                def scale_factors(t):
                    n = at(b, TPS, t)
                    pool.wait_ge(ssq_ready, n + 1)
                    pool.sem_inc(waited, 1)
                    g.tensor_scalar(rms[:, :], ssq[:, :], 1.0 / HD, RMS_EPS, ALU.mult, ALU.add).then_inc(rms_step, 1)
                    pool.wait_ge(rms_step, n + 1)
                    pool.sem_inc(waited, 1)
                    g.tensor_tensor(rms[:, :], rms[:, :], minus_half[:, :], ALU.pow).then_inc(rms_ready, 1)

                def narrow(t):
                    pool.wait_ge(misc_free, at(b, NA, released(prologue, ("TK", t))))
                    pool.sem_inc(waited, 1)
                    for i in range(2):
                        g.tensor_copy(QT16[:, to, i, t, :, :], QT[:, to, i, t, :, :])
                    g.tensor_copy(KT16[:, to, :, t * P:(t + 1) * P], KT[:, to, :, t * P:(t + 1) * P])\
                     .then_inc(cast_ready, 1)

                for t in range(TPS):
                    scale_factors(t)
                    if t:
                        narrow(t - 1)
                narrow(TPS - 1)

            pairs_of(body, pool)

        @block.tensor
        def _(pe):
            pe.sem_inc(misc_full, NM - NF - 1)
            pe.sem_inc(max_scores, 2 * (G_UNITS - G_LEAD))
            pe.sem_inc(scores, G_UNITS)
            pe.sem_inc(pv_done, G_UNITS)
            pe.wait_ge(loaded, LOADED)
            pe.wait_ge(made, MADE)

            def pv(b, par, u):
                t, g = u // KVH, u % KVH
                pe.wait_ge(exp_done, at(b, G_UNITS, u + 1))
                pe.wait_ge(norm_ready, at(b, G_UNITS, u))
                for a in range(REP):
                    o = out_bank[:, a * (HD + 1):(a + 1) * (HD + 1)]
                    last = nc.tensor.matmul(o, probs[:, u % 2, a, :], V[:, par, t, g, :], start=True, stop=True)
                    if t:
                        last = nc.tensor.matmul(o[0:WINDOW], probs_prev[P - WINDOW:, u % 2, a, :],
                                                V[P - WINDOW:, par, t - 1, g, :], start=False, stop=True,
                                                skip_group_check=True)
                last.then_inc(pv_done, 1)

            def turn(bank):
                for t in range(TPS):
                    last = nc.tensor.transpose(bank[:, t * P:(t + 1) * P], hn[:, t, :], identity[:, :])
                return last

            pe.wait_ge(hn_ready, 1)
            turn(banks[:, (NM - NF - 1) % 2, :]).then_inc(misc_full, 1)

            def body(pe, b, par, prologue):
                to = (par + 1) % 2

                def misc_use(u, what, j):
                    known = {j_: (w_, a_) for _, w_, j_, a_ in steps(prologue)}
                    if j - 2 in known:
                        before, a = known[j - 2]
                        if before[0] == "OUT":
                            pe.wait_ge(added, at(b, TPS, before[1] + 1))
                        else:
                            pe.wait_ge(misc_free, at(b, NA, a + 1))
                    elif prologue:
                        pe.wait_ge(misc_free, NA - NF)
                    else:
                        pe.wait_ge(misc_free, at(b, NA, 0))
                        if j == 0:
                            pe.wait_ge(added, at(b, TPS, 0))
                    kind, t = what[0], what[-1]
                    misc = banks[:, j % 2, :]
                    if kind == "HT":
                        pe.wait_ge(hn_ready, b + 3)
                        last = turn(misc)
                    elif kind in ("QA", "QB", "KV"):
                        w = {"QA": wq[:, 0:T], "QB": wq[:, T:], "KV": wkv[:, :]}[kind]
                        last = nc.tensor.matmul(misc[:, :], hT[:, t * P:(t + 1) * P], w, start=True, stop=True)
                    elif kind in ("TQA", "TQB", "TK"):
                        if kind == "TQA":
                            pe.wait_ge(scaled_ready, at(b, TPS, t + 1))
                        h0 = {"TQA": 0, "TQB": 8, "TK": 16}[kind]
                        for x in range(2 if kind == "TK" else 4):
                            last = nc.tensor.transpose(misc[:, x * P:(x + 1) * P],
                                                       scaled[:, t % 2, h0 + 2 * x:h0 + 2 * x + 2, :]
                                                       .rearrange("p h d -> p (h d)"), identity[:, :])
                    elif kind == "MAX":
                        pe.wait_ge(max_done, at(b, 2 * G_UNITS, 2 * u))
                        last = nc.tensor.transpose(misc[0:QH, 0:P], M[:, t % 2, :], identity[:, :])
                    elif kind in ("YT0", "YT1"):
                        pe.wait_ge(norm_ready, at(b, G_UNITS, KVH * (t + 1)))
                        for x in range(4):
                            q = x + (4 if kind == "YT1" else 0)
                            last = nc.tensor.transpose(misc[:, x * P:(x + 1) * P], on[:, q * P:(q + 1) * P],
                                                       identity[:, :])
                    else:
                        pe.wait_ge(misc_free, at(b, NA, released(False, ("YT1", t))))
                        for q in range(8):
                            last = nc.tensor.matmul(misc[:, 0:C], yT[:, q, :], wo[:, q, :],
                                                    start=(q == 0), stop=(q == 7))
                    last.then_inc(misc_full, 1)

                def misc_uses(u, place):
                    for _, what, j, _ in [e for e in steps(prologue) if e[0] == (u, place)]:
                        misc_use(u, what, j)

                for u in range(G_UNITS + 1):
                    if u == G_UNITS and not prologue:
                        pv(b, par, G_UNITS - 1)
                    misc_uses(u, 0)
                    if in_body(u, prologue):
                        n = u + G_LEAD
                        pb = to if n >= G_UNITS else par
                        t, g = (n % G_UNITS) // KVH, n % KVH
                        if g == 0:
                            pe.wait_ge(cast_ready, at(b, TPS, t + 1) if n >= G_UNITS else at(b, TPS, 0))
                        rows, i = slice(64 * (g % 2), 64 * (g % 2) + 64), g // 2
                        W, c0 = (BAND, t * P - WINDOW) if t else (P, 0)
                        for half in range(2):
                            if not (prologue and n == G_UNITS):
                                pe.wait_ge(max_done, at(b, 2 * G_UNITS, 2 * u + half - 1))
                            for x in range(2):
                                nc.tensor.matmul(max_bank[:, half, x * W:(x + 1) * W],
                                                 QT16[rows, pb, i, t, 2 * half + x, :],
                                                 KT16[rows, pb, i, c0:c0 + W], start=True, stop=True)
                            nc.tensor.matmul(max_bank[:, half, 0:2 * W].rearrange("p (x k) -> p x k", x=2),
                                             ident16[:, :],
                                             mask_qk[:, BAND - W:].unsqueeze(1).to_broadcast([P, 2, W]),
                                             start=False, stop=True, skip_group_check=True)\
                              .then_inc(max_scores, 1)
                    misc_uses(u, 1)
                    if u < G_UNITS and not prologue:
                        t, g = u // KVH, u % KVH
                        rows, i = slice(64 * (g % 2), 64 * (g % 2) + 64), g // 2
                        if g == 0:
                            if t:
                                pe.wait_ge(misc_free, at(b, NA, released(False, ("MAX", t))))
                        pe.wait_ge(exp_done, at(b, G_UNITS, u - 1))
                        o = exp_bank[:, u % 2, :]
                        nc.tensor.matmul(o, KT[rows, par, i, t * P:(t + 1) * P],
                                         QT[rows, par, i, t, :, :].rearrange("p a q -> p (a q)"),
                                         start=True, stop=True)
                        nc.tensor.matmul(o.rearrange("p (a q) -> p a q", a=REP), ident16[:, :],
                                         mask_kq[:, :].unsqueeze(1).to_broadcast([P, REP, P]),
                                         start=False, stop=True, skip_group_check=True)
                        for a in range(REP):
                            oa = exp_bank[:, u % 2, a * P:(a + 1) * P]
                            last = nc.tensor.matmul(oa, select[:, REP * g + a, :], MT[:, t % 2, :],
                                                    start=False, stop=True, skip_group_check=True)
                        if t:
                            top = slice(P - WINDOW, P)
                            nc.tensor.matmul(prev_bank[rows, 0:REP * WINDOW],
                                             KT[rows, par, i, t * P - WINDOW:t * P],
                                             QT[rows, par, i, t, :, 0:WINDOW], start=True, stop=True)
                            nc.tensor.matmul(prev_bank[rows, 0:REP * WINDOW]
                                             .rearrange("p (a q) -> p a q", a=REP), ident16[:, top],
                                             mask_prev[:, :].unsqueeze(1).to_broadcast([P, REP, WINDOW]),
                                             start=False, stop=True, skip_group_check=True)
                            for a in range(REP):
                                oa = prev_bank[rows, a * WINDOW:(a + 1) * WINDOW]
                                last = nc.tensor.matmul(oa, select[:, REP * g + a, 0:WINDOW], MT[:, t % 2, 0:WINDOW],
                                                        start=False, stop=True, skip_group_check=True)
                        last.then_inc(scores, 1)
                        if u >= 1:
                            pv(b, par, u - 1)
                    misc_uses(u, 2)

            pairs_of(body, pe)

        @block.scalar
        def _(act):
            act.sem_inc(misc_free, NA - NF - 1)
            act.sem_inc(exp_done, G_UNITS)
            act.wait_ge(made, MADE)
            act.wait_ge(misc_full, NM - NF)
            nc.scalar.activation(hT[:, :], banks[:, (NM - NF - 1) % 2, :], ACT.Copy).then_inc(misc_free, 1)

            def body(act, b, par, prologue):
                to = (par + 1) % 2

                def misc_uses(u, places):
                    for _, what, j, _ in [e for e in steps(prologue)
                                          if e[0][0] == u and e[0][1] in places and e[1][0] != "OUT"]:
                        kind, t = what[0], what[-1]
                        misc = banks[:, j % 2, :]
                        act.wait_ge(misc_full, at(b, NM, j + 1))
                        if kind == "HT":
                            last = nc.scalar.activation(hT[:, :], misc[:, :], ACT.Copy)
                        elif kind in ("QA", "QB", "KV"):
                            if kind == "QA" and not (prologue and t == 0):
                                act.wait_ge(ssq_ready, at(b, TPS, t))
                            if kind == "QA" and not (prologue and t < 2):
                                act.wait_ge(scaled_ready, at(b, TPS, t - 1))
                            h0, nh = {"QA": (0, 8), "QB": (8, 8), "KV": (16, 4)}[kind]
                            flat = lambda x: x[:, h0:h0 + nh, :].rearrange("p h d -> p (h d)")
                            nc.scalar.activation(flat(raw[:, t % 2]), misc[:, 0:nh * HD], ACT.Copy)
                            last = nc.scalar.activation(flat(squares), misc[:, 0:nh * HD], ACT.Square)
                            if kind == "KV":
                                last.then_inc(squares_ready, 1)
                                last = nc.scalar.activation(V[:, to, t, :, 0:HD],
                                                            misc[:, KVH * HD:].rearrange("p (h d) -> p h d", d=HD),
                                                            ACT.Copy)
                        elif kind in ("TQA", "TQB"):
                            last = nc.scalar.activation(QT[:, to, 0 if kind == "TQA" else 1, t, :, :]
                                                        .rearrange("p a q -> p (a q)"), misc[:, :], ACT.Copy)
                        elif kind == "TK":
                            last = nc.scalar.activation(KT[:, to, :, t * P:(t + 1) * P],
                                                        misc[:, 0:2 * P].rearrange("p (i k) -> p i k", i=2),
                                                        ACT.Identity, scale=norm_w[:, 0:1])
                        elif kind == "MAX":
                            last = nc.scalar.activation(MT[:, t % 2, :], misc[0:QH, 0:P], ACT.Copy, scale=-1.0)
                        else:
                            q0 = 0 if kind == "YT0" else 4
                            if kind == "YT0":
                                act.wait_ge(misc_full, at(b, NM, filled(False, ("OUT", t - 1)) if t else 0))
                            last = nc.scalar.activation(yT[:, q0:q0 + 4, :].rearrange("p q n -> p (q n)"),
                                                        misc[:, :], ACT.Copy)
                        last.then_inc(misc_free, 1)

                for u in range(G_UNITS + 1):
                    misc_uses(u, (0, 1))
                    if u < G_UNITS and not prologue:
                        t = u // KVH
                        act.wait_ge(scores, at(b, G_UNITS, u + 1))
                        act.wait_ge(pv_done, at(b, G_UNITS, u - 1))
                        last = nc.scalar.activation(probs[:, u % 2, :, :].rearrange("p a q -> p (a q)"),
                                                    exp_bank[:, u % 2, :], ACT.Exp, scale=HD ** -0.5)
                        if t:
                            top = slice(P - WINDOW, P)
                            half = slice(64 * (u % 2), 64 * (u % 2) + 64)
                            last = nc.scalar.activation(probs_prev[top, u % 2, :, :].rearrange("p a q -> p (a q)"),
                                                        prev_bank[half, 0:REP * WINDOW], ACT.Exp,
                                                        scale=HD ** -0.5)
                        last.then_inc(exp_done, 1)
                    misc_uses(u, (2,))

            pairs_of(body, act)

        @block.vector
        def _(dve):
            v = nc.vector
            dve.sem_inc(max_done, 2 * (G_UNITS - G_LEAD))
            dve.sem_inc(norm_ready, G_UNITS)
            dve.sem_inc(added, TPS)

            def normalise(b, u):
                g = u % KVH
                dve.wait_ge(pv_done, at(b, G_UNITS, u + 1))
                o = out_bank[:, 0:REP * (HD + 1)].rearrange("p (a d) -> p a d", a=REP)
                v.reciprocal(rec[:, :], o[:, :, HD]).then_inc(rec_ready, 1)
                dve.wait_ge(rec_ready, b * G_UNITS + u + 1)
                if g == 0 and u:
                    dve.wait_ge(misc_full, at(b, NM, filled(False, ("YT1", u // KVH - 1))))
                n = REP * HD
                v.tensor_tensor(on[:, g * n:(g + 1) * n].rearrange("p (a d) -> p a d", a=REP), o[:, :, 0:HD],
                                rec[:, :].unsqueeze(2).to_broadcast([P, REP, HD]), ALU.mult).then_inc(norm_ready, 1)

            def layernorm(b):
                tokens, moments = X[:, bass.ds(b * TPS, TPS), :], stats[:, bass.ds(b * TPS, TPS), :]
                for t in range(TPS):
                    last = v.tensor_scalar(hn[:, t, :], tokens[:, t, :], moments[:, t:t + 1, 0],
                                           moments[:, t:t + 1, 1], ALU.subtract, ALU.mult)
                last.then_inc(hn_ready, 1)

            layernorm(0)

            def body(dve, b, par, prologue):
                for u in range(G_UNITS + 1):
                    if u == G_UNITS // 2:
                        dve.wait_ge(misc_full, NM - NF if prologue else at(b, NM, 0))
                        layernorm(b + 2)
                    if u == G_UNITS and not prologue:
                        normalise(b, G_UNITS - 1)
                    if in_body(u, prologue):
                        n = (u + G_LEAD) % G_UNITS
                        t, g = n // KVH, n % KVH
                        W = BAND if t else P
                        for half in range(2):
                            dve.wait_ge(max_scores, at(b, 2 * G_UNITS, 2 * u + half + 1))
                            h = REP * g + 2 * half
                            v.reduce_max(M[:, t % 2, h:h + 2],
                                         max_bank[:, half, 0:2 * W].rearrange("p (x w) -> p x w", x=2), AX.X)\
                             .then_inc(max_done, 1)
                    for _, what, j, _ in [e for e in steps(prologue) if e[0][0] == u and e[1][0] == "OUT"]:
                        tile = b * TPS + what[1]
                        dve.wait_ge(misc_full, at(b, NM, j + 1))
                        v.tensor_tensor(tile_of(X, tile), tile_of(X, tile), banks[:, j % 2, 0:C], ALU.add)\
                         .then_inc(added, 1)
                    if u < G_UNITS and not prologue and u >= 1:
                        normalise(b, u - 1)
                    if u % 3 == 1 and u // 3 < TPS:
                        dve.wait_ge(squares_ready, at(b, TPS, u // 3 + 1))
                        v.reduce_sum(ssq[:, :], squares[:, :, :], AX.X).then_inc(ssq_ready, 1)
                    if u % 3 == 0 and u and u // 3 <= TPS:
                        t = u // 3 - 1
                        dve.wait_ge(rms_ready, at(b, TPS, t + 1))
                        if t >= 2:
                            dve.wait_ge(misc_full, at(b, NM, filled(prologue, ("TK", t - 2))))
                        v.tensor_tensor(scaled[:, t % 2, :, :], raw[:, t % 2, :, :],
                                        rms[:, :].unsqueeze(2).to_broadcast([P, NORMED, HD]), ALU.mult)\
                         .then_inc(scaled_ready, 1)

            pairs_of(body, dve)


DH, DK = 4, 32
TAPS = 4
QKV = 3 * C
L2_EPS = 1e-6
REACH = 2 * P
FILTER_PAD = 3 * P
CH_GROUP = 8


def delta_inputs(nc, tag, io, X, stats, identity, v_all, beta, qk_dram):
    with Stage(nc, tag) as s:
        w = s.sb("w", [P, QKV])
        taps = s.sb("taps", [P, TAPS, QKV])
        w_beta = s.sb("w_beta", [P, DH])
        minus_half = s.sb("minus_half", [P, TPS * 2 * DH])
        hn = s.sb("hn", [P, 2, TPS, C])
        hT = s.sb("hT", [P, 2, TAPS - 1 + T])
        qk = s.sb("qk", [P, 2, TPS, 2 * C])
        squares = s.sb("squares", [P, TPS, 2 * C])
        ssq, scale = s.sb("ssq", [P, TPS * 2 * DH]), s.sb("scale", [P, TPS * 2 * DH])
        unit = s.sb("unit", [P, 2, TPS, 2 * C])
        t_bank = s.ps("t_bank", [P, 2, T])
        p_bank = s.ps("p_bank", [P, TPS, T])

        loaded, made = s.sem("weights_loaded"), s.sem("constants_made")
        hn_ready, turned, hT_ready = s.sem("hn_ready"), s.sem("turned_1"), s.sem("hT_ready_1")
        projected, silu_done, beta_kept = s.sem("projected_1"), s.sem("silu_done_1"), s.sem("beta_kept_1")
        squares_ready, ssq_ready = s.sem("squares_ready"), s.sem("ssq_ready")
        scale_step, scale_ready, unit_ready = s.sem("scale_step"), s.sem("scale_ready"), s.sem("unit_ready_2")
        stored = [s.sem(f"stored{n}_1") for n in range(2)]
        beta_all, waited = s.sem("beta_all"), s.sem("waited")
        LOADED, MADE = 16 * 3, 4
        block = s.block()

        def sequences(body, eng):
            with eng.Fori(0, B // 2 - 1) as i:
                for n in range(2):
                    body(i, i * 2 + n, n, 2)
            body(B // 2 - 1, B - 2, 0, 1)
            body(B // 2 - 1, B - 1, 1, 0)

        @block.sync
        def _(sp):
            sp.dma_start(w[:, :], io["w_qkv"]).then_inc(loaded, 16)
            sp.dma_start(taps[:, :, :], io["conv"].partition_broadcast(P)).then_inc(loaded, 16)
            sp.dma_start(w_beta[:, :], io["w_beta"]).then_inc(loaded, 16)
            for n in range(2):
                sp.sem_inc(stored[n], 16)
            with sp.Fori(0, B // 2) as i:
                for n in range(2):
                    sp.wait_ge(unit_ready, i * 2 + (n + 3))
                    sp.dma_start(qk_dram[bass.ds(i * 2 + n, 1)].rearrange("o p t c -> p (o t) c"), unit[:, n, :, :])\
                      .then_inc(stored[n], 16)
            for n in range(2):
                sp.wait_ge(stored[n], 16 * (B // 2 + 1))

        @block.gpsimd
        def _(pool):
            g = nc.gpsimd
            g.memset(hT[:, :, 0:TAPS - 1], 0.0).then_inc(made, 1)
            g.memset(minus_half[:, :], -0.5).then_inc(made, 1)
            g.memset(v_all[:, :, :], 0.0).then_inc(made, 1)
            pool.wait_ge(made, MADE)
            with pool.Fori(0, B // 2) as i:
                for n in range(2):
                    b = i * 2 + n
                    pool.wait_ge(silu_done, b + 2)
                    g.tensor_tensor(squares[:, :, :], qk[:, n, :, :], qk[:, n, :, :], ALU.mult)\
                     .then_inc(squares_ready, 1)
                    pool.wait_ge(ssq_ready, b + 1)
                    pool.sem_inc(waited, 1)
                    g.tensor_scalar(scale[:, :], ssq[:, :], L2_EPS, None, ALU.add).then_inc(scale_step, 1)
                    pool.wait_ge(scale_step, b + 1)
                    g.tensor_tensor(scale[:, :], scale[:, :], minus_half[:, :], ALU.pow).then_inc(scale_ready, 1)

        @block.tensor
        def _(pe):
            pe.sem_inc(turned, 1)
            pe.sem_inc(projected, 1)

            def turn(n):
                for t in range(TPS):
                    last = nc.tensor.transpose(t_bank[:, n, t * P:(t + 1) * P], hn[:, n, t, :], identity[:, :])
                last.then_inc(turned, 1)

            pe.wait_ge(made, MADE)
            pe.wait_ge(hn_ready, 1)
            turn(0)

            def body(i, b, n, follow):
                if follow:
                    pe.wait_ge(hn_ready, b + 2)
                    pe.wait_ge(hT_ready, b + 1)
                    turn((n + 1) % 2)
                pe.wait_ge(hT_ready, b + 2)
                pe.wait_ge(silu_done, b + 1)
                pe.wait_ge(beta_kept, b + 1)
                for t in range(TPS):
                    for j in range(TAPS):
                        nc.tensor.matmul(p_bank[:, t, 0:QKV], hT[:, n, t * P + j:t * P + j + P], taps[:, j, :],
                                         start=(j == 0), stop=(j == TAPS - 1))
                    now = hT[:, n, TAPS - 1 + t * P:TAPS - 1 + (t + 1) * P]
                    last = nc.tensor.matmul(p_bank[:, t, QKV:QKV + DH], now, w_beta[:, :], start=True, stop=True)
                last.then_inc(projected, 1)

            sequences(body, pe)

        @block.scalar
        def _(act):
            act.sem_inc(hT_ready, 1)
            act.sem_inc(silu_done, 1)
            act.wait_ge(made, MADE)
            act.wait_ge(turned, 2)
            nc.scalar.activation(hT[:, 0, TAPS - 1:], t_bank[:, 0, :], ACT.Copy).then_inc(hT_ready, 1)

            def body(i, b, n, follow):
                if follow:
                    act.wait_ge(turned, b + 3)
                    act.wait_ge(projected, b + 1)
                    nc.scalar.activation(hT[:, (n + 1) % 2, TAPS - 1:], t_bank[:, (n + 1) % 2, :], ACT.Copy)\
                      .then_inc(hT_ready, 1)
                act.wait_ge(projected, b + 2)
                act.wait_ge(unit_ready, b + 1)
                nc.scalar.activation(qk[:, n, :, :], p_bank[:, :, 0:2 * C], ACT.Silu)
                nc.scalar.activation(v_all[:, bass.ds(b * (TPS + 1) + 1, TPS), :], p_bank[:, :, 2 * C:QKV],
                                     ACT.Silu).then_inc(silu_done, 1)

            sequences(body, act)
            act.wait_ge(beta_kept, B + 1)
            nc.scalar.activation(beta[:, 0:NT, :], beta[:, 0:NT, :], ACT.Sigmoid).then_inc(beta_all, 1)

        @block.vector
        def _(dve):
            v = nc.vector
            dve.sem_inc(beta_kept, 1)
            dve.sem_inc(unit_ready, 2)
            dve.wait_ge(loaded, LOADED)
            v.tensor_tensor(taps[:, :, :], taps[:, :, :], w[:, :].unsqueeze(1).to_broadcast([P, TAPS, QKV]),
                            ALU.mult).then_inc(made, 1)

            def normalise(b, n):
                tokens, moments = X[:, bass.ds(b * TPS, TPS), :], stats[:, bass.ds(b * TPS, TPS), :]
                for t in range(TPS):
                    last = v.tensor_scalar(hn[:, n, t, :], tokens[:, t, :], moments[:, t:t + 1, 0],
                                           moments[:, t:t + 1, 1], ALU.subtract, ALU.mult)
                last.then_inc(hn_ready, 1)

            normalise(0, 0)
            normalise(1, 1)

            def body(i, b, n, follow):
                dve.wait_ge(projected, b + 2)
                dve.wait_ge(silu_done, b + 2)
                v.tensor_copy(beta[:, bass.ds(b * TPS, TPS), :], p_bank[:, :, QKV:QKV + DH]).then_inc(beta_kept, 1)
                if follow == 2:
                    dve.wait_ge(turned, b + 2)
                    normalise(b + 2, n)
                dve.wait_ge(squares_ready, b + 1)
                v.reduce_sum(ssq[:, :], squares[:, :, :].rearrange("p t (h d) -> p (t h) d", d=DK), AX.X)\
                 .then_inc(ssq_ready, 1)
                dve.wait_ge(scale_ready, b + 1)
                dve.wait_ge(stored[n], i * 16 + 16)
                v.tensor_tensor(unit[:, n, :, :].rearrange("p t (h d) -> p (t h) d", d=DK),
                                qk[:, n, :, :].rearrange("p t (h d) -> p (t h) d", d=DK),
                                scale[:, :].unsqueeze(2).to_broadcast([P, TPS * 2 * DH, DK]), ALU.mult)\
                 .then_inc(unit_ready, 1)

            sequences(body, dve)


def long_filters(nc, tag, io, v_all, filtered):
    groups = C // CH_GROUP
    HALF = B * (TPS + 1) // 2
    with Stage(nc, tag) as s:
        band = s.sb("band", [P, 4, CH_GROUP, REACH])
        flip = s.sb("flip", [P, P])
        flipped = s.sb("flipped", [P, 2, 2, HALF, CH_GROUP])
        bank = s.ps("bank", [P, 4, T])
        flip_bank = s.ps("flip_bank", [P, 2, 2, T])

        loaded = [s.sem(f"loaded{n}") for n in range(4)]
        made, step, products = s.sem("flip_made"), s.sem("flip_step"), s.sem("products")
        flip_done, flip_kept = s.sem("flip_done"), s.sem("flip_kept_1")
        kept = [s.sem("kept_short_2"), s.sem("kept_long_2")]
        block = s.block()

        @block.sync
        def _(sp):
            def load(g, n):
                for j, name in enumerate(("short", "long")):
                    rows = io[name]
                    src = bass.AP(tensor=rows.tensor, offset=g * (CH_GROUP * FILTER_PAD),
                                  ap=[[1, P], [FILTER_PAD, CH_GROUP], [1, REACH]])
                    sp.dma_start(band[:, 2 * n + j, :, :], src).then_inc(loaded[2 * n + j], 16)
            for n in range(2):
                load(n, n)
            with sp.Fori(0, groups // 2 - 1) as i:
                for n in range(2):
                    sp.wait_ge(products, (i * 2 + (n + 1)) * 2)
                    load(i * 2 + (n + 2), n)

        @block.gpsimd
        def _(pool):
            nc.gpsimd.memset(flip[:, :], 0.0).then_inc(step, 1)
            pool.wait_ge(step, 1)
            nc.gpsimd.affine_select(out=flip[:, :], in_=flip[:, :], compare_op=ALU.not_equal, fill=1.0,
                                    base=1 - P, pattern=[[1, P]], channel_multiplier=1).then_inc(made, 1)

        def groups_of(body, eng):
            with eng.Fori(0, groups // 2 - 1) as i:
                for n in range(2):
                    body(i, i * 2 + n, n, True)
            body(groups // 2 - 1, groups - 2, 0, True)
            body(groups // 2 - 1, groups - 1, 1, False)

        @block.tensor
        def _(pe):
            pe.wait_ge(made, 1)

            def turn(g, n):
                for half in range(2):
                    last = nc.tensor.matmul(flip_bank[:, n, half, 0:HALF * CH_GROUP], flip[:, :],
                                            v_all[:, half * HALF:(half + 1) * HALF, bass.ds(g * CH_GROUP, CH_GROUP)],
                                            start=True, stop=True)
                last.then_inc(flip_done, 1)

            def body(i, g, n, ahead):
                if ahead:
                    turn(g + 1, (n + 1) % 2)
                pe.wait_ge(flip_kept, g + 2)
                for j in range(2):
                    m = 2 * n + j
                    pe.wait_ge(loaded[m], (i + 1) * 16)
                    pe.wait_ge(kept[j], g + 1)
                    for c in range(CH_GROUP):
                        o = bank[:, m, c * NT:(c + 1) * NT]
                        tiles = flipped[:, n, :, :, c].rearrange("p f (b t) -> p (f b) t", t=TPS + 1)
                        nc.tensor.matmul(o, band[:, m, c, 0:P], tiles[:, :, 1:], start=True, stop=False)
                        last = nc.tensor.matmul(o, band[:, m, c, P:REACH], tiles[:, :, 0:TPS],
                                                start=False, stop=True)
                    last.then_inc(products, 1)

            turn(0, 0)
            groups_of(body, pe)

        def keep(eng, copy, i, g, n, j):
            m = 2 * n + j
            eng.wait_ge(products, g * 2 + (j + 1))
            copy(filtered[:, j, :, bass.ds(g * CH_GROUP, CH_GROUP)],
                 bank[:, m, :].rearrange("p (c t) -> p t c", c=CH_GROUP)).then_inc(kept[j], 1)

        @block.scalar
        def _(act):
            act.sem_inc(kept[0], 2)
            act.sem_inc(flip_kept, 1)

            def keep_flipped(g, n):
                act.wait_ge(flip_done, g + 1)
                nc.scalar.activation(flipped[:, n, :, :, :].rearrange("p f t c -> p f (t c)"),
                                     flip_bank[:, n, :, 0:HALF * CH_GROUP], ACT.Copy).then_inc(flip_kept, 1)

            def body(i, g, n, ahead):
                if ahead:
                    keep_flipped(g + 1, (n + 1) % 2)
                keep(act, lambda o, x: nc.scalar.activation(o, x, ACT.Copy), i, g, n, 0)

            keep_flipped(0, 0)
            groups_of(body, act)

        @block.vector
        def _(dve):
            dve.sem_inc(kept[1], 2)
            groups_of(lambda i, g, n, ahead: keep(dve, nc.vector.tensor_copy, i, g, n, 1), dve)


CHUNK = 32
CPT = P // CHUNK
SOLVED = B * T // CHUNK // 2


def chunk_products(nc, tag, io, identity, beta, local_all, qk_dram, a_dram):
    with Stage(nc, tag) as s:
        masks = s.sb("masks", [P, 2, CHUNK])
        qk = s.sb("qk", [P, 2, TPS, 2 * C])
        kb = s.sb("kb", [P, 2, TPS, C])
        turned = s.sb("turned", [P, 2, 3, P])
        A = s.sb("A", [P, 2, TPS, DH, CHUNK])
        t_bank, bank = s.ps("t_bank", [P, 2, T]), s.ps("bank", [P, DH, T])

        masks_in, qk_in = s.sem("masks_in"), [s.sem(f"qk_in{n}") for n in range(2)]
        kb_ready, turns_done, turned_kept = s.sem("kb_ready"), s.sem("turns_done"), s.sem("turned_kept")
        products, products_kept, a_ready = s.sem("products_2"), s.sem("products_kept_1"), s.sem("a_ready")
        stored, waited = [s.sem(f"stored{n}_1") for n in range(2)], s.sem("waited")
        block = s.block()

        def sequences(body, eng):
            with eng.Fori(0, B // 2 - 1) as i:
                for n in range(2):
                    body(i, i * 2 + n, n, True)
            body(B // 2 - 1, B - 2, 0, True)
            body(B // 2 - 1, B - 1, 1, False)

        @block.sync
        def _(sp):
            sp.dma_start(masks[:, :, :], io["chunk_masks"].rearrange("m p i -> p m i")).then_inc(masks_in, 16)
            for n in range(2):
                sp.sem_inc(stored[n], 16)
                sp.dma_start(qk[:, n, :, :], qk_dram[n]).then_inc(qk_in[n], 16)

            def store(b, n):
                sp.wait_ge(a_ready, b + 1)
                sp.dma_start(a_dram[bass.ds(b, 1)].rearrange("o (t p) n -> p (o t) n", p=P),
                             A[:, n, :, :, :].rearrange("p t h i -> p t (h i)")).then_inc(stored[n], 16)

            with sp.Fori(0, B // 2 - 1) as i:
                for n in range(2):
                    b = i * 2 + n
                    store(b, n)
                    sp.dma_start(qk[:, n, :, :], qk_dram[bass.ds(b + 2, 1)].rearrange("o p t c -> p (o t) c"))\
                      .then_inc(qk_in[n], 16)
            for n in range(2):
                store(B - 2 + n, n)
            for n in range(2):
                sp.wait_ge(stored[n], 16 * (B // 2 + 1))

        @block.gpsimd
        def _(pool):
            def weigh(i, b, n):
                pool.wait_ge(qk_in[n], (i + 1) * 16)
                pool.sem_inc(waited, 1)
                heads = lambda x: x.rearrange("p t (h d) -> p t h d", d=DK)
                nc.gpsimd.tensor_tensor(heads(kb[:, n, :, :]), heads(qk[:, n, :, C:]),
                                        beta[:, bass.ds(b * TPS, TPS), :].unsqueeze(3)
                                        .to_broadcast([P, TPS, DH, DK]), ALU.mult).then_inc(kb_ready, 1)

            def body(i, b, n, ahead):
                if ahead:
                    pool.wait_ge(turns_done, b * TPS + 1)
                    weigh(i + n, b + 1, (n + 1) % 2)

            weigh(0, 0, 0)
            sequences(body, pool)

        @block.tensor
        def _(pe):
            def turn(b, n, t):
                if t == 0:
                    pe.wait_ge(kb_ready, b + 1)
                for x, src in enumerate((qk[:, n, t, C:], kb[:, n, t, :], qk[:, n, t, 0:C])):
                    last = nc.tensor.transpose(t_bank[:, t % 2, x * P:(x + 1) * P], src, identity[:, :])
                last.then_inc(turns_done, 1)

            def body(i, b, n, ahead):
                for t in range(TPS):
                    if t < TPS - 1:
                        turn(b, n, t + 1)
                    elif ahead:
                        turn(b + 1, (n + 1) % 2, 0)
                    c, m = b * TPS + t, t % 2
                    pe.wait_ge(turned_kept, c + 1)
                    pe.wait_ge(products_kept, c + 1)
                    pe.sem_inc(waited, 1)
                    for h in range(DH):
                        rows = slice(DK * h, DK * h + DK)
                        for x in range(CPT):
                            cols = slice(CHUNK * x, CHUNK * x + CHUNK)
                            last = nc.tensor.matmul(bank[cols, h, 0:2 * CHUNK]
                                                    .rearrange("p (x i) -> p x i", x=2), turned[rows, m, 0, cols],
                                                    turned[rows, m, 1:3, cols], start=True, stop=True)
                    last.then_inc(products, 1)

            turn(0, 0, 0)
            sequences(body, pe)

        @block.scalar
        def _(act):
            def body(i, b, n, ahead):
                for t in range(TPS):
                    c = b * TPS + t
                    act.wait_ge(turns_done, c + 1)
                    act.wait_ge(products, c + 1)
                    nc.scalar.activation(turned[:, t % 2, :, :].rearrange("p x n -> p (x n)"),
                                         t_bank[:, t % 2, 0:3 * P], ACT.Copy).then_inc(turned_kept, 1)

            sequences(body, act)

        @block.vector
        def _(dve):
            v = nc.vector
            dve.sem_inc(products, 2)
            dve.sem_inc(products_kept, 1)
            dve.wait_ge(masks_in, 16)

            def body(i, b, n, ahead):
                for t in range(TPS):
                    c = b * TPS + t
                    dve.wait_ge(products, c + 3)
                    if t == 0:
                        dve.wait_ge(stored[n], (i + 1) * 16)
                    part = lambda x: bank[:, :, x * CHUNK:(x + 1) * CHUNK]
                    over = lambda x: masks[:, x, :].unsqueeze(1).to_broadcast([P, DH, CHUNK])
                    last = v.tensor_tensor(A[:, n, t, :, :], part(0), over(0), ALU.mult)
                    if t == TPS - 1:
                        last.then_inc(a_ready, 1)
                    v.tensor_tensor(local_all[:, bass.ds(c, 1), :].rearrange("p o (h i) -> p (o h) i", h=DH),
                                    part(1), over(1), ALU.mult).then_inc(products_kept, 1)

            sequences(body, dve)


def solve_chunks(nc, tag, a_dram, t_dram):
    with Stage(nc, tag) as s:
        A = s.sb("A", [P, 2, CHUNK, DH, CHUNK])
        S = s.sb("S", [P, 2, CHUNK, DH, CHUNK])
        terms = s.sb("terms", [P, 2, DH * (CHUNK - 1) ** 2])
        loaded, cleared, ones = s.sem("loaded"), s.sem("cleared"), s.sem("ones_set")
        terms_ready = [s.sem(f"terms_ready{g}") for g in range(2)]
        row_ready, stored = [s.sem(f"row_ready{g}") for g in range(2)], s.sem("stored")
        chunks = [x.rearrange("b (c j) n -> (b c) (j n)", j=CHUNK) for x in (a_dram, t_dram)]
        flat = lambda x, g: x[:, g].rearrange("p k h i -> p (k h i)")
        block = s.block()

        @block.sync
        def _(sp):
            for g in range(2):
                sp.dma_start(flat(A, g), chunks[0][g * SOLVED:(g + 1) * SOLVED]).then_inc(loaded, 16)
            for g in range(2):
                sp.wait_ge(row_ready[g], CHUNK - 1)
                sp.dma_start(chunks[1][g * SOLVED:(g + 1) * SOLVED], flat(S, g)).then_inc(stored, 16)
            sp.wait_ge(stored, 32)

        @block.gpsimd
        def _(pool):
            nc.gpsimd.memset(S[:, :, :, :, :], 0.0).then_inc(cleared, 1)
            pool.wait_ge(cleared, 1)
            for g in range(2):
                for h in range(DH):
                    at = flat(S, g)[:, h * CHUNK:(CHUNK - 1) * (DH * CHUNK + 1) + h * CHUNK + 1:DH * CHUNK + 1]
                    nc.gpsimd.memset(at, 1.0).then_inc(ones, 1)

        @block.vector
        def _(dve):
            v = nc.vector
            dve.wait_ge(loaded, 32)
            dve.wait_ge(ones, 2 * DH)
            for i in range(1, CHUNK):
                view = lambda g: terms[:, g, 0:DH * i * i].rearrange("p (h k j) -> p h k j", h=DH, k=i)
                for g in range(2):
                    if i > 1:
                        dve.wait_ge(row_ready[g], i - 1)
                    v.tensor_tensor(view(g), A[:, g, 0:i, :, i].rearrange("p j h -> p h j").unsqueeze(2)
                                    .to_broadcast([P, DH, i, i]),
                                    S[:, g, 0:i, :, 0:i].rearrange("p k h j -> p h k j"), ALU.mult)\
                     .then_inc(terms_ready[g], 1)
                for g in range(2):
                    dve.wait_ge(terms_ready[g], i)
                    v.reduce_sum(S[:, g, 0:i, :, i].rearrange("p k h -> p h k"), view(g), AX.X)\
                     .then_inc(row_ready[g], 1)


def delta_states(nc, tag, identity, v_all, beta, local_all, qk_dram, t_dram, delta_dram):
    STEPS = TPS * CPT
    with Stage(nc, tag) as s:
        same_head = s.sb("same_head", [P, P])
        minus_beta = s.sb("minus_beta", [P, NT, DH])
        qk, inv = s.sb("qk", [P, 2, 2, 2 * C]), s.sb("inv", [P, 2, 2, DH, CHUNK])
        vk = s.sb("vk", [P, 2, DH, 2, DK])
        local = s.sb("local", [P, 2, 2, C])
        w = s.sb("w", [P, 2, C])
        wqT = s.sb("wqT", [P, 2, 2, 2, P])
        U, S, out = s.sb("U", [P, 2, C]), s.sb("S", [P, 2, C]), s.sb("out", [P, 2, TPS, C])
        uw_bank = s.ps("uw_bank", [P, 2, 2, T])
        t_bank, s_bank = s.ps("t_bank", [P, 2, T]), s.ps("s_bank", [P, 2, T])
        OUT_AT = 2 * C

        made, cleared, waited = s.sem("constants_made"), s.sem("cleared"), s.sem("waited")
        tile_in = [[s.sem(f"tile_in{n}{m}") for m in range(2)] for n in range(2)]
        stored = [s.sem(f"stored{n}_1") for n in range(2)]
        per_seq = lambda name: [s.sem(f"{name}{n}") for n in range(2)]
        vk_ready, uw_done, w_kept = per_seq("vk_ready"), per_seq("uw_done"), per_seq("w_kept")
        turned, wqT_ready = per_seq("turned"), per_seq("wqT_ready")
        u_done, u_kept, s_done, s_kept = (per_seq("u_done"), per_seq("u_kept"), per_seq("s_done"),
                                          per_seq("s_kept"))
        out_done, out_kept = per_seq("out_done_1_"), per_seq("out_kept_1_")
        block = s.block()

        def seq_pairs(body, eng):
            with eng.Fori(0, B // 2 - 1) as i:
                body(i, True)
            body(B // 2 - 1, False)

        def following(i, t, more):
            if t < TPS - 1:
                return i, t + 1, i * TPS + (t + 1)
            return (i + 1, 0, i * TPS + TPS) if more else None

        @block.sync
        def _(sp):
            def load(i, t, n):
                b = i * 2 + n
                sem = tile_in[n][t % 2]
                sp.dma_start(qk[:, n, t % 2, :], qk_dram[bass.ds(b, 1), :, t, :].rearrange("o p c -> p (o c)"))\
                  .then_inc(sem, 16)
                sp.dma_start(inv[:, n, t % 2, :, :].rearrange("p h i -> p (h i)"),
                             t_dram[bass.ds(b, 1), t * P:(t + 1) * P].rearrange("o p n -> p (o n)")).then_inc(sem, 16)

            for n in range(2):
                sp.sem_inc(stored[n], 16)
                for t in range(2):
                    load(0, t, n)

            def body(i, more):
                for t in range(TPS):
                    for n in range(2):
                        sp.wait_ge(out_done[n], i * TPS + (t + 2))
                        sp.sem_inc(waited, 1)
                        if t + 2 < TPS:
                            load(i, t + 2, n)
                        elif more:
                            load(i + 1, t + 2 - TPS, n)
                        if t == TPS - 1:
                            sp.wait_ge(out_kept[n], i * TPS + (TPS + 1))
                            sp.sem_inc(waited, 1)
                            sp.dma_start(delta_dram[bass.ds(i * 2 + n, 1)].rearrange("o p t c -> p (o t) c"),
                                         out[:, n, :, :]).then_inc(stored[n], 16)

            seq_pairs(body, sp)
            for n in range(2):
                sp.wait_ge(stored[n], 16 * (B // 2 + 1))

        @block.gpsimd
        def _(pool):
            g = nc.gpsimd
            g.tensor_scalar(minus_beta[:, :, :], beta[:, 0:NT, :], -1.0, None, ALU.mult).then_inc(made, 1)
            pool.wait_ge(made, 2)

            def weigh(i, t, count):
                for n in range(2):
                    b = i * 2 + n
                    pool.wait_ge(tile_in[n][t % 2], (i * 2 + (t // 2 + 1)) * 32)
                    if not (isinstance(count, int) and count == 0):
                        pool.wait_ge(uw_done[n], count)
                        pool.sem_inc(waited, 1)
                        pool.wait_ge(out_done[n], count)
                    pool.sem_inc(waited, 1)
                    weights = lambda x: x[:, bass.ds(b * TPS + t, 1), :].rearrange("p o h -> p (o h)").unsqueeze(2)\
                        .to_broadcast([P, DH, DK])
                    heads = lambda x: x.rearrange("p (h d) -> p h d", d=DK)
                    g.tensor_tensor(vk[:, n, :, 1, :], heads(qk[:, n, t % 2, C:]), weights(minus_beta), ALU.mult)
                    g.tensor_copy(local[:, n, t % 2, :],
                                  local_all[:, bass.ds(b * TPS + t, 1), :].rearrange("p o n -> p (o n)"))
                    vt = v_all[:, bass.ds(b * (TPS + 1) + (1 + t), 1), :].rearrange("p o c -> p (o c)")
                    g.tensor_tensor(vk[:, n, :, 0, :], heads(vt), weights(beta), ALU.mult).then_inc(vk_ready[n], 1)

            def body(i, more):
                for t in range(TPS):
                    if following(i, t, more):
                        weigh(*following(i, t, more))

            weigh(0, 0, 0)
            seq_pairs(body, pool)

        @block.tensor
        def _(pe):
            pe.wait_ge(made, 2)
            for n in range(2):
                pe.sem_inc(out_done[n], 1)

            def solve(i, t, count):
                for n in range(2):
                    pe.wait_ge(vk_ready[n], count + 1)
                    pe.sem_inc(waited, 1)
                    for c in range(CPT):
                        rows = slice(CHUNK * c, CHUNK * c + CHUNK)
                        for h in range(DH):
                            last = nc.tensor.matmul(uw_bank[rows, n, t % 2, h * 2 * DK:(h + 1) * 2 * DK],
                                                    inv[rows, n, t % 2, h, :],
                                                    vk[rows, n, h, :, :].rearrange("p x d -> p (x d)"),
                                                    start=(h == 0), stop=True, skip_group_check=(h > 0))
                    last.then_inc(uw_done[n], 1)

            def turn(i, t, count):
                for n in range(2):
                    pe.wait_ge(w_kept[n], count + 1)
                    nc.tensor.transpose(t_bank[:, n, 0:P], w[:, n, :], identity[:, :])
                    nc.tensor.transpose(t_bank[:, n, P:2 * P], qk[:, n, t % 2, 0:C], identity[:, :])\
                      .then_inc(turned[n], 1)

            def body(i, more):
                for t in range(TPS):
                    behind = following(i, t, more)
                    for c in range(CPT):
                        k = t * CPT + c
                        rows = slice(CHUNK * c, CHUNK * c + CHUNK)
                        for n in range(2):
                            if c == 0:
                                pe.wait_ge(wqT_ready[n], i * TPS + (t + 1))
                                pe.wait_ge(out_kept[n], i * TPS + (t + 1))
                            if k:
                                pe.wait_ge(s_kept[n], i * (STEPS - 1) + k)
                                u = uw_bank[rows, n, t % 2, 0:OUT_AT].rearrange("p (h x d) -> p h x d", x=2, d=DK)
                                u = u[:, 0:DH, 0, :]
                                nc.tensor.matmul(u, wqT[:, n, t % 2, 0, rows],
                                                 S[:, n, :].rearrange("p (h d) -> p h d", d=DK),
                                                 start=False, stop=True, skip_group_check=True)
                                nc.tensor.matmul(uw_bank[rows, n, t % 2, OUT_AT:OUT_AT + C],
                                                 wqT[:, n, t % 2, 1, rows], S[:, n, :],
                                                 start=False, stop=True, skip_group_check=True)\
                                  .then_inc(u_done[n], 1)
                        for n in range(2):
                            pe.wait_ge(u_kept[n], i * STEPS + (k + 1))
                            pe.sem_inc(waited, 1)
                            if k < STEPS - 1:
                                nc.tensor.matmul(s_bank[:, n, 0:C], qk[rows, n, t % 2, C:], U[rows, n, :],
                                                 start=(k == 0), stop=True, skip_group_check=(k > 0))\
                                  .then_inc(s_done[n], 1)
                            for h in range(DH):
                                cols = slice(DK * h, DK * h + DK)
                                o = uw_bank[rows, n, t % 2, OUT_AT + DK * h:OUT_AT + DK * h + DK]
                                last = nc.tensor.matmul(o,
                                                        local[rows, n, t % 2, cols], U[rows, n, cols],
                                                        start=False, stop=True, skip_group_check=True)
                            if c == CPT - 1:
                                last.then_inc(out_done[n], 1)
                        if behind and c == 0:
                            solve(*behind)
                        if behind and c == 2:
                            turn(*behind)

            solve(0, 0, 0)
            turn(0, 0, 0)
            seq_pairs(body, pe)

        @block.scalar
        def _(act):
            def keep_w(i, t, count):
                for n in range(2):
                    act.wait_ge(uw_done[n], count + 1)
                    nc.scalar.activation(w[:, n, :].rearrange("p (h d) -> p h d", d=DK),
                                         uw_bank[:, n, t % 2, :].rearrange("p (h x d) -> p h x d", x=2, d=DK)
                                         [:, 0:DH, 1, :], ACT.Copy).then_inc(w_kept[n], 1)

            def keep_turned(i, t, count):
                for n in range(2):
                    act.wait_ge(turned[n], count + 1)
                    nc.scalar.activation(wqT[:, n, t % 2, :, :].rearrange("p x n -> p (x n)"),
                                         t_bank[:, n, 0:2 * P], ACT.Copy).then_inc(wqT_ready[n], 1)

            def body(i, more):
                for t in range(TPS):
                    behind = following(i, t, more)
                    for c in range(CPT):
                        k = t * CPT + c
                        rows = slice(CHUNK * c, CHUNK * c + CHUNK)
                        for n in range(2):
                            if k:
                                act.wait_ge(u_done[n], i * (STEPS - 1) + k)
                            u = uw_bank[rows, n, t % 2, :].rearrange("p (h x d) -> p h x d", x=2, d=DK)[:, 0:DH, 0, :]
                            nc.scalar.activation(U[rows, n, :].rearrange("p (h d) -> p h d", d=DK), u, ACT.Copy)\
                              .then_inc(u_kept[n], 1)
                        if behind and c == 0:
                            keep_w(*behind)
                        if behind and c == 2:
                            keep_turned(*behind)
                    for n in range(2):
                        if t == 0:
                            act.wait_ge(stored[n], (i + 1) * 16)
                        act.wait_ge(out_done[n], i * TPS + (t + 2))
                        nc.scalar.activation(out[:, n, t, :], uw_bank[:, n, t % 2, OUT_AT:OUT_AT + C], ACT.Copy)\
                          .then_inc(out_kept[n], 1)

            for n in range(2):
                act.sem_inc(out_kept[n], 1)
            keep_w(0, 0, 0)
            keep_turned(0, 0, 0)
            seq_pairs(body, act)

        @block.vector
        def _(dve):
            v = nc.vector
            v.memset(same_head[:, :], 0.0).then_inc(cleared, 1)
            dve.wait_ge(cleared, 1)
            for h in range(DH):
                last = v.memset(same_head[DK * h:DK * h + DK, DK * h:DK * h + DK], 1.0)
            last.then_inc(made, 1)
            dve.wait_ge(made, 2)

            def body(i, more):
                for k in range(STEPS - 1):
                    for n in range(2):
                        dve.wait_ge(s_done[n], i * (STEPS - 1) + (k + 1))
                        v.tensor_tensor(S[:, n, :], s_bank[:, n, 0:C], same_head[:, :], ALU.mult)\
                         .then_inc(s_kept[n], 1)

            seq_pairs(body, dve)


SOURCES = 4
KINDS = 4
FLOOR = 0.05
SUM_EPS = 1e-5


def gated_sum(nc, tag, io, X, stats, identity, v_all, filtered, delta_dram):
    TH = TPS * DH
    with Stage(nc, tag) as s:
        w1 = s.sb("w1", [P, C])
        w1_stats = s.sb("w1_stats", [P, C])
        b1, w2, wo = s.sb("b1", [P, 1]), s.sb("w2", [P, SOURCES]), s.sb("wo", [P, C])
        rms_w = s.sb("rms_w", [P, DK])
        bias, b2 = s.sb("bias", [P, DH, SOURCES]), s.sb("b2", [P, SOURCES])
        log_temp, inv_temp = s.sb("log_temp", [P, DH]), s.sb("inv_temp", [P, DH])
        soft, residual = s.sb("soft", [P, DH]), s.sb("residual", [P, DH])
        minus_half = s.sb("minus_half", [P, TH])
        delta = s.sb("delta", [P, 2, TPS, C])
        stat = s.sb("stat", [P, 2, TH, DK])
        squares = s.sb("squares", [P, SOURCES, TH, DK])
        weighted = s.sb("weighted", [P, SOURCES, TH, DK])
        length = s.sb("length", [P, TH, SOURCES])
        hn = s.sb("hn", [P, 2, TPS, C])
        hT, statT = s.sb("hT", [P, T]), s.sb("statT", [P, T])
        hidden = s.sb("hidden", [P, DH, T])
        logits, top = s.sb("logits", [P, TH, SOURCES]), s.sb("top", [P, TH])
        shares, rec = s.sb("shares", [P, TH, SOURCES]), s.sb("rec", [P, TH])
        o, o_sq = s.sb("o", [P, TH, DK]), s.sb("o_sq", [P, TH, DK])
        rms = s.sb("rms", [P, TH])
        on, oT = s.sb("on", [P, TH, DK]), s.sb("oT", [P, T])
        t_bank, stat_bank = s.ps("t_bank", [P, T]), s.ps("stat_bank", [P, T])
        hidden_bank = s.ps("hidden_bank", [P, DH, T])
        logit_bank, y_bank = s.ps("logit_bank", [P, T]), s.ps("y_bank", [P, T])

        loaded, made, step = s.sem("weights_loaded"), s.sem("constants_made"), s.sem("constants_step")
        delta_in = [s.sem(f"delta_in{n}") for n in range(2)]
        sums_step, sums_ready = s.sem("sums_step"), s.sem("sums_ready")
        centred, squares_ready = s.sem("centred"), s.sem("squares_ready")
        length_step, variances_ready = s.sem("length_step"), s.sem("variances_ready")
        lengths_ready, hn_ready = s.sem("lengths_ready"), s.sem("hn_ready")
        turned, turned_kept = s.sem("turned"), s.sem("turned_kept")
        hidden_done, gelu_done, logits_done = s.sem("hidden_done"), s.sem("gelu_done"), s.sem("logits_done")
        soft_step, exp_ready, shares_ready = s.sem("soft_step"), s.sem("exp_ready"), s.sem("shares_ready")
        shared, filters_shared = s.sem("sources_shared"), s.sem("filters_shared")
        o_ready, o_sq_ready = s.sem("o_ready"), s.sem("o_sq_ready")
        ms_ready, rms_step, rms_ready = s.sem("ms_ready"), s.sem("rms_step"), s.sem("rms_ready")
        waited = s.sem("waited")
        floor_done, on_step, on_ready = s.sem("floor_done"), s.sem("on_step"), s.sem("on_ready")
        added = s.sem("added_1")
        o_turned, oT_kept, y_done = s.sem("o_turned"), s.sem("oT_kept"), s.sem("y_done")
        LOADED, MADE = 16 * 13, 7
        SOFT_STEPS = 10
        block = s.block()

        def sequences(body, eng):
            with eng.Fori(0, B // 2 - 1) as i:
                for n in range(2):
                    body(i, i * 2 + n, n, 2)
            body(B // 2 - 1, B - 2, 0, 1)
            body(B // 2 - 1, B - 1, 1, 0)

        def heads(x):
            return x.rearrange("p t (h d) -> p (t h) d", d=DK)

        def sources(b, n):
            filters = filtered[:, :, bass.ds(b * TPS, TPS), :].rearrange("p s t (h d) -> p s (t h) d", d=DK)
            return [(0, 2, filters), (2, 1, heads(delta[:, n, :, :]).unsqueeze(1)),
                    (3, 1, heads(v_all[:, bass.ds(b * (TPS + 1) + 1, TPS), :]).unsqueeze(1))]

        def share_out(eng, source):
            s0, k, x = source
            share = shares[:, :, s0:s0 + k].rearrange("p n s -> p s n").unsqueeze(3).to_broadcast([P, k, TH, DK])
            return eng.tensor_tensor(weighted[:, s0:s0 + k, :, :], x, share, ALU.mult)

        def kind(n, k):
            return stat[:, n, :, k:SOURCES * KINDS:KINDS]

        @block.sync
        def _(sp):
            sp.dma_start(w1[:, :], io["w1"][0:C]).then_inc(loaded, 16)
            for h in range(DH):
                sp.dma_start(w1_stats[DK * h:DK * h + SOURCES * KINDS, :], io["w1"][C:]).then_inc(loaded, 16)
            sp.dma_start(b1[:, :], io["b1"].unsqueeze(1)).then_inc(loaded, 16)
            sp.dma_start(w2[:, :], io["w2"]).then_inc(loaded, 16)
            sp.dma_start(wo[:, :], io["wo"]).then_inc(loaded, 16)
            sp.dma_start(rms_w[:, :], io["rms_w"].partition_broadcast(P)).then_inc(loaded, 16)
            sp.dma_start(bias[:, :, :], io["base_bias"].partition_broadcast(P)).then_inc(loaded, 16)
            sp.dma_start(b2[:, :], io["b2"].partition_broadcast(P)).then_inc(loaded, 16)
            sp.dma_start(log_temp[:, :], io["log_temp"].partition_broadcast(P)).then_inc(loaded, 16)
            sp.dma_start(residual[:, :], io["residual"].partition_broadcast(P)).then_inc(loaded, 16)
            for n in range(2):
                sp.dma_start(delta[:, n, :, :], delta_dram[n]).then_inc(delta_in[n], 16)
            with sp.Fori(0, B // 2 - 1) as i:
                for n in range(2):
                    sp.wait_ge(shared, i * 2 + (n + 1))
                    sp.dma_start(delta[:, n, :, :], delta_dram[bass.ds(i * 2 + (n + 2), 1)]
                                 .rearrange("o p t c -> p (o t) c")).then_inc(delta_in[n], 16)

        @block.gpsimd
        def _(pool):
            g = nc.gpsimd
            g.memset(minus_half[:, :], -0.5).then_inc(made, 1)
            g.memset(stat[:, :, :, :], 0.0).then_inc(made, 1)
            pool.wait_ge(loaded, LOADED)
            pool.wait_ge(made, MADE)

            def centre(b, n):
                pool.wait_ge(sums_ready, b + 1)
                pool.sem_inc(waited, 1)
                for s0, k, x in sources(b, n):
                    mean = kind(n, 0)[:, :, s0:s0 + k].rearrange("p n s -> p s n").unsqueeze(3)\
                        .to_broadcast([P, k, TH, DK])
                    last = g.tensor_tensor(squares[:, s0:s0 + k, :, :], x, mean, ALU.subtract)
                last.then_inc(centred, 1)

            def body(i, b, n, follow):
                m = (n + 1) % 2
                if follow:
                    centre(b + 1, m)
                pool.wait_ge(shares_ready, b + 1)
                pool.sem_inc(waited, 1)
                for source in sources(b, n)[1:]:
                    last = share_out(g, source)
                last.then_inc(shared, 1)
                pool.wait_ge(ms_ready, b + 1)
                pool.sem_inc(rms_step, 1)
                g.tensor_scalar(rms[:, :], rms[:, :], 1.0 / DK, SUM_EPS, ALU.mult, ALU.add).then_inc(rms_step, 1)
                pool.wait_ge(rms_step, b * 2 + 2)
                g.tensor_tensor(rms[:, :], rms[:, :], minus_half[:, :], ALU.pow).then_inc(rms_ready, 1)
                pool.wait_ge(on_step, b + 1)
                g.tensor_tensor(on[:, :, :], on[:, :, :], rms_w[:, :].unsqueeze(1).to_broadcast([P, TH, DK]),
                                ALU.mult).then_inc(on_ready, 1)

            centre(0, 0)
            sequences(body, pool)

        @block.tensor
        def _(pe):
            pe.wait_ge(loaded, LOADED)
            pe.wait_ge(made, MADE)

            pe.sem_inc(added, 1)

            def network(b, n, first):
                pe.wait_ge(hn_ready, b + 1)
                pe.wait_ge(variances_ready, b + 1)
                pe.wait_ge(lengths_ready, b + 1)
                for t in range(TPS):
                    cols = slice(t * P, (t + 1) * P)
                    nc.tensor.transpose(t_bank[:, cols], hn[:, n, t, :], identity[:, :])
                    last = nc.tensor.transpose(stat_bank[:, cols],
                                               stat[:, n, t * DH:(t + 1) * DH, :].rearrange("p h k -> p (h k)"),
                                               identity[:, :])
                last.then_inc(turned, 1)
                pe.wait_ge(turned_kept, b + 1)
                for h in range(DH):
                    rows = slice(DK * h, DK * h + SOURCES * KINDS)
                    nc.tensor.matmul(hidden_bank[:, h, :], w1[:, :], hT[:, :], start=True, stop=False)
                    nc.tensor.matmul(hidden_bank[:, h, :], w1_stats[rows, :], statT[rows, :], start=False, stop=True)\
                      .then_inc(hidden_done, 1)
                if not first:
                    pe.wait_ge(soft_step, b * SOFT_STEPS + (1 - SOFT_STEPS))
                for h in range(DH):
                    pe.wait_ge(gelu_done, b * DH + (h + 1))
                    for t in range(TPS):
                        c = (t * DH + h) * SOURCES
                        last = nc.tensor.matmul(logit_bank[:, c:c + SOURCES], hidden[:, h, t * P:(t + 1) * P],
                                                w2[:, :], start=True, stop=True)
                last.then_inc(logits_done, 1)

            def body(i, b, n, follow):
                if follow:
                    network(b + 1, (n + 1) % 2, False)
                pe.wait_ge(on_ready, b + 1)
                for t in range(TPS):
                    last = nc.tensor.transpose(t_bank[:, t * P:(t + 1) * P],
                                               on[:, t * DH:(t + 1) * DH, :].rearrange("p h d -> p (h d)"),
                                               identity[:, :])
                last.then_inc(o_turned, 1)
                pe.wait_ge(oT_kept, b + 1)
                pe.wait_ge(added, b + 1)
                for t in range(TPS):
                    last = nc.tensor.matmul(y_bank[:, t * P:(t + 1) * P], oT[:, t * P:(t + 1) * P], wo[:, :],
                                            start=True, stop=True)
                last.then_inc(y_done, 1)

            network(0, 0, True)
            sequences(body, pe)

        @block.scalar
        def _(act):
            act.wait_ge(loaded, LOADED)
            nc.scalar.activation(soft[:, :], log_temp[:, :], ACT.Abs).then_inc(step, 1)
            act.wait_ge(step, 1)
            nc.scalar.activation(soft[:, :], soft[:, :], ACT.Exp, scale=-1.0).then_inc(step, 1)
            act.wait_ge(step, 3)
            nc.scalar.activation(soft[:, :], soft[:, :], ACT.Ln).then_inc(step, 1)
            nc.scalar.activation(residual[:, :], residual[:, :], ACT.Sigmoid).then_inc(step, 1)

            def square(b):
                act.wait_ge(centred, b + 1)
                nc.scalar.activation(squares[:, :, :, :], squares[:, :, :, :], ACT.Square).then_inc(squares_ready, 1)

            def network(b, n):
                act.wait_ge(length_step, b * 2 + 2)
                nc.scalar.activation(kind(n, 3), length[:, :, :], ACT.Sqrt).then_inc(lengths_ready, 1)
                act.wait_ge(turned, b + 1)
                nc.scalar.activation(hT[:, :], t_bank[:, :], ACT.Copy)
                nc.scalar.activation(statT[:, :], stat_bank[:, :], ACT.Copy).then_inc(turned_kept, 1)
                for h in range(DH):
                    act.wait_ge(hidden_done, b * DH + (h + 1))
                    nc.scalar.activation(hidden[:, h, :], hidden_bank[:, h, :], ACT.Gelu, bias=b1[:, 0:1])\
                      .then_inc(gelu_done, 1)

            def body(i, b, n, follow):
                if follow:
                    square(b + 1)
                act.wait_ge(soft_step, b * SOFT_STEPS + 4)
                nc.scalar.activation(shares[:, :, :], logits[:, :, :], ACT.Exp).then_inc(exp_ready, 1)
                if follow:
                    network(b + 1, (n + 1) % 2)
                act.wait_ge(o_turned, b + 1)
                nc.scalar.activation(oT[:, :], t_bank[:, :], ACT.Copy).then_inc(oT_kept, 1)

            square(0)
            network(0, 0)
            sequences(body, act)

        @block.vector
        def _(dve):
            v = nc.vector
            dve.wait_ge(loaded, LOADED)
            v.tensor_tensor(bias[:, :, :], bias[:, :, :], b2[:, :].unsqueeze(1).to_broadcast([P, DH, SOURCES]),
                            ALU.add).then_inc(made, 1)
            dve.wait_ge(step, 2)
            v.tensor_scalar(soft[:, :], soft[:, :], 1.0, None, ALU.add).then_inc(step, 1)
            dve.wait_ge(step, 5)
            v.tensor_scalar(residual[:, :], residual[:, :], 0.5, None, ALU.mult).then_inc(made, 1)
            v.tensor_scalar(log_temp[:, :], log_temp[:, :], 0.0, 1e-4, ALU.max, ALU.add).then_inc(made, 1)
            dve.wait_ge(made, 5)
            v.tensor_tensor(inv_temp[:, :], log_temp[:, :], soft[:, :], ALU.add).then_inc(made, 1)
            dve.wait_ge(made, 6)
            v.reciprocal(inv_temp[:, :], inv_temp[:, :]).then_inc(made, 1)
            dve.wait_ge(made, MADE)

            def sums(b, n, i):
                dve.wait_ge(delta_in[n], (i + 1) * 16)
                for s0, k, x in sources(b, n):
                    out = lambda j: kind(n, j)[:, :, s0:s0 + k].rearrange("p n s -> p s n")
                    v.reduce_sum(out(0), x, AX.X)
                    last = v.reduce_sum(out(2), x, AX.X, apply_absolute_value=True)
                last.then_inc(sums_step, 1)
                dve.wait_ge(sums_step, b + 1)
                both = stat[:, n, :, 0:SOURCES * KINDS:2]
                v.tensor_scalar(both, both, 1.0 / DK, None, ALU.mult).then_inc(sums_ready, 1)
                tokens, moments = X[:, bass.ds(b * TPS, TPS), :], stats[:, bass.ds(b * TPS, TPS), :]
                for t in range(TPS):
                    last = v.tensor_scalar(hn[:, n, t, :], tokens[:, t, :], moments[:, t:t + 1, 0],
                                           moments[:, t:t + 1, 1], ALU.subtract, ALU.mult)
                last.then_inc(hn_ready, 1)

            def variances(b, n):
                dve.wait_ge(squares_ready, b + 1)
                v.scalar_tensor_tensor(length[:, :, :], kind(n, 0), float(DK), kind(n, 0), ALU.mult, ALU.mult)
                v.reduce_sum(kind(n, 1).rearrange("p n s -> p s n"), squares[:, :, :, :], AX.X)\
                 .then_inc(length_step, 1)
                dve.wait_ge(length_step, b * 2 + 1)
                v.tensor_tensor(length[:, :, :], length[:, :, :], kind(n, 1), ALU.add).then_inc(length_step, 1)
                dve.wait_ge(length_step, b * 2 + 2)
                v.tensor_scalar(kind(n, 1), kind(n, 1), 1.0 / DK, None, ALU.mult).then_inc(variances_ready, 1)

            def body(i, b, n, follow):
                m = (n + 1) % 2
                def done(k):
                    return b * SOFT_STEPS + k

                def each(x):
                    return x.unsqueeze(2).to_broadcast([P, TH, SOURCES])

                dve.wait_ge(logits_done, b + 1)
                v.tensor_tensor(logits[:, :, :].rearrange("p (t h) s -> p t (h s)", h=DH),
                                logit_bank[:, 0:TH * SOURCES].rearrange("p (t k) -> p t k", t=TPS),
                                bias[:, :, :].rearrange("p h s -> p (h s)").unsqueeze(1)
                                .to_broadcast([P, TPS, DH * SOURCES]), ALU.add).then_inc(soft_step, 1)
                dve.wait_ge(soft_step, done(1))
                v.tensor_tensor(logits[:, :, :].rearrange("p (t h) s -> p t h s", h=DH),
                                logits[:, :, :].rearrange("p (t h) s -> p t h s", h=DH),
                                inv_temp[:, :].unsqueeze(1).unsqueeze(3).to_broadcast([P, TPS, DH, SOURCES]),
                                ALU.mult).then_inc(soft_step, 1)
                dve.wait_ge(soft_step, done(2))
                v.reduce_max(top[:, :], logits[:, :, :], AX.X).then_inc(soft_step, 1)
                dve.wait_ge(soft_step, done(3))
                v.tensor_tensor(logits[:, :, :], logits[:, :, :], each(top[:, :]), ALU.subtract)\
                 .then_inc(soft_step, 1)
                if follow:
                    variances(b + 1, m)
                dve.wait_ge(exp_ready, b + 1)
                for j in range(2):
                    v.reduce_sum(rec[:, :], shares[:, :, :], AX.X).then_inc(soft_step, 1)
                    dve.wait_ge(soft_step, done(3 * j + 5))
                    v.reciprocal(rec[:, :], rec[:, :]).then_inc(soft_step, 1)
                    dve.wait_ge(soft_step, done(3 * j + 6))
                    last = v.tensor_tensor(shares[:, :, :], shares[:, :, :], each(rec[:, :]), ALU.mult)
                    last.then_inc(soft_step, 1)
                    if j == 0:
                        dve.wait_ge(soft_step, done(7))
                        v.tensor_scalar(shares[:, :, 0:2], shares[:, :, 0:2], FLOOR, None, ALU.max)\
                         .then_inc(floor_done, 1)
                        dve.wait_ge(floor_done, b + 1)
                dve.wait_ge(soft_step, done(10))
                short = shares[:, :, 0].rearrange("p (t h) -> p t h", h=DH)
                v.tensor_tensor(short, short, residual[:, :].unsqueeze(1).to_broadcast([P, TPS, DH]), ALU.add)\
                 .then_inc(shares_ready, 1)
                dve.wait_ge(shares_ready, b + 1)
                share_out(v, sources(b, n)[0]).then_inc(filters_shared, 1)
                dve.wait_ge(shared, b + 1)
                dve.wait_ge(filters_shared, b + 1)
                v.reduce_sum(o[:, :, :], weighted[:, :, :, :].rearrange("p s n d -> p n d s"), AX.X)\
                 .then_inc(o_ready, 1)
                dve.wait_ge(o_ready, b + 1)
                v.tensor_tensor(o_sq[:, :, :], o[:, :, :], o[:, :, :], ALU.mult).then_inc(o_sq_ready, 1)
                dve.wait_ge(o_sq_ready, b + 1)
                v.reduce_sum(rms[:, :], o_sq[:, :, :], AX.X).then_inc(ms_ready, 1)
                dve.wait_ge(rms_ready, b + 1)
                v.tensor_tensor(on[:, :, :], o[:, :, :], rms[:, :].unsqueeze(2).to_broadcast([P, TH, DK]), ALU.mult)\
                 .then_inc(on_step, 1)
                if follow == 2:
                    sums(b + 2, n, i + 1)
                dve.wait_ge(y_done, b + 1)
                x = X[:, bass.ds(b * TPS, TPS), :].rearrange("p t c -> p (t c)")
                v.tensor_tensor(x, x, y_bank[:, :], ALU.add).then_inc(added, 1)

            sums(0, 0, 0)
            variances(0, 0)
            sums(1, 1, 0)
            sequences(body, dve)


def gated_delta(nc, tag, io, X, stats, identity):
    qk_dram = nc.dram_tensor(f"{tag}_qk_dram", (B, P, TPS, 2 * C), F32, kind="Internal").ap()
    delta_dram = nc.dram_tensor(f"{tag}_delta_dram", (B, P, TPS, C), F32, kind="Internal").ap()
    a_dram = nc.dram_tensor(f"{tag}_a_dram", (B, T, C), F32, kind="Internal").ap()
    t_dram = nc.dram_tensor(f"{tag}_t_dram", (B, T, C), F32, kind="Internal").ap()
    with Stage(nc, tag) as s:
        v_all = s.sb("v_all", [P, B * (TPS + 1), C])
        beta = s.sb("beta", [P, NT + TPS, DH])
        delta_inputs(nc, f"{tag}_in", io, X, stats, identity, v_all, beta, qk_dram)
        with Stage(nc, f"{tag}_chunks") as chunks:
            local_all = chunks.sb("local_all", [P, NT, C])
            chunk_products(nc, f"{tag}_products", io, identity, beta, local_all, qk_dram, a_dram)
            solve_chunks(nc, f"{tag}_solve", a_dram, t_dram)
            delta_states(nc, f"{tag}_states", identity, v_all, beta, local_all, qk_dram, t_dram, delta_dram)
        filtered = s.sb("filtered", [P, 2, NT, C])
        long_filters(nc, f"{tag}_fir", io, v_all, filtered)
        gated_sum(nc, f"{tag}_gate", io, X, stats, identity, v_all, filtered, delta_dram)


def build(nc, io, layers=range(8)):
    with Stage(nc, "main") as s:
        X = s.sb("X", [P, NT + 2 * TPS, C])
        stats = s.sb("stats", [P, NT + 2 * TPS, 2])
        identity = s.sb("identity", [P, P])
        sorted_in = s.dram("sorted_in", (SORTED + SPARE, P, C))
        sorted_out = s.dram("sorted_out", (SORTED, P, C))
        load_x(nc, io, X, stats, identity)
        for n in layers:
            layernorm_stats(nc, f"l{n}", X, stats)
            if n in (0, 4):
                sub = {k[3:]: v for k, v in io.items() if k.startswith(f"a{n}_")}
                attention16(nc, f"l{n}", sub, X, stats, identity, causal=(n == 0), rope=(n == 4), biased=(n == 0))
            elif n in (1, 3):
                sub = {k[4:]: v for k, v in io.items() if k.startswith("ffn_")}
                mixture(nc, f"l{n}", sub, X, stats, identity, sorted_in, sorted_out, first=(n == FIRST_MIXTURE))
            elif n in (5, 7):
                sub = {k[4:]: v for k, v in io.items() if k.startswith("mix_")}
                channel_mix(nc, f"l{n}", sub, X, stats, identity)
            elif n == 2:
                sub = {k[4:]: v for k, v in io.items() if k.startswith("swa_")}
                window_attention(nc, f"l{n}", sub, X, stats, identity)
            else:
                sub = {k[3:]: v for k, v in io.items() if k.startswith("dr_")}
                gated_delta(nc, f"l{n}", sub, X, stats, identity)
        store_x(nc, io, X)


def layout(inputs):
    import numpy as np
    g = {k: np.asarray(v) for k, v in inputs.items()}
    a = {"x": g["L0_attn_a_x"]}
    w, bq = g["L0_attn_a_w_qkv"], g["L0_attn_a_b_qkv"]
    for j, n in enumerate("qkv"):
        a[f"a0_w_{n}"], a[f"a0_b_{n}"] = w[:, j * C:(j + 1) * C], bq[j * C:(j + 1) * C]
    a["a0_w_out"], a["a0_b_out"] = g["L0_attn_a_w_out"], g["L0_attn_a_b_out"]
    swap = np.arange(C) ^ 1
    for n in "qkv":
        a[f"a4_w_{n}"] = g[f"L1_attn_a_w{n}"].T
    for n in "qk":
        a[f"a4_w_{n}_swapped"] = g[f"L1_attn_a_w{n}"][swap].T
    a["a4_w_out"] = g["L1_attn_a_wo"].T
    f = np.float32
    inv = (f(1) / f(10000) ** (np.arange(0, D, 2, dtype=f) / f(D))).astype(f)
    angle = np.outer(np.arange(T, dtype=f), inv).astype(f)
    which = (np.arange(C) % D) // 2
    sign = np.where(np.arange(C) % 2 == 0, f(-1), f(1))
    a["a4_cos"] = np.cos(angle).astype(f).T[which]
    a["a4_sin"] = np.sin(angle).astype(f).T[which] * sign[:, None]
    order = np.arange(C).reshape(PAIRS, 2, D).transpose(1, 2, 0).reshape(C)
    for n in ("a0_w_q", "a0_w_k", "a4_w_q", "a4_w_k", "a4_w_q_swapped", "a4_w_k_swapped"):
        a[n] = a[n][:, order]
    for n in ("a0_b_q", "a0_b_k", "a4_cos", "a4_sin"):
        a[n] = a[n][order]
    a["ffn_w_router"], a["ffn_b_router"] = g["L0_ffn_Wr"], g["L0_ffn_br"]
    a["ffn_w1"], a["ffn_w2"], a["ffn_b2"] = g["L0_ffn_W1"], g["L0_ffn_W2"], g["L0_ffn_b2"]
    a["ffn_b1"] = g["L0_ffn_b1"].reshape(E, FC, P).transpose(2, 0, 1)
    for n in "rkv":
        a[f"mix_w_{n}"] = g[f"L1_ffn_W_{n}"].T
    for n in "rk":
        a[f"mix_mu_{n}"] = g[f"L1_ffn_mu_{n}"]
    wq = g["L0_attn_b_wq"].reshape(2, 2, REP, HD, C).transpose(0, 2, 1, 3, 4).reshape(QH * HD, C)
    a["swa_w_q"] = wq.T
    a["swa_w_kv"] = np.concatenate([g["L0_attn_b_wk"], g["L0_attn_b_wv"]]).T
    a["swa_w_out"] = g["L0_attn_b_wo"].T
    a["swa_q_norm"], a["swa_k_norm"] = g["L0_attn_b_q_norm_w"], g["L0_attn_b_k_norm_w"]
    d = {n: g[f"L1_attn_b_{n}"] for n in ("Wq", "Wk", "Wv", "Wb", "W1", "b1", "W2", "b2", "log_temp", "base_bias",
                                          "conv_residual_logit", "rms_w", "Wo", "conv_q", "conv_k", "conv_v",
                                          "fir_short", "fir_long")}
    a["dr_w_qkv"] = np.concatenate([d["Wq"], d["Wk"], d["Wv"]], 1)
    a["dr_conv"] = np.concatenate([d["conv_q"], d["conv_k"], d["conv_v"]]).T
    a["dr_w_beta"], a["dr_w1"], a["dr_b1"], a["dr_w2"], a["dr_b2"] = d["Wb"], d["W1"], d["b1"], d["W2"], d["b2"]
    a["dr_log_temp"], a["dr_base_bias"], a["dr_residual"] = d["log_temp"], d["base_bias"], d["conv_residual_logit"]
    a["dr_rms_w"], a["dr_wo"] = d["rms_w"], d["Wo"]
    for n in ("short", "long"):
        taps = d[f"fir_{n}"].reshape(C, -1)
        row = np.zeros((C, FILTER_PAD), taps.dtype)
        row[:, P - 1:P - 1 + taps.shape[1]] = taps[:, ::-1]
        a[f"dr_{n}"] = row
    j, i = np.arange(P)[:, None] % CHUNK, np.arange(CHUNK)[None, :]
    a["dr_chunk_masks"] = np.stack([np.where(j < i, f(-1), f(0)), np.where(j <= i, f(1), f(0))])
    return {k: np.ascontiguousarray(v) for k, v in a.items()}


def kernel(**inputs):
    import concourse.bacc as _bacc
    from concourse import mybir as _mybir
    from concourse.bass_utils import run_bass_kernel_spmd as _run

    arrays = {f"in_{k}_dram": v for k, v in layout(inputs).items()}
    nc = _bacc.Bacc("TRN2", target_bir_lowering=False, num_devices=1)
    io = {k[3:-5]: nc.dram_tensor(k, v.shape, _mybir.dt.from_np(v.dtype), kind="ExternalInput").ap()
          for k, v in arrays.items()}
    io["out"] = nc.dram_tensor("out_0_dram", (B, T, C), F32, kind="ExternalOutput").ap()
    build(nc, io)
    r = _run(nc, [arrays], core_ids=[0])
    return r.results[0]["out_0_dram"]
```
